# Optimizing a Trainium2 kernel written in Bass

```python
import numpy as np
import jax
import jax.numpy as jnp

def _softmax(x, axis=-1):
    return jax.nn.softmax(x, axis=axis)

def _gelu(x):
    return jax.nn.gelu(x, approximate=True)

def _silu(x):
    return jax.nn.silu(x)

def _sigmoid(x):
    return jax.nn.sigmoid(x)

def _layernorm(x, axis=-1, eps=1e-05):
    m = jnp.mean(x, axis=axis, keepdims=True)
    v = jnp.var(x, axis=axis, keepdims=True)
    return (x - m) / jnp.sqrt(v + eps)

def _scatter_add(tgt, idx, src, axis=0):
    return tgt.at[idx].add(src)

def _segment_sum(src, seg, n):
    return jax.ops.segment_sum(src, seg, n)
kernel_name = 'mk_flamingo_gated_d1_seqx_r8_252915'

def setup_inputs(seed: int=0):
    np.random.seed(seed)
    _w = jnp.asarray

    def _rec_inputs():
        import jax
        import jax.numpy as jnp
        _rk = jax.random.key(seed)
        x = -0.0003929 + 0.9999 * jax.random.normal(jax.random.fold_in(_rk, 1), (16, 128, 256), jnp.float32)
        _lenS = 128 - jax.random.randint(jax.random.fold_in(_rk, 7), (16,), 0, max(1, 128 // 4) + 1, jnp.int32)
        _lenS2 = 128 - jax.random.randint(jax.random.fold_in(_rk, 8), (16,), 0, max(1, 128 // 4) + 1, jnp.int32)
        _ctx_2048P = jax.random.normal(jax.random.fold_in(_rk, 11), (16, 16, 256), jnp.float32)
        _ctx_2048c = jax.random.dirichlet(jax.random.fold_in(_rk, 511), 0.3 * jnp.ones((16,), jnp.float32), (16, 128))
        _ctx_2048t = jnp.einsum('bsk,bkd->bsd', _ctx_2048c, _ctx_2048P)
        _ctx_2048t = _ctx_2048t * jax.lax.rsqrt(jnp.mean(jnp.square(_ctx_2048t)) + 1e-12) * 0.953939
        ctx_2048 = 2.81802e-05 + 1.00001 * (_ctx_2048t + 0.3 * jax.random.normal(jax.random.fold_in(_rk, 611), (16, 128, 256), jnp.float32))
        _g = jax.random.normal(jax.random.fold_in(_rk, 9001), (2, 1), jnp.float32)
        _g = jnp.sign(_g) * jnp.maximum(jnp.abs(_g), 1.0) + (_g == 0) * 1.0
        g_xattn = _g[0]
        g_ffn = _g[1]
        return (x, ctx_2048, g_xattn, g_ffn)
    x, ctx_2048, g_xattn, g_ffn = _rec_inputs()

    def _L0_xattn_setup():
        import jax, jax.numpy as jnp
        import numpy as np
        N, D, L = (8, 128, 256)
        key = jax.random.key(seed)
        ks = jax.random.split(key, 5)
        s = 1.0 / np.sqrt(D)
        return {'X1': jax.random.normal(ks[0], (N, D, L), dtype=jnp.float32), 'X2': jax.random.normal(ks[1], (N, D, L), dtype=jnp.float32), 'QW': jax.random.normal(ks[2], (D, D), dtype=jnp.float32) * s, 'Qb': jnp.zeros((D,), dtype=jnp.float32), 'KW': jax.random.normal(ks[3], (D, D), dtype=jnp.float32) * s, 'Kb': jnp.zeros((D,), dtype=jnp.float32), 'VW': jax.random.normal(ks[4], (D, D), dtype=jnp.float32) * s, 'Vb': jnp.zeros((D,), dtype=jnp.float32)}
    _L0_xattn_all = _L0_xattn_setup()
    _L0_xattn_in = {k: v for k, v in _L0_xattn_all.items() if k in ('QW', 'Qb', 'KW', 'Kb', 'VW', 'Vb')}
    del _L0_xattn_all

    def _L0_ffn_setup():
        import jax, jax.numpy as jnp
        import numpy as np
        TOP_K = 6
        N_GROUP = 8
        TOPK_GROUP = 3
        CAPACITY = 96
        RSF = 1.0
        key = jax.random.key(seed)
        ks = jax.random.split(key, 8)
        B, S, H = (1, 512, 256)
        E, M = (64, 176)
        MS = 352
        sc = 0.02
        return {'hidden_states': jax.random.normal(ks[0], (B, S, H), jnp.float32), 'gate_weight': jax.random.normal(ks[1], (E, H), jnp.float32) * sc, 'Wg': jax.random.normal(ks[2], (E, M, H), jnp.float32) * sc, 'Wu': jax.random.normal(ks[3], (E, M, H), jnp.float32) * sc, 'Wd': jax.random.normal(ks[4], (E, H, M), jnp.float32) * sc, 'Sg': jax.random.normal(ks[5], (MS, H), jnp.float32) * sc, 'Su': jax.random.normal(ks[6], (MS, H), jnp.float32) * sc, 'Sd': jax.random.normal(ks[7], (H, MS), jnp.float32) * sc}
    _L0_ffn_all = _L0_ffn_setup()
    _L0_ffn_in = {k: v for k, v in _L0_ffn_all.items() if k in ('gate_weight', 'Wg', 'Wu', 'Wd', 'Sg', 'Su', 'Sd')}
    del _L0_ffn_all
    return {'x': x, 'ctx_2048': ctx_2048, 'g_xattn': g_xattn, 'g_ffn': g_ffn, 'L0_xattn_QW': _L0_xattn_in['QW'], 'L0_xattn_Qb': _L0_xattn_in['Qb'], 'L0_xattn_KW': _L0_xattn_in['KW'], 'L0_xattn_Kb': _L0_xattn_in['Kb'], 'L0_xattn_VW': _L0_xattn_in['VW'], 'L0_xattn_Vb': _L0_xattn_in['Vb'], 'L0_ffn_gate_weight': _L0_ffn_in['gate_weight'], 'L0_ffn_Wg': _L0_ffn_in['Wg'], 'L0_ffn_Wu': _L0_ffn_in['Wu'], 'L0_ffn_Wd': _L0_ffn_in['Wd'], 'L0_ffn_Sg': _L0_ffn_in['Sg'], 'L0_ffn_Su': _L0_ffn_in['Su'], 'L0_ffn_Sd': _L0_ffn_in['Sd']}

def reference(x, ctx_2048, g_xattn, g_ffn, L0_xattn_QW, L0_xattn_Qb, L0_xattn_KW, L0_xattn_Kb, L0_xattn_VW, L0_xattn_Vb, L0_ffn_gate_weight, L0_ffn_Wg, L0_ffn_Wu, L0_ffn_Wd, L0_ffn_Sg, L0_ffn_Su, L0_ffn_Sd):
    import jax
    import jax.numpy as jnp

    def _L0_xattn_ref(X1, X2, QW, Qb, KW, Kb, VW, Vb):
        import jax, jax.numpy as jnp
        import numpy as np
        N, D, L = (8, 128, 256)
        q = jnp.einsum('ndl,ed->nle', X1, QW) + Qb
        k = jnp.einsum('ndl,ed->nle', X2, KW) + Kb
        v = jnp.einsum('ndl,ed->nle', X2, VW) + Vb
        scores = jnp.einsum('nqd,nkd->nqk', q, k)
        attn = jax.nn.softmax(scores, axis=-1)
        H = jnp.einsum('nqk,nkd->nqd', attn, v)
        return jnp.swapaxes(H, -1, -2)

    def _L0_ffn_ref(hidden_states, gate_weight, Wg, Wu, Wd, Sg, Su, Sd):
        import jax, jax.numpy as jnp
        import numpy as np
        TOP_K = 6
        N_GROUP = 8
        TOPK_GROUP = 3
        CAPACITY = 96
        RSF = 1.0
        B, S, H = hidden_states.shape
        E, M, _ = Wg.shape
        K, NG, TG, C = (TOP_K, N_GROUP, TOPK_GROUP, CAPACITY)
        x = hidden_states.reshape(-1, H)
        T = x.shape[0]
        logits = x.astype(jnp.float32) @ gate_weight.astype(jnp.float32).T
        scores = jax.nn.softmax(logits, axis=-1)
        group_scores = scores.reshape(T, NG, E // NG).max(axis=-1)
        _, gidx = jax.lax.top_k(group_scores, TG)
        gmask = jnp.zeros((T, NG), scores.dtype).at[jnp.arange(T)[:, None], gidx].set(1.0)
        smask = jnp.repeat(gmask, E // NG, axis=1)
        tmp_scores = jnp.where(smask > 0, scores, 0.0)
        topk_w, topk_i = jax.lax.top_k(tmp_scores, K)
        topk_w = topk_w * RSF
        flat = topk_i.reshape(-1)
        oh = jax.nn.one_hot(flat, E, dtype=jnp.int32)
        pos = jnp.sum(jnp.cumsum(oh, axis=0) * oh, axis=-1) - 1
        slot = flat * C + jnp.minimum(pos, C - 1)
        tok = jnp.arange(T * K) // K
        buf = jnp.zeros((E * C, H), x.dtype).at[slot].set(x[tok]).reshape(E, C, H)
        g = jnp.einsum('ech,emh->ecm', buf, Wg)
        u = jnp.einsum('ech,emh->ecm', buf, Wu)
        out = jnp.einsum('ecm,ehm->ech', jax.nn.silu(g) * u, Wd).reshape(E * C, H)
        yk = out[slot].reshape(T, K, H)
        y = jnp.sum(yk * topk_w[..., None].astype(yk.dtype), axis=1)
        shared = jax.nn.silu(x @ Sg.T) * (x @ Su.T) @ Sd.T
        return (y + shared).reshape(B, S, H)
    x = x + jnp.tanh(g_xattn[0]) * _L0_xattn_ref(_layernorm(x, axis=-1), ctx_2048, L0_xattn_QW, L0_xattn_Qb, L0_xattn_KW, L0_xattn_Kb, L0_xattn_VW, L0_xattn_Vb)
    x = x + jnp.tanh(g_ffn[0]) * _L0_ffn_ref(_layernorm(x, axis=-1), L0_ffn_gate_weight, L0_ffn_Wg, L0_ffn_Wu, L0_ffn_Wd, L0_ffn_Sg, L0_ffn_Su, L0_ffn_Sd)
    return x

_drawn_inputs = setup_inputs


def setup_inputs(seed=0):
    import zlib

    import numpy as np

    out = dict(_drawn_inputs(seed))
    spreads = {'L0_xattn_Qb': (0.0, 0.1), 'L0_xattn_Kb': (0.0, 2.0), 'L0_xattn_Vb': (0.0, 0.512)}
    factors = {'L0_ffn_gate_weight': 8.0,
     'L0_ffn_Wg': 8.0,
     'L0_ffn_Wu': 8.0,
     'L0_ffn_Wd': 8.0,
     'L0_ffn_Sg': 4.011,
     'L0_ffn_Su': 3.977,
     'L0_ffn_Sd': 3.986}
    for name, (base, spread) in spreads.items():
        noise = np.random.default_rng([zlib.crc32(name.encode()), seed]).standard_normal(out[name].shape)
        drawn = base * np.exp(spread * noise) if base else spread * noise
        out[name] = jnp.asarray(drawn.astype(out[name].dtype))
    for name, factor in factors.items():
        out[name] = (out[name] * factor).astype(out[name].dtype)
    return out
```

```python
from contextlib import ExitStack

import concourse.bass as bass
from concourse import mybir

F32 = mybir.dt.float32
BF16 = mybir.dt.bfloat16
I32 = mybir.dt.int32
U32 = mybir.dt.uint32
ACT = mybir.ActivationFunctionType
ALU = mybir.AluOpType
AX = mybir.AxisListType.X

P = 128
N = 16
PAIRS = N // 2
L = 256
H2 = L // P
T = N * P
E = 64
K = 6
NG = 8
TG = 3
C = 96
LAST = C - 1
M = 176
MH = M // 2
MS = 352
MT = [(0, 128), (128, 128), (256, 96)]
EPS = 1e-5
W = 16
FAR = 8192
GE = 2
GROUPS = E // GE
RING = 12
SAVED = 4
GU = H2 * 2 * M
DW = 2 * L
AHEAD = 6
ROWS = 8
OUTS = 8
MAGIC = 1597463007.0
K_ATT = 21
K_ROUTE = 33


def wait(eng, sem, value):
    if not isinstance(value, int) or value > 0:
        eng.wait_ge(sem, value)


def wait_apart(eng, sem, value, waited):
    wait(eng, sem, value)
    if not isinstance(value, int):
        eng.sem_inc(waited, 1)


class Steps:

    def __init__(self, eng, sem, base):
        self.eng, self.sem, self.base, self.n = eng, sem, base, 0

    def did(self, instruction):
        instruction.then_inc(self.sem, 1)
        self.n += 1

    def settled(self, waited=None):
        if waited is None:
            wait(self.eng, self.sem, self.base + self.n)
        else:
            wait_apart(self.eng, self.sem, self.base + self.n, waited)


def build(nc, x, ctx, cols, qkv, gate, sgu, sd, sd2, wgu, wd, out):
    xn_dram = nc.dram_tensor("xn_rows", (T + C, L), F32).ap()
    acc_dram = [nc.dram_tensor(f"acc_rows{i}", (T + C, L), F32).ap() for i in range(2)]
    table_dram = nc.dram_tensor("slot_table", (C * E, W), F32).ap()
    last_dram = nc.dram_tensor("last_rows", (E, L), F32).ap()

    with ExitStack() as stack:
        def sb(name, shape, dt=F32):
            return stack.enter_context(nc.sbuf_tensor(name, shape, dt))

        def sem(name):
            return stack.enter_context(nc.semaphore(name))

        ident = sb("ident", [P, P])
        ident_b = sb("ident_b", [P, P], BF16)
        before = sb("before", [P, P], BF16)
        ones_b = sb("ones_b", [P, P], BF16)
        iota_g = sb("iota_g", [P, NG])
        iota_e = sb("iota_e", [P, E])
        row_id = sb("row_id", [P, 1])
        is_last = sb("is_last", [P, 1])
        last_dump = sb("last_dump", [P, 1])
        token = sb("token", [P, N])
        fill0 = sb("fill0", [P, 1])
        zeros = sb("zeros", [P, 1024])
        cols_sb = sb("cols_sb", [P, 5])
        tanh_g = sb("tanh_g", [P, 2])
        vb_g = sb("vb_g", [P, 1])
        qkv_sb = sb("qkv_sb", [P, 3 * P])
        gate_sb = sb("gate_sb", [P, H2, E])
        sgu_sb = sb("sgu_sb", [P, H2, 2 * MS])
        sd_sb = sb("sd_sb", [P, 3, L])
        x_all = sb("x_all", [P, N, L])
        ctx_sb = sb("ctx_sb", [P, 2, 2, L])
        stats = sb("stats", [P, N, 6])
        mv = sb("mv", [P, N, 2])
        rstd1 = sb("rstd1", [P, N])
        shift1 = sb("shift1", [P, N])
        x1n = sb("x1n", [P, 2, L])
        qk_sb = sb("qk_sb", [P, 2, 2 * L])
        v_sb = sb("v_sb", [P, 2, 2 * P])
        neg_max = sb("neg_max", [P, 2, 2])
        p_sb = sb("p_sb", [P, 2, 2, L])
        p_sum = sb("p_sum", [P, 2, 2])
        p_inv = sb("p_inv", [P, 2, 2])
        pt_sb = sb("pt_sb", [P, 2, 2 * L])
        h_sb = sb("h_sb", [P, 2, 2, P])
        stats2 = sb("stats2", [P, 2, 6])
        mv2 = sb("mv2", [P, 2, 2])
        var2 = sb("var2", [P, 2])
        nhalf = sb("nhalf", [P, 2])
        guess = sb("guess", [P, 2])
        newt = sb("newt", [P, 2])
        xn2 = sb("xn2", [P, 2, L])
        xt_sb = sb("xt_sb", [P, H2, 2 * P])
        lg_max = sb("lg_max", [P, 2])
        es = sb("es", [P, 2, E])
        es_sum = sb("es_sum", [P, 2])
        es_inv = sb("es_inv", [P, 2])
        score = sb("score", [P, 2, E])
        g_max = sb("g_max", [P, 2, NG])
        g_top = sb("g_top", [P, 2, 8])
        g_idx = sb("g_idx", [P, 2, 8], U32)
        g_eq = sb("g_eq", [P, 2, NG, TG])
        g_mask = sb("g_mask", [P, 2, NG])
        kept = sb("kept", [P, 2, E])
        e_top = sb("e_top", [P, 2, 8])
        e_idx = sb("e_idx", [P, 2, 8], U32)
        pick = sb("pick", [P, 2, K, E], BF16)
        counts = sb("counts", [P, E])
        pos = sb("pos", [P, 2, E])
        newest = sb("newest", [P, E])
        over = sb("over", [P, 2, E])
        w_over = sb("w_over", [P, 2, E])
        pos_pick = sb("pos_pick", [P, 2, K, E])
        pos_k = sb("pos_k", [P, 2, K])
        far_k = sb("far_k", [P, 2, K])
        row_k = sb("row_k", [P, 2, K])
        slot_idx = sb("slot_idx", [P, 2, 2 * K], I32)
        meta = sb("meta", [P, 2, 2 * K, W])
        w_over_t = sb("w_over_t", [E, T])
        tanh_sb = sb("tanh_sb", [P, 2, 2 * P])
        half_sb = sb("half_sb", [P, 2, 2 * P])
        act_t = sb("act_t", [P, 3, 2 * P])
        w_ring = sb("w_ring", [P, RING * GE * GU])
        d_ring = sb("d_ring", [MH, RING * GE * DW])
        table = sb("table", [C, E * W])
        table_fill = table
        gidx = sb("gidx", [C, E], I32)
        sidx = sb("sidx", [C, E], I32)
        slot_w = sb("slot_w", [C, E])
        newest_col = sb("newest_col", [E, 1])
        newest_sel = sb("newest_sel", [E, C])
        gidx_now = sb("gidx_now", [C, 8 + AHEAD], I32)
        sidx_now = sb("sidx_now", [C, 8], I32)
        rows = x_all[0:C, OUTS:OUTS + ROWS, :]
        rows_t = p_sb[:, :, :, :].rearrange("p a h f -> p (a h f)")[:, 0:2 * H2 * C]\
            .rearrange("p (a f) -> p a f", a=2)
        silu_sb = pt_sb[0:C, :, 0:M]
        act_sb = sb("act_sb", [C, 2, M])
        act_tt = sb("act_tt", [MH, 2, 2 * C])
        outs = x_all[0:C, 0:OUTS, :]
        acc1 = w_ring[:, 0:N * L].rearrange("p (n f) -> p n f", n=N)
        last_sb = w_ring[0:E, N * L:(N + 1) * L]

        bank = [stack.enter_context(nc.psum_tensor(f"bank{i}", [P, 512], F32)) for i in range(8)]

        s = {name: sem(name) for name in """
            x_in0 x_in1 x_in2 x_in3 small_in ctx_in0 ctx_in1 fills_in
            ident_ready consts_ready dve_setup tanh_ready setup_step stats_ready std_ready norm1_ready
            x1n_ready x_plus qk_done v_done qk_out v_out s_done nmax_ready p_ready p_inv_ready
            pt_done pt_out h_done h_out ht_done x1_ready att_step xn2_ready xn_saved
            xt_done xt_out lg_done lgmax_ready es_ready route_step pick_ready pos_done wov_ready
            wovt_done wov_out slots_ready meta_in0 meta_in1 gu_done th_ready act_ready down_done y_ready y_saved
            w_in0 w_in1 table_in newest_t newest_ready newest_mm tables_ready table_step
            idx_now rows_in0 rows_in1 rows_in2 rows_in3
            rows_in4 rows_in5 rows_in6 rows_in7 t_done t_out eg_done silu_ready a_ready
            at_done at_out o_done o_ready acc_in0 acc_in1 lasts_saved0 lasts_saved1 lasts_in
            acc0_back0 acc0_back1 ov_done sum_step sum_ready result_saved waited_dve waited_pe waited_pool""".split()}

        block = stack.enter_context(nc.Block())

        @block.sync
        def _(sp):
            for i in range(4):
                sp.dma_start(x_all[:, 4 * i:4 * i + 4, :], x[:, 4 * i:4 * i + 4, :]).then_inc(s[f"x_in{i}"], 16)
            sp.wait_ge(s["dve_setup"], 1)
            zero4 = zeros[:, :].rearrange("p (a f) -> p a f", a=1).to_broadcast([P, 4, 1024])
            sp.dma_start(acc_dram[1][0:T, :].rearrange("(p a) f -> p (a f)", p=P)
                         .rearrange("p (a f) -> p a f", a=4), zero4).then_inc(s["fills_in"], 16)
            for d in (xn_dram, acc_dram[0], acc_dram[1]):
                sp.dma_start(d[T:T + C, :], zeros[0:C, 0:L]).then_inc(s["fills_in"], 16)
            sp.wait_ge(s["dve_setup"], 3)
            sp.dma_start(table_dram.rearrange("(c e) w -> c (e w)", c=C), table_fill[:, :])\
                .then_inc(s["fills_in"], 16)

            def load_weights(g, par):
                fixed = isinstance(g, int)
                at = g % RING if fixed else sp.snap(g % RING)
                at_gu = at * (GE * GU) if fixed else sp.snap(at * (GE * GU))
                at_d = at * (GE * DW) if fixed else sp.snap(at * (GE * DW))
                landed = (g // 2) * 32 if fixed else sp.snap((g // 2) * 32)
                freed = (g - RING + 1) * GE if fixed else sp.snap((g - RING + 1) * GE)
                wait(sp, s[f"w_in{par}"], landed)
                wait(sp, s["o_done"], freed)
                sp.dma_start(w_ring[:, bass.ds(at_gu, GE * GU)], wgu[g]).then_inc(s[f"w_in{par}"], 16)
                sp.dma_start(d_ring[:, bass.ds(at_d, GE * DW)], wd[g]).then_inc(s[f"w_in{par}"], 16)

            def saves(r, att, route):
                if att:
                    lo = r * (2 * P)
                    wait(sp, s["xn2_ready"], r + 1)
                    sp.dma_start(xn_dram[bass.ds(lo, 2 * P), :].rearrange("(n p) f -> p n f", p=P),
                                 xn2[:, :, :]).then_inc(s["xn_saved"], 16)
                if route:
                    lo = (r - 1) * (2 * P)
                    wait(sp, s["y_ready"], 2 * r)
                    sp.dma_start(acc_dram[0][bass.ds(lo, 2 * P), :].rearrange("(n p) f -> p n f", p=P),
                                 x_all[:, bass.ds(2 * r - 2, 2), :]).then_inc(s["y_saved"], 16)

            for r in range(PAIRS):
                for g in range(2 * r, min(2 * r + 2, RING)):
                    load_weights(g, g % 2)
                saves(r, True, r > 0)
            saves(PAIRS, False, True)

            sp.wait_ge(s["meta_in0"], 16 * K * N // 2)
            sp.wait_ge(s["meta_in1"], 16 * K * N // 2)
            sp.dma_start(table[:, :], table_dram.rearrange("(c e) w -> c (e w)", c=C)).then_inc(s["table_in"], 16)

            with sp.Fori(RING // 2, GROUPS // 2) as h:
                for par in range(2):
                    load_weights(2 * h + par, par)

            sp.wait_ge(s["acc_in0"], 16 * E // 2)
            sp.wait_ge(s["acc_in1"], 16 * E // 2)
            for par in range(2):
                sp.wait_ge(s[f"lasts_saved{par}"], 8 * E // SAVED)
            sp.dma_start(last_sb, last_dram).then_inc(s["lasts_in"], 16)

            for h in range(2):
                half = slice(h * T // 2, (h + 1) * T // 2)
                for acc, to in ((acc_dram[0], x_all), (acc_dram[1], acc1)):
                    sp.dma_start(to[:, h * N // 2:(h + 1) * N // 2, :],
                                 acc[half, :].rearrange("(n p) f -> p n f", p=P))\
                        .then_inc(s[f"acc0_back{h}"], 16)
            for r in range(PAIRS):
                sp.wait_ge(s["sum_ready"], r + 1)
                sp.dma_start(out[:, 2 * r:2 * r + 2, :], x_all[:, 2 * r:2 * r + 2, :]).then_inc(s["result_saved"], 16)
            sp.wait_ge(s["result_saved"], 16 * PAIRS)

        qk_ps = bank[0]
        v_ps = bank[1][:, 0:L]
        down_ps = [bank[1][:, L:2 * L], bank[0][:, 0:L]]
        s_ps = bank[2]
        pt_ps = bank[3]
        h_ps = bank[4][:, 0:L]
        ht_ps = bank[4][:, L:2 * L]
        wt_ps = bank[3][0:E, 0:2 * P]
        gu_ps = [bank[6], bank[5], bank[6]]
        xt_ps = bank[5]
        lg_ps = bank[7][:, 0:2 * E]
        pos_ps = bank[7][:, 2 * E:4 * E]
        sel_ps = bank[7][:, 4 * E:6 * E]
        cnt_ps = bank[7][:, 6 * E:7 * E]

        @block.tensor
        def _(pe):
            def mm(o, lhsT, rhs, start=True, stop=True):
                return pe.matmul(o, lhsT, rhs, start=start, stop=stop, skip_group_check=True)

            def project(r, i):
                t = 2 * r + i
                wait(pe, s["x1n_ready"], t + 1)
                wait(pe, s["qk_out"], t)
                if i == 0:
                    wait(pe, s["y_ready"], 2 * r - 2)
                mm(qk_ps[:, 0:L], qkv_sb[:, 0:P], x1n[:, i, :])
                c = ctx_sb[:, ctx_par[0], i, :]
                mm(qk_ps[:, L:2 * L], qkv_sb[:, P:2 * P], c).then_inc(s["qk_done"], 1)
                wait(pe, s["v_out"], t)
                for h in range(2):
                    last = mm(v_ps[:, h * P:(h + 1) * P], c[:, h * P:(h + 1) * P], qkv_sb[:, 2 * P:3 * P])
                last.then_inc(s["v_done"], 1)

            def scores(r, i):
                t = 2 * r + i
                wait(pe, s["qk_out"], t + 1)
                wait(pe, s["p_ready"], t)
                for h in range(2):
                    last = mm(s_ps[:, h * L:(h + 1) * L], qk_sb[:, i, h * P:(h + 1) * P], qk_sb[:, i, L:2 * L])
                last.then_inc(s["s_done"], 1)

            def turn_p(r, i):
                t = 2 * r + i
                wait(pe, s["p_ready"], t + 1)
                wait(pe, s["pt_out"], t)
                if i == 0:
                    wait(pe, s["wov_out"], r - 1)
                for h in range(2):
                    for k in range(2):
                        last = pe.transpose(pt_ps[:, k * L + h * P:k * L + (h + 1) * P],
                                            p_sb[:, i, h, k * P:(k + 1) * P], ident[:, :])
                last.then_inc(s["pt_done"], 1)

            def attend(r, i):
                t = 2 * r + i
                wait(pe, s["pt_out"], t + 1)
                wait(pe, s["v_out"], t + 1)
                wait(pe, s["x1_ready"], t)
                for h in range(2):
                    for k in range(2):
                        last = mm(h_ps[:, h * P:(h + 1) * P], pt_sb[:, i, k * L + h * P:k * L + (h + 1) * P],
                                  v_sb[:, i, k * P:(k + 1) * P], start=k == 0, stop=k == 1)
                last.then_inc(s["h_done"], 1)

            def turn_h(r, i):
                t = 2 * r + i
                wait(pe, s["h_out"], t + 1)
                for h in range(2):
                    last = pe.transpose(ht_ps[:, h * P:(h + 1) * P], h_sb[:, i, h, :], ident[:, :])
                last.then_inc(s["ht_done"], 1)

            def turn_x(r):
                wait(pe, s["xn2_ready"], r)
                wait(pe, s["act_ready"], 3 * (r - 1) - 1)
                for i in range(2):
                    for h in range(H2):
                        last = pe.transpose(xt_ps[:, h * L + i * P:h * L + (i + 1) * P],
                                            xn2[:, i, h * P:(h + 1) * P], ident[:, :])
                last.then_inc(s["xt_done"], 1)

            def logits(r):
                wait(pe, s["xt_out"], r)
                wait(pe, s["wov_ready"], r - 1)
                for i in range(2):
                    for h in range(H2):
                        last = mm(lg_ps[:, i * E:(i + 1) * E], xt_sb[:, h, i * P:(i + 1) * P], gate_sb[:, h, :],
                                  start=h == 0, stop=h == H2 - 1)
                last.then_inc(s["lg_done"], 1)

            def shared_up(r, m):
                lo, n = MT[m]
                if m == 0:
                    wait(pe, s["xt_out"], r)
                    wait(pe, s["act_ready"], 3 * (r - 1))
                if m == 2:
                    wait(pe, s["act_ready"], 3 * r - 2)
                for b in range(2):
                    for h in range(H2):
                        last = mm(gu_ps[m][0:n, b * L:(b + 1) * L], sgu_sb[:, h, b * MS + lo:b * MS + lo + n],
                                  xt_sb[:, h, :], start=h == 0, stop=h == H2 - 1)
                last.then_inc(s["gu_done"], 1)

            def places(r):
                wait(pe, s["pick_ready"], r)
                wait(pe, s["slots_ready"], r - 1)
                for k in range(K):
                    mm(pos_ps[:, 0:E], before[:, :], pick[:, 0, k, :], start=k == 0, stop=k == K - 1)
                for k in range(K):
                    mm(pos_ps[:, E:2 * E], before[:, :], pick[:, 1, k, :], start=k == 0, stop=False)
                for k in range(K):
                    mm(pos_ps[:, E:2 * E], ones_b[:, :], pick[:, 0, k, :], start=False, stop=k == K - 1)
                for i in range(2):
                    for k in range(K):
                        mm(sel_ps[:, i * E:(i + 1) * E], ident_b[:, :], pick[:, i, k, :],
                           start=k == 0, stop=k == K - 1)
                for i in range(2):
                    for k in range(K):
                        last = mm(cnt_ps, ones_b[:, :], pick[:, i, k, :],
                                  start=i + k == 0, stop=i + k == K)
                last.then_inc(s["pos_done"], 1)

            def shared_down(r, i):
                wait(pe, s["act_ready"], 3 * r)
                for m, (lo, n) in enumerate(MT):
                    last = mm(down_ps[i], act_t[0:n, m, i * P:(i + 1) * P], sd_sb[0:n, m, :],
                              start=m == 0, stop=m == 2)
                last.then_inc(s["down_done"], 1)

            def turn_w(r, att):
                if att:
                    wait(pe, s["pt_out"], 2 * r + 2)
                wait_apart(pe, s["wov_ready"], r, waited)
                for i in range(2):
                    last = pe.transpose(wt_ps[:, i * P:(i + 1) * P], w_over[:, i, :], ident[:, :])
                last.then_inc(s["wovt_done"], 1)

            ctx_par = [0]
            waited = s["waited_pe"]
            pe.wait_ge(s["ident_ready"], 2)
            pe.wait_ge(s["consts_ready"], 3)
            pe.wait_ge(s["small_in"], 16 * 6)

            def step(r, att, route, par=0):
                ctx_par[0] = par
                if att:
                    wait(pe, s[f"ctx_in{par}"], r * 8 + 16 - 8 * par)
                    project(r, 0)
                    scores(r, 0)
                if route:
                    turn_x(r)
                if att:
                    project(r, 1)
                if route:
                    logits(r)
                    shared_up(r, 0)
                if att:
                    turn_p(r, 0)
                    scores(r, 1)
                if route:
                    shared_up(r, 1)
                if att:
                    attend(r, 0)
                    turn_p(r, 1)
                if route:
                    places(r)
                if att:
                    turn_h(r, 0)
                if route:
                    shared_up(r, 2)
                if att:
                    attend(r, 1)
                if route:
                    shared_down(r, 0)
                if att:
                    turn_h(r, 1)
                if route:
                    shared_down(r, 1)
                    turn_w(r, att)

            step(0, True, False, 0)
            step(1, True, True, 1)
            with pe.Fori(1, PAIRS // 2) as h:
                step(2 * h, True, True, 0)
                step(2 * h + 1, True, True, 1)
            step(PAIRS, False, True)

            nt_ps, nr_ps = bank[0][0:E, 0:P], bank[0][0:C, P:P + E]
            pe.wait_ge(s["route_step"], K_ROUTE * PAIRS)
            pe.wait_ge(s["y_ready"], N)
            pe.transpose(nt_ps, newest[:, :], ident[:, :]).then_inc(s["newest_t"], 1)
            pe.wait_ge(s["newest_ready"], 1)
            mm(nr_ps, newest_sel[:, :], ident[0:E, 0:E]).then_inc(s["newest_mm"], 1)

            t_ps = bank[2][:, 0:H2 * C]
            at_ps = bank[3][0:MH, 0:2 * C]
            eg_ps = [bank[4][0:C, 0:2 * M], bank[5][0:C, 0:2 * M]]
            o_ps = [bank[6][0:C, 0:L], bank[7][0:C, 0:L]]

            def turn_rows(e, b):
                wait(pe, s[f"rows_in{b % ROWS}"], (e - b % ROWS) * (16 // ROWS) + 16)
                wait(pe, s["t_out"], e)
                for h in range(H2):
                    last = pe.transpose(t_ps[:, h * C:(h + 1) * C], rows[:, b % ROWS, h * P:(h + 1) * P],
                                        ident[0:C, 0:C])
                last.then_inc(s["t_done"], 1)

            def at_ring(e, words):
                return e % (RING * GE) * words

            def up(e, b):
                if b % GE == 0:
                    wait(pe, s[f"w_in{b // GE % 2}"], e * (16 // GE) + 32 - 16 * (b // GE % 2))
                at = at_ring(e, GU)
                at = at if isinstance(at, int) else pe.snap(at)
                wait(pe, s["t_out"], e + 1)
                wait(pe, s["a_ready"], e - 1)
                for h in range(H2):
                    last = mm(eg_ps[b % 2], rows_t[:, b % 2, h * C:(h + 1) * C],
                              w_ring[:, bass.ds(at + h * 2 * M, 2 * M)], start=h == 0, stop=h == H2 - 1)
                last.then_inc(s["eg_done"], 1)

            def turn_act(e, b):
                wait(pe, s["a_ready"], e + 1)
                wait(pe, s["at_out"], e)
                for m in range(2):
                    last = pe.transpose(at_ps[:, m * C:(m + 1) * C], act_sb[:, b % 2, m * MH:(m + 1) * MH],
                                        ident[0:C, 0:C])
                last.then_inc(s["at_done"], 1)

            def down(e, b):
                at = at_ring(e, DW)
                at = at if isinstance(at, int) else pe.snap(at)
                wait(pe, s["at_out"], e + 1)
                wait(pe, s["o_ready"], e - 1)
                for m in range(2):
                    last = mm(o_ps[b % 2], act_tt[:, b % 2, m * C:(m + 1) * C],
                              d_ring[:, bass.ds(at + m * L, L)], start=m == 0, stop=m == 1)
                last.then_inc(s["o_done"], 1)

            def expert(e, b):
                known = isinstance(e, int)
                if not known or e < E - 1:
                    turn_rows(e + 1, b + 1)
                if not known or e < E:
                    up(e, b)
                if not known or e > 1:
                    down(e - 2, b - 2)
                if not known or 0 < e <= E:
                    turn_act(e - 1, b - 1)

            pe.wait_ge(s["x1_ready"], N)
            pe.wait_ge(s["es_ready"], PAIRS)
            pe.wait_ge(s["slots_ready"], PAIRS)
            pe.wait_ge(s["wov_out"], PAIRS)
            pe.wait_ge(s["act_ready"], 3 * PAIRS)
            turn_rows(0, 0)
            for e in range(10):
                expert(e, e)
            with pe.Fori(1, E // 8 - 1) as q:
                for b in range(2, 10):
                    expert(8 * q + b, b)
            for e in range(E - 6, E + 2):
                expert(e, e)

            pe.wait_ge(s["lasts_in"], 16)
            for t in range(N):
                r, i = t // 2, t % 2
                wait(pe, s["sum_ready"], r - 3)
                mm(bank[r % 4][:, i * L:(i + 1) * L], w_over_t[:, t * P:(t + 1) * P], last_sb)\
                    .then_inc(s["ov_done"], 1)

        @block.scalar
        def _(act):
            act.dma_start(cols_sb[:, :], cols).then_inc(s["small_in"], 16)
            act.dma_start(qkv_sb[:, :], qkv).then_inc(s["small_in"], 16)
            act.dma_start(ctx_sb[:, 0, :, :], ctx[:, 0:2, :]).then_inc(s["ctx_in0"], 16)
            act.dma_start(ctx_sb[:, 1, :, :], ctx[:, 2:4, :]).then_inc(s["ctx_in1"], 16)
            act.dma_start(gate_sb[:, :, :], gate).then_inc(s["small_in"], 16)
            act.dma_start(sgu_sb[:, :, :], sgu).then_inc(s["small_in"], 16)
            act.dma_start(sd_sb[:, 0:2, :], sd).then_inc(s["small_in"], 16)
            act.dma_start(sd_sb[0:MT[2][1], 2, :], sd2).then_inc(s["small_in"], 16)

            act.wait_ge(s["stats_ready"], 1)
            act.activation(rstd1[:, :], rstd1[:, :], ACT.Sqrt).then_inc(s["std_ready"], 1)
            act.wait_ge(s["small_in"], 96)
            act.activation(tanh_g[:, :], cols_sb[:, 3:5], ACT.Tanh).then_inc(s["tanh_ready"], 1)

            def norm1(r, i):
                t = 2 * r + i
                wait(act, s["norm1_ready"], 1)
                wait(act, s["qk_done"], t - 1)
                at = t if isinstance(t, int) else act.snap(t)
                act.activation(x1n[:, i, :], x_all[:, bass.ds(at, 1), :].rearrange("p a f -> p (a f)"),
                               ACT.Identity, scale=rstd1[:, bass.ds(at, 1)], bias=shift1[:, bass.ds(at, 1)])\
                    .then_inc(s["x1n_ready"], 1)

            def take_qkv(r, i):
                t = 2 * r + i
                wait(act, s["qk_done"], t + 1)
                wait(act, s["s_done"], t - 1)
                act.activation(qk_sb[:, i, 0:L], qk_ps[:, 0:L], ACT.Identity, bias=cols_sb[:, 0:1])
                act.activation(qk_sb[:, i, L:2 * L], qk_ps[:, L:2 * L], ACT.Identity, bias=cols_sb[:, 1:2])\
                    .then_inc(s["qk_out"], 1)
                wait(act, s["v_done"], t + 1)
                wait(act, s["h_done"], t - 1)
                act.activation(v_sb[:, i, :], v_ps, ACT.Copy).then_inc(s["v_out"], 1)

            def exps(r, i):
                t = 2 * r + i
                wait(act, s["nmax_ready"], t + 1)
                wait(act, s["pt_done"], t - 1)
                wait(act, s["p_inv_ready"], t - 1)
                for h in range(2):
                    last = act.activation(p_sb[:, i, h, :], s_ps[:, h * L:(h + 1) * L], ACT.Exp,
                                          bias=neg_max[:, i, h:h + 1], accum_out=p_sum[:, i, h:h + 1])
                last.then_inc(s["p_ready"], 1)

            def take_pt(r, i):
                t = 2 * r + i
                wait(act, s["pt_done"], t + 1)
                wait(act, s["h_done"], t - 1)
                act.activation(pt_sb[:, i, :], pt_ps[:, :], ACT.Copy).then_inc(s["pt_out"], 1)

            def take_h(r, i):
                t = 2 * r + i
                wait(act, s["h_done"], t + 1)
                wait(act, s["p_inv_ready"], t + 1)
                wait(act, s["ht_done"], t - 1)
                for h in range(2):
                    last = act.activation(h_sb[:, i, h, :], h_ps[:, h * P:(h + 1) * P], ACT.Copy,
                                          scale=p_inv[:, i, h:h + 1])
                last.then_inc(s["h_out"], 1)

            def take_xt(r):
                wait(act, s["xt_done"], r)
                wait(act, s["gu_done"], 3 * (r - 1))
                act.activation(xt_sb[:, :, :].rearrange("p h t -> p (h t)"), xt_ps[:, :], ACT.Copy)\
                    .then_inc(s["xt_out"], 1)

            def exp_logits(r):
                wait(act, s["lgmax_ready"], r)
                for i in range(2):
                    last = act.activation(es[:, i, :], lg_ps[:, i * E:(i + 1) * E], ACT.Exp,
                                          bias=lg_max[:, i:i + 1], accum_out=es_sum[:, i:i + 1])
                last.then_inc(s["es_ready"], 1)

            def tanh_part(r, m):
                lo, n = MT[m]
                wait(act, s["gu_done"], 3 * (r - 1) + m + 1)
                b = m % 2
                wait(act, s["act_ready"], 3 * (r - 1) + m - 1 - (m == 0))
                act.activation(tanh_sb[0:n, b, :], gu_ps[m][0:n, 0:L], ACT.Tanh, scale=0.5)\
                    .then_inc(s["th_ready"], 1)

            def take_wov(r):
                wait(act, s["wovt_done"], r)
                at = (r - 1) * (2 * P)
                at = at if isinstance(at, int) else act.snap(at)
                act.activation(w_over_t[:, bass.ds(at, 2 * P)], wt_ps, ACT.Copy,
                               scale=tanh_g[0:E, 1:2]).then_inc(s["wov_out"], 1)

            def step(r, att, route, par=0, load=True):
                if att:
                    take_qkv(r, 0)
                    exps(r, 0)
                if route:
                    take_xt(r)
                if att:
                    take_qkv(r, 1)
                    if load:
                        at = 2 * r + 4
                        at = at if isinstance(at, int) else act.snap(at)
                        act.dma_start(ctx_sb[:, par, :, :], ctx[:, bass.ds(at, 2), :]).then_inc(s[f"ctx_in{par}"], 16)
                if route:
                    exp_logits(r)
                    tanh_part(r, 0)
                if att:
                    take_pt(r, 0)
                    exps(r, 1)
                if route:
                    tanh_part(r, 1)
                if att:
                    take_h(r, 0)
                    take_pt(r, 1)
                if route:
                    tanh_part(r, 2)
                if att:
                    take_h(r, 1)
                    if not isinstance(r, int) or r < PAIRS - 1:
                        norm1(r + 1, 0)
                        norm1(r + 1, 1)
                if route:
                    take_wov(r)

            norm1(0, 0)
            norm1(0, 1)
            act.wait_ge(s["tanh_ready"], 1)
            step(0, True, False, 0)
            step(1, True, True, 1)
            with act.Fori(1, PAIRS // 2 - 1) as h:
                step(2 * h, True, True, 0)
                step(2 * h + 1, True, True, 1)
            step(PAIRS - 2, True, True, 0, load=False)
            step(PAIRS - 1, True, True, 1, load=False)
            step(PAIRS, False, True)

            t_ps = bank[2][:, 0:H2 * C]
            eg_ps = [bank[4][0:C, 0:2 * M], bank[5][0:C, 0:2 * M]]
            o_ps = [bank[6][0:C, 0:L], bank[7][0:C, 0:L]]

            def take_rows(e, b):
                wait(act, s["t_done"], e + 1)
                wait(act, s["eg_done"], e - 1)
                act.activation(rows_t[:, b % 2, :], t_ps, ACT.Copy).then_inc(s["t_out"], 1)

            def silu(e, b):
                wait(act, s["eg_done"], e + 1)
                wait(act, s["a_ready"], e - 1)
                act.activation(silu_sb[:, b % 2, :], eg_ps[b % 2][:, 0:M], ACT.Silu).then_inc(s["silu_ready"], 1)

            def take_out(e, b):
                at = e if isinstance(e, int) else act.snap(e)
                wait(act, s["o_done"], e + 1)
                wait(act, s[f"acc_in{b % 2}"], 8 * (e - OUTS) + 16 - 8 * (b % 2))
                wait(act, s[f"lasts_saved{b // SAVED % 2}"], 2 * (e - b % SAVED) - 8 * (b // SAVED % 2))
                act.activation(outs[:, b % OUTS, :], o_ps[b % 2], ACT.Copy, scale=slot_w[:, bass.ds(at, 1)])\
                    .then_inc(s["o_ready"], 1)

            def save_lasts(e, b):
                at = e - (SAVED - 1)
                at = at if isinstance(at, int) else act.snap(at)
                wait(act, s["o_ready"], e + 1)
                lo = (b - (SAVED - 1)) % OUTS
                act.dma_start(last_dram[bass.ds(at, SAVED), :].rearrange("(a e) f -> a e f", a=1),
                              outs[LAST:C, lo:lo + SAVED, :]).then_inc(s[f"lasts_saved{b // SAVED % 2}"], 16)

            def expert(e, b):
                known = isinstance(e, int)
                if not known or e < E - 1:
                    take_rows(e + 1, b + 1)
                if not known or e < E:
                    silu(e, b)
                if not known or e > 1:
                    take_out(e - 2, b - 2)
                    if b % SAVED == 1:
                        save_lasts(e - 2, b - 2)

            act.wait_ge(s["tables_ready"], 3)
            act.wait_ge(s["y_saved"], 16 * PAIRS)
            take_rows(0, 0)
            for e in range(11):
                expert(e, e)
            with act.Fori(0, (E - 16) // 8) as q:
                for b in range(11, 19):
                    expert(8 * q + b, b)
            for e in range(E - 5, E + 2):
                expert(e, e)

        @block.vector
        def _(dve):
            setup = Steps(dve, s["setup_step"], 0)
            waited = s["waited_dve"]
            dve.memset(zeros[:, :], 0.0).then_inc(s["dve_setup"], 1)
            setup.did(dve.memset(counts[:, :], 0.0))
            setup.did(dve.memset(newest[:, :], 0.0))
            setup.did(dve.memset(meta[:, :, :, :], 0.0))
            setup.did(dve.memset(table_fill[:, :], 0.0))
            dve.wait_ge(s["consts_ready"], 5)
            setup.did(dve.tensor_scalar(is_last[:, :], row_id[:, :], float(LAST), None, ALU.is_equal))
            setup.settled()
            setup.did(dve.tensor_scalar(last_dump[:, :], is_last[:, :], float(T + LAST), None, ALU.mult))
            setup.settled()
            setup.did(dve.scalar_tensor_tensor(fill0[:, :], row_id[:, :], float(T), last_dump[:, :],
                                               ALU.add, ALU.subtract))
            setup.settled()
            dve.tensor_copy(table_fill[:, :].bitcast(I32).rearrange("c (e w) -> c e w", w=W)[:, :, 0:1],
                            fill0[0:C, :].rearrange("c (a b) -> c a b", a=1).to_broadcast([C, E, 1]))\
                .then_inc(s["dve_setup"], 2)
            for t in range(N):
                if t % 4 == 0:
                    dve.wait_ge(s[f"x_in{t // 4}"], 16)
                setup.did(dve.bn_stats(stats[:, t, :], x_all[:, t, :]))
            setup.settled()
            for t in range(N):
                setup.did(dve.bn_aggr(mv[:, t, :], stats[:, t, :]))
            setup.settled()
            dve.tensor_scalar(rstd1[:, :], mv[:, :, 1], EPS, None, ALU.add).then_inc(s["stats_ready"], 1)
            dve.wait_ge(s["std_ready"], 1)
            setup.did(dve.reciprocal(rstd1[:, :], rstd1[:, :]))
            setup.settled()
            dve.scalar_tensor_tensor(shift1[:, :], mv[:, :, 0], -1.0, rstd1[:, :], ALU.mult, ALU.mult)\
                .then_inc(s["norm1_ready"], 1)
            dve.wait_ge(s["tanh_ready"], 1)
            dve.tensor_tensor(vb_g[:, :], cols_sb[:, 2:3], tanh_g[:, 0:1], ALU.mult).then_inc(s["dve_setup"], 1)

            def smax(r, i):
                t = 2 * r + i
                wait(dve, s["s_done"], t + 1)
                wait(dve, s["p_ready"], t - 1)
                dve.tensor_reduce(neg_max[:, i, :], s_ps[:, :].rearrange("p (h k) -> p h k", h=2), AX, ALU.max,
                                  negate=True).then_inc(s["nmax_ready"], 1)

            def inverse_sum(r, i):
                t = 2 * r + i
                wait(dve, s["p_ready"], t + 1)
                wait(dve, s["h_out"], t - 1)
                dve.reciprocal(p_inv[:, i, :], p_sum[:, i, :]).then_inc(s["p_inv_ready"], 1)

            def residual(r, i, at, go):
                t = 2 * r + i
                wait(dve, s["ht_done"], t + 1)
                wait(dve, s["x_plus"], t + 1)
                tile = x_all[:, at + i, :] if isinstance(at, int) else \
                    x_all[:, bass.ds(at + i, 1), :].rearrange("p a f -> p (a f)")
                dve.scalar_tensor_tensor(tile, ht_ps, tanh_g[:, 0:1], tile, ALU.mult, ALU.add)\
                    .then_inc(s["x1_ready"], 1)
                wait_apart(dve, s["x1_ready"], t + 1, waited)
                go.did(dve.bn_stats(stats2[:, i, :], tile))
                go.settled(waited)
                go.did(dve.bn_aggr(mv2[:, i, :], stats2[:, i, :]))

            def norm2(r, at, go):
                go.settled()
                go.did(dve.tensor_scalar(var2[:, :], mv2[:, :, 1], EPS, None, ALU.add))
                go.settled()
                go.did(dve.tensor_scalar(guess[:, :].bitcast(I32), var2[:, :].bitcast(I32), 1, None,
                                         ALU.logical_shift_right))
                go.did(dve.tensor_scalar(nhalf[:, :], var2[:, :], -0.5, None, ALU.mult))
                go.settled()
                go.did(dve.tensor_scalar(guess[:, :].bitcast(I32), guess[:, :].bitcast(I32), -1.0, MAGIC,
                                         ALU.mult, ALU.add))
                go.settled()
                for _ in range(3):
                    for i in range(2):
                        go.did(dve.tensor_scalar(newt[:, i:i + 1], guess[:, i:i + 1], guess[:, i:i + 1],
                                                 nhalf[:, i:i + 1], ALU.mult, ALU.mult))
                    go.settled()
                    for i in range(2):
                        go.did(dve.tensor_scalar(guess[:, i:i + 1], newt[:, i:i + 1], 1.5, guess[:, i:i + 1],
                                                 ALU.add, ALU.mult))
                    go.settled()
                wait(dve, s["xt_done"], r)
                wait(dve, s["xn_saved"], 16 * r)
                for i in range(2):
                    tile = x_all[:, at + i, :] if isinstance(at, int) else \
                        x_all[:, bass.ds(at + i, 1), :].rearrange("p a f -> p (a f)")
                    ins = dve.tensor_scalar(xn2[:, i, :], tile, mv2[:, i, 0:1], guess[:, i:i + 1],
                                            ALU.subtract, ALU.mult)
                    if i == 0:
                        go.did(ins)
                    else:
                        ins.then_inc(s["xn2_ready"], 1)

            def shared_act(r, m, go):
                lo, n = MT[m]
                wait(dve, s["th_ready"], 3 * (r - 1) + m + 1)
                wait(dve, s["down_done"], 2 * (r - 1))
                g, u = gu_ps[m][0:n, 0:L], gu_ps[m][0:n, L:2 * L]
                go.did(dve.scalar_tensor_tensor(half_sb[0:n, m % 2, :], tanh_sb[0:n, m % 2, :], 1.0, g,
                                                ALU.add, ALU.mult))
                go.settled()
                dve.scalar_tensor_tensor(act_t[0:n, m, :], half_sb[0:n, m % 2, :], 0.5, u, ALU.mult, ALU.mult)\
                    .then_inc(s["act_ready"], 1)

            def choose_groups(r, go):
                wait(dve, s["lg_done"], r)
                wait(dve, s["es_ready"], r - 1)
                dve.tensor_reduce(lg_max[:, :], lg_ps.rearrange("p (i e) -> p i e", i=2), AX, ALU.max, negate=True)\
                    .then_inc(s["lgmax_ready"], 1)
                wait(dve, s["es_ready"], r)
                go.did(dve.reciprocal(es_inv[:, :], es_sum[:, :]))
                go.settled()
                for i in range(2):
                    go.did(dve.tensor_scalar(score[:, i, :], es[:, i, :], es_inv[:, i:i + 1], None, ALU.mult))
                go.settled()
                go.did(dve.tensor_reduce(g_max[:, :, :], score[:, :, :].rearrange("p i (g e) -> p i g e", g=NG),
                                         AX, ALU.max))
                go.settled(waited)
                for i in range(2):
                    go.did(dve.max(g_top[:, i, :], g_max[:, i, :]))
                go.settled(waited)
                for i in range(2):
                    go.did(dve.max_index(g_idx[:, i, :], g_top[:, i, :], g_max[:, i, :]))
                go.settled()
                for i in range(2):
                    go.did(dve.tensor_tensor(
                        g_eq[:, i, :, :], iota_g[:, :].rearrange("p (g a) -> p g a", a=1).to_broadcast([P, NG, TG]),
                        g_idx[:, i, 0:TG].rearrange("p (a j) -> p a j", a=1).to_broadcast([P, NG, TG]),
                        ALU.is_equal))
                go.settled()
                go.did(dve.tensor_reduce(g_mask[:, :, :], g_eq[:, :, :, :], AX, ALU.add))
                go.settled()
                wait(dve, s["route_step"], K_ROUTE * (r - 1))
                go.did(dve.tensor_tensor(
                    kept[:, :, :].rearrange("p i (g e) -> p (i g) e", g=NG),
                    score[:, :, :].rearrange("p i (g e) -> p (i g) e", g=NG),
                    g_mask[:, :, :].rearrange("p i (g a) -> p (i g) a", a=1).to_broadcast([P, 2 * NG, E // NG]),
                    ALU.mult))

            def choose_experts(r, go):
                go.settled(waited)
                for i in range(2):
                    go.did(dve.max(e_top[:, i, :], kept[:, i, :]))
                go.settled(waited)
                for i in range(2):
                    go.did(dve.max_index(e_idx[:, i, :], e_top[:, i, :], kept[:, i, :]))
                go.settled()
                wait(dve, s["pos_done"], r - 1)
                for i in range(2):
                    ins = dve.tensor_tensor(
                        pick[:, i, :, :], iota_e[:, :].rearrange("p (a e) -> p a e", a=1).to_broadcast([P, K, E]),
                        e_idx[:, i, 0:K].rearrange("p (k a) -> p k a", a=1).to_broadcast([P, K, E]), ALU.is_equal)
                    if i == 0:
                        go.did(ins)
                    else:
                        ins.then_inc(s["pick_ready"], 1)

            def place(r, at, buf, go):
                wait(dve, s["pos_done"], r)
                wait(dve, s["wovt_done"], r - 1)
                go.did(dve.tensor_tensor(
                    pos[:, :, :], pos_ps.rearrange("p (i e) -> p i e", i=2),
                    counts[:, :].rearrange("p (a e) -> p a e", a=1).to_broadcast([P, 2, E]), ALU.add))
                for i in range(2):
                    tok = token[:, at + i:at + i + 1] if isinstance(at, int) else token[:, bass.ds(at + i, 1)]
                    go.did(dve.scalar_tensor_tensor(newest[:, :], sel_ps[:, i * E:(i + 1) * E], tok, newest[:, :],
                                                    ALU.mult, ALU.max))
                    go.settled()
                go.did(dve.tensor_tensor(counts[:, :], counts[:, :], cnt_ps, ALU.add))
                go.did(dve.scalar_tensor_tensor(over[:, :, :], pos[:, :, :], float(LAST), kept[:, :, :],
                                                ALU.is_ge, ALU.mult))
                for i in range(2):
                    go.did(dve.tensor_tensor(
                        pos_pick[:, i, :, :], pick[:, i, :, :],
                        pos[:, i, :].rearrange("p (a e) -> p a e", a=1).to_broadcast([P, K, E]), ALU.mult))
                go.settled()
                dve.tensor_tensor(w_over[:, :, :], over[:, :, :], sel_ps.rearrange("p (i e) -> p i e", i=2),
                                  ALU.mult).then_inc(s["wov_ready"], 1)
                go.did(dve.tensor_reduce(pos_k[:, :, :], pos_pick[:, :, :, :], AX, ALU.add))
                go.settled()
                go.did(dve.tensor_scalar(far_k[:, :, :], pos_k[:, :, :], float(LAST), float(FAR),
                                         ALU.is_ge, ALU.mult))
                go.did(dve.scalar_tensor_tensor(row_k[:, :, :], pos_k[:, :, :], float(E), e_idx[:, :, 0:K],
                                                ALU.mult, ALU.add))
                go.settled()
                wait(dve, s[f"meta_in{buf}"], 16 * K * (r - 1 - buf))
                m, sl = meta[:, buf, :, :], slot_idx[:, buf, :]
                go.did(dve.tensor_scalar(m[:, :, 1:2].rearrange("p (i k) a -> p i (k a)", i=2), e_top[:, :, 0:K],
                                         tanh_g[:, 1:2], None, ALU.mult))
                for i in range(2):
                    tok = token[:, at + i:at + i + 1] if isinstance(at, int) else token[:, bass.ds(at + i, 1)]
                    go.did(dve.tensor_copy(m[:, i * K:(i + 1) * K, 0:1].bitcast(I32),
                                           tok.rearrange("p (a b) -> p a b", a=1).to_broadcast([P, K, 1])))
                dve.tensor_tensor(sl.rearrange("p (i k) -> p i k", i=2), far_k[:, :, :], row_k[:, :, :], ALU.add)\
                    .then_inc(s["slots_ready"], 1)

            def shared_out(r, i, at):
                wait(dve, s["down_done"], 2 * (r - 1) + i + 1)
                tile = x_all[:, at + i, :] if isinstance(at, int) else \
                    x_all[:, bass.ds(at + i, 1), :].rearrange("p a f -> p (a f)")
                dve.scalar_tensor_tensor(tile, down_ps[i], tanh_g[:, 1:2], tile, ALU.mult, ALU.add)\
                    .then_inc(s["y_ready"], 1)

            def step(r, att, route, par=0):
                fixed = isinstance(r, int)
                go_a = Steps(dve, s["att_step"], r * K_ATT)
                go_r = Steps(dve, s["route_step"], (r - 1) * K_ROUTE)
                at = 2 * r if fixed else dve.snap(2 * r)
                at_r = 2 * r - 2 if fixed else dve.snap(2 * r - 2)
                if att:
                    smax(r, 0)
                    inverse_sum(r, 0)
                if route:
                    choose_groups(r, go_r)
                    choose_experts(r, go_r)
                    shared_act(r, 0, go_r)
                if att:
                    smax(r, 1)
                    inverse_sum(r, 1)
                if route:
                    shared_act(r, 1, go_r)
                if att:
                    residual(r, 0, at, go_a)
                if route:
                    place(r, at_r, (par + 1) % 2, go_r)
                    shared_act(r, 2, go_r)
                    shared_out(r, 0, at_r)
                if att:
                    residual(r, 1, at, go_a)
                if route:
                    shared_out(r, 1, at_r)
                if att:
                    norm2(r, at, go_a)
                assert not att or go_a.n == K_ATT, go_a.n
                assert not route or go_r.n == K_ROUTE, go_r.n

            step(0, True, False, 0)
            step(1, True, True, 1)
            with dve.Fori(1, PAIRS // 2) as h:
                step(2 * h, True, True, 0)
                step(2 * h + 1, True, True, 1)
            step(PAIRS, False, True, 0)

            go = Steps(dve, s["table_step"], 0)
            nt_ps, nr_ps = bank[0][0:E, 0:P], bank[0][0:C, P:P + E]
            dve.wait_ge(s["newest_t"], 1)
            go.did(dve.tensor_reduce(newest_col[:, :], nt_ps, AX, ALU.max))
            go.did(dve.memset(newest_sel[:, :], 0.0))
            go.settled()
            dve.tensor_copy(newest_sel[:, LAST:C], newest_col[:, :]).then_inc(s["newest_ready"], 1)
            dve.wait_ge(s["newest_mm"], 1)
            dve.wait_ge(s["table_in"], 16)
            names = table[:, :].bitcast(I32).rearrange("c (e w) -> c e w", w=W)[:, :, 0]
            weights = table[:, :].rearrange("c (e w) -> c e w", w=W)[:, :, 1]
            dve.tensor_tensor(gidx[:, :], names, nr_ps, ALU.add).then_inc(s["tables_ready"], 1)
            dve.tensor_scalar(sidx[:, :], names, last_dump[0:C, :], None, ALU.add).then_inc(s["tables_ready"], 1)
            dve.tensor_scalar(slot_w[:, :], weights, is_last[0:C, :], None, ALU.add)\
                .then_inc(s["tables_ready"], 1)

            at_ps = bank[3][0:MH, 0:2 * C]
            eg_ps = [bank[4][0:C, 0:2 * M], bank[5][0:C, 0:2 * M]]

            def take_act(e, b):
                wait(dve, s["at_done"], e + 1)
                wait(dve, s["o_done"], e - 1)
                dve.tensor_copy(act_tt[:, b % 2, :], at_ps).then_inc(s["at_out"], 1)

            def multiply(e, b):
                wait(dve, s["silu_ready"], e + 1)
                wait(dve, s["at_done"], e - 1)
                dve.tensor_tensor(act_sb[:, b % 2, :], silu_sb[:, b % 2, :], eg_ps[b % 2][:, M:2 * M], ALU.mult)\
                    .then_inc(s["a_ready"], 1)

            multiply(0, 0)
            for e in range(1, 9):
                multiply(e, e)
                take_act(e - 1, e - 1)
            with dve.Fori(1, E // 8 - 1) as q:
                for b in range(1, 9):
                    multiply(8 * q + b, b)
                    take_act(8 * q + b - 1, b - 1)
            for e in range(E - 7, E):
                multiply(e, e)
                take_act(e - 1, e - 1)
            take_act(E - 1, E - 1)

            for r in range(PAIRS):
                dve.wait_ge(s[f"acc0_back{r // (PAIRS // 2)}"], 32)
                a = x_all[:, 2 * r:2 * r + 2, :].rearrange("p n f -> p (n f)")
                dve.tensor_tensor(a, a, acc1[:, 2 * r:2 * r + 2, :].rearrange("p n f -> p (n f)"), ALU.add)\
                    .then_inc(s["sum_step"], 1)
                dve.wait_ge(s["sum_step"], r + 1)
                dve.wait_ge(s["ov_done"], 2 * r + 2)
                dve.tensor_tensor(a, a, bank[r % 4][:, :], ALU.add).then_inc(s["sum_ready"], 1)

        @block.gpsimd
        def _(pool):
            pool.memset(ident[:, :], 0.0).then_inc(s["ident_ready"], 1)
            pool.wait_ge(s["ident_ready"], 1)
            pool.affine_select(out=ident[:, :], in_=ident[:, :], compare_op=ALU.not_equal, fill=1.0, base=0,
                               pattern=[[-1, P]], channel_multiplier=1).then_inc(s["ident_ready"], 1)
            pool.memset(ones_b[:, :], 1.0).then_inc(s["consts_ready"], 1)
            pool.wait_ge(s["consts_ready"], 1)
            pool.wait_ge(s["ident_ready"], 2)
            pool.tensor_copy(ident_b[:, :], ident[:, :]).then_inc(s["consts_ready"], 1)
            pool.affine_select(out=before[:, :], in_=ones_b[:, :], compare_op=ALU.is_ge, fill=0.0, base=-1,
                               pattern=[[1, P]], channel_multiplier=-1).then_inc(s["consts_ready"], 1)
            pool.iota(row_id[:, :], pattern=[[0, 1]], base=0, channel_multiplier=1,
                      allow_small_or_imprecise_dtypes=True).then_inc(s["consts_ready"], 1)
            pool.iota(iota_g[:, :], pattern=[[1, NG]], base=0, channel_multiplier=0,
                      allow_small_or_imprecise_dtypes=True)
            pool.iota(iota_e[:, :], pattern=[[1, E]], base=0, channel_multiplier=0,
                      allow_small_or_imprecise_dtypes=True)
            pool.iota(token[:, :], pattern=[[P, N]], base=0, channel_multiplier=1,
                      allow_small_or_imprecise_dtypes=True).then_inc(s["consts_ready"], 1)

            last_row = pool.to_reg(C * E - 1)
            waited = s["waited_pool"]

            def add_bias(r, i):
                t = 2 * r + i
                at = t if isinstance(t, int) else pool.snap(t)
                wait_apart(pool, s["x1n_ready"], t + 1, waited)
                tile = x_all[:, bass.ds(at, 1), :].rearrange("p a f -> p (a f)")
                pool.tensor_tensor(tile, tile, vb_g[:, :].to_broadcast([P, L]), ALU.add).then_inc(s["x_plus"], 1)

            def scatter(r, buf):
                wait_apart(pool, s["slots_ready"], r, waited)
                for k in range(2 * K):
                    pool.indirect_dma_start(
                        table_dram, bass.IndirectOffsetOnAxis(ap=slot_idx[:, buf, k:k + 1], axis=0),
                        meta[:, buf, k, :], None, bounds_check=last_row, oob_is_err=False)\
                        .then_inc(s[f"meta_in{buf}"], 16)

            pool.wait_ge(s["dve_setup"], 4)
            for i in range(2):
                add_bias(0, i)
            for i in range(2):
                add_bias(1, i)
            pool.wait_ge(s["fills_in"], 80)
            scatter(1, 0)
            with pool.Fori(1, PAIRS // 2) as h:
                for par in range(2):
                    for i in range(2):
                        add_bias(2 * h + par, i)
                    scatter(2 * h + par, (par + 1) % 2)
            scatter(PAIRS, 1)

            def gather(e, b, col):
                wait_apart(pool, s["t_done"], e - ROWS + 1, waited)
                pool.indirect_dma_start(rows[:, b % ROWS, :], None, xn_dram,
                                        bass.IndirectOffsetOnAxis(ap=gidx_now[:, col:col + 1], axis=0))\
                    .then_inc(s[f"rows_in{b % ROWS}"], 16)

            def add_up(e, b):
                wait(pool, s["o_ready"], e + 1)
                wait_apart(pool, s[f"acc_in{b % 2}"], 8 * e - 8 * (b % 2), waited)
                pool.indirect_dma_start(acc_dram[b % 2],
                                        bass.IndirectOffsetOnAxis(ap=sidx_now[:, b:b + 1], axis=0),
                                        outs[:, b % OUTS, :], None, compute_op=ALU.add)\
                    .then_inc(s[f"acc_in{b % 2}"], 16)

            pool.wait_ge(s["tables_ready"], 2)
            pool.wait_ge(s["xn_saved"], 16 * PAIRS)
            pool.wait_ge(s["y_saved"], 16 * PAIRS)
            pool.tensor_copy(gidx_now[:, 8:8 + AHEAD], gidx[:, 0:AHEAD]).then_inc(s["idx_now"], 1)
            pool.wait_ge(s["idx_now"], 1)
            for e in range(AHEAD):
                gather(e, e, 8 + e)

            def eight(q, n):
                for half in range(2):
                    at = 8 * q + 4 * half
                    at_g = at + AHEAD
                    m = max(min(n - 4 * half, 4), 0)
                    if not isinstance(q, int):
                        at, at_g = pool.snap(at), pool.snap(at_g)
                    wait(pool, s["t_done"], 8 * q + AHEAD - 4 + 4 * half)
                    if m > 0:
                        pool.tensor_copy(gidx_now[:, 4 * half:4 * half + m], gidx[:, bass.ds(at_g, m)])\
                            .then_inc(s["idx_now"], 1)
                    pool.tensor_copy(sidx_now[:, 4 * half:4 * half + 4], sidx[:, bass.ds(at, 4)])\
                        .then_inc(s["idx_now"], 1)
                    wait_apart(pool, s["idx_now"], 4 * q + 2 * half + 2 + (m > 0), waited)
                    for b in range(4 * half, 4 * half + 4):
                        if b < n:
                            gather(8 * q + AHEAD + b, b + AHEAD, b)
                        add_up(8 * q + b, b)

            eight(0, 8)
            with pool.Fori(1, E // 8 - 1) as q:
                eight(q, 8)
            eight(E // 8 - 1, 8 - AHEAD)


def kernel(**inputs):
    import numpy as np
    import concourse.bacc as bacc
    from concourse.bass_utils import run_bass_kernel_spmd

    a = {k: np.asarray(v) for k, v in inputs.items()}

    qkv = np.concatenate([a[f"L0_xattn_{n}W"].T for n in "QKV"], axis=1)
    cols = np.stack([a["L0_xattn_Qb"], a["L0_xattn_Kb"], a["L0_xattn_Vb"],
                     np.repeat(a["g_xattn"], P), np.repeat(a["g_ffn"], P)], axis=1)
    gu = np.concatenate([a["L0_ffn_Wg"], a["L0_ffn_Wu"]], axis=1)
    gu = gu.reshape(GROUPS, GE, 2 * M, H2, P).transpose(0, 4, 1, 3, 2).reshape(GROUPS, P, GE * GU)
    wd = a["L0_ffn_Wd"].reshape(GROUPS, GE, L, 2, MH).transpose(0, 4, 1, 3, 2).reshape(GROUPS, MH, GE * DW)
    sgu = np.concatenate([a["L0_ffn_Sg"], a["L0_ffn_Su"]], axis=0).reshape(2 * MS, H2, P).transpose(2, 1, 0)
    sd = a["L0_ffn_Sd"].T
    arrays = {
        "x_in": a["x"].transpose(1, 0, 2),
        "ctx_in": a["ctx_2048"].transpose(1, 0, 2),
        "cols_in": cols,
        "qkv_in": qkv,
        "gate_in": a["L0_ffn_gate_weight"].reshape(E, H2, P).transpose(2, 1, 0),
        "sgu_in": sgu,
        "sd_in": sd[0:2 * P].reshape(2, P, L).transpose(1, 0, 2),
        "sd2_in": sd[2 * P:],
        "wgu_in": gu,
        "wd_in": wd,
    }
    arrays = {k: np.ascontiguousarray(v) for k, v in arrays.items()}
    nc = bacc.Bacc("TRN2", target_bir_lowering=False, num_devices=1)
    args = [nc.dram_tensor(k, v.shape, mybir.dt.from_np(v.dtype), kind="ExternalInput").ap()
            for k, v in arrays.items()]
    args.append(nc.dram_tensor("result", (P, N, L), F32, kind="ExternalOutput").ap())
    build(nc, *args)
    r = run_bass_kernel_spmd(nc, [arrays], core_ids=[0])
    return r.results[0]["result"].transpose(1, 0, 2)
```

```python
from contextlib import ExitStack

import concourse.bass as bass
from concourse import mybir

F32 = mybir.dt.float32
BF16 = mybir.dt.bfloat16
I32 = mybir.dt.int32
U32 = mybir.dt.uint32
ACT = mybir.ActivationFunctionType
ALU = mybir.AluOpType
AX = mybir.AxisListType.X

P = 128
N = 16
PAIRS = N // 2
L = 256
H2 = L // P
T = N * P
E = 64
K = 6
NG = 8
TG = 3
C = 96
LAST = C - 1
M = 176
MH = M // 2
MS = 352
MT = [(0, 128), (128, 128), (256, 96)]
EPS = 1e-5
W = 16
GONE = -2.0
TAKEN = -1.0
FAR = 262144
XW = L + E
GE = 2
GROUPS = E // GE
RING = 12
SAVED = 4
GU = H2 * 2 * M
DW = 2 * L
AHEAD = 6
ROWS = 8
OUTS = 8
MAGIC = 1597463007.0
K_ATT = 18
K_ROUTE = 28

def wait(eng, sem, value):
    if not isinstance(value, int) or value > 0:
        eng.wait_ge(sem, value)


def wait_apart(eng, sem, value, waited):
    wait(eng, sem, value)
    if not isinstance(value, int):
        eng.sem_inc(waited, 1)


class Steps:

    def __init__(self, eng, sem, base):
        self.eng, self.sem, self.base, self.n = eng, sem, base, 0

    def did(self, instruction):
        instruction.then_inc(self.sem, 1)
        self.n += 1

    def settled(self, waited=None):
        if waited is None:
            wait(self.eng, self.sem, self.base + self.n)
        else:
            wait_apart(self.eng, self.sem, self.base + self.n, waited)


def build(nc, x, ctx, cols, qkv, gate, sgu, sd, sd2, wgu, wd, out):
    xn_dram = nc.dram_tensor("xn_rows", (T + C, XW), F32).ap()
    acc_dram = [nc.dram_tensor(f"acc_rows{i}", (T + C, L), F32).ap() for i in range(2)]
    table_dram = nc.dram_tensor("slot_table", (C * E, W), F32).ap()
    last_dram = nc.dram_tensor("last_rows", (E, L), F32).ap()

    with ExitStack() as stack:
        def sb(name, shape, dt=F32):
            return stack.enter_context(nc.sbuf_tensor(name, shape, dt))

        def sem(name):
            return stack.enter_context(nc.semaphore(name))

        ident = sb("ident", [P, P])
        ident_b = sb("ident_b", [P, P], BF16)
        before = sb("before", [P, P], BF16)
        ones_b = sb("ones_b", [P, P], BF16)
        row_base = sb("row_base", [P, E])
        row_id = sb("row_id", [P, 1])
        is_last = sb("is_last", [P, 1])
        not_last = sb("not_last", [P, 1])
        last_dump = sb("last_dump", [P, 1])
        token = sb("token", [P, N])
        fill0 = sb("fill0", [P, 1])
        zeros = sb("zeros", [P, 1024])
        cols_sb = sb("cols_sb", [P, 5])
        tanh_g = sb("tanh_g", [P, 2])
        vb_g = sb("vb_g", [P, 1])
        qkv_sb = sb("qkv_sb", [P, 3 * P])
        gate_sb = sb("gate_sb", [P, H2, E])
        sgu_sb = sb("sgu_sb", [P, H2, 2 * MS])
        sd_sb = sb("sd_sb", [P, 3, L])
        x_all = sb("x_all", [P, N, L])
        ctx_sb = sb("ctx_sb", [P, 2, 2, L])
        stats = sb("stats", [P, N, 6])
        mv = sb("mv", [P, N, 2])
        var1 = sb("var1", [P, N])
        nhalf1 = sb("nhalf1", [P, N])
        newt1 = sb("newt1", [P, N])
        rstd1 = sb("rstd1", [P, N])
        shift1 = sb("shift1", [P, N])
        x1n = sb("x1n", [P, 2, L])
        qk_sb = sb("qk_sb", [P, 2, 2 * L])
        v_sb = sb("v_sb", [P, 2, 2 * P])
        neg_max = sb("neg_max", [P, 2, 2])
        p_sb = sb("p_sb", [P, 2, 2, L])
        p_sum = sb("p_sum", [P, 2, 2])
        p_inv = sb("p_inv", [P, 2, 2])
        pt_sb = sb("pt_sb", [P, 2, 2 * L])
        h_sb = sb("h_sb", [P, 2, 2, P])
        stats2 = sb("stats2", [P, 2, 6])
        mv2 = sb("mv2", [P, 2, 2])
        var2 = sb("var2", [P, 2])
        nhalf = sb("nhalf", [P, 2])
        guess = sb("guess", [P, 2])
        newt = sb("newt", [P, 2])
        xn2 = sb("xn2", [P, 2, L])
        xt_sb = sb("xt_sb", [P, H2, 2 * P])
        lg_max = sb("lg_max", [P, 2])
        es = sb("es", [P, 2, E])
        es_sum = sb("es_sum", [P, 2])
        es_inv = sb("es_inv", [P, 2])
        es_w = sb("es_w", [P, 2])
        g_max = sb("g_max", [P, 2, NG + 8 - TG])
        g_top = sb("g_top", [P, 2, 8])
        g_rep = sb("g_rep", [P, 2, NG + 8 - TG])
        kept = sb("kept", [P, 2, E + 8 - K])
        e_top = sb("e_top", [P, 2, 8])
        e_rep = sb("e_rep", [P, 2, E + 8 - K])
        sel = sb("sel", [P, 2, E], BF16)
        w_row = sb("w_row", [P, 2, E])
        counts = sb("counts", [P, E])
        pos = sb("pos", [P, 2, E])
        newest = sb("newest", [P, E])
        w_over = sb("w_over", [P, 2, E])
        code = sb("code", [P, 2, E])
        row_code = sb("row_code", [P, 2, E])
        row_top = sb("row_top", [P, 2, 8])
        slot_idx = sb("slot_idx", [P, 2, 2 * K], I32)
        meta = sb("meta", [P, 2, 2, W])
        w_over_t = sb("w_over_t", [E, T])
        tanh_sb = sb("tanh_sb", [P, 2, 2 * P])
        half_sb = sb("half_sb", [P, 2, 2 * P])
        act_t = sb("act_t", [P, 3, 2 * P])
        w_ring = sb("w_ring", [P, RING * GE * GU])
        d_ring = sb("d_ring", [MH, RING * GE * DW])
        table = sb("table", [C, E * W])
        table_fill = table
        gidx = sb("gidx", [C, E], I32)
        sidx = sb("sidx", [C, E], I32)
        slot_w = sb("slot_w", [C, 4])
        newest_col = sb("newest_col", [E, 1])
        newest_sel = sb("newest_sel", [E, C])
        gidx_now = sb("gidx_now", [C, 8 + AHEAD], I32)
        sidx_now = sb("sidx_now", [C, 8], I32)
        rows_a = x_all[0:C, OUTS:N, :].rearrange("p n f -> p (n f)")
        rows_b = qk_sb[0:C, :, :].rearrange("p a f -> p (a f)")
        rows = [rows_a[:, i * XW:(i + 1) * XW] for i in range(ROWS - 2)] + \
            [rows_b[:, i * XW:(i + 1) * XW] for i in range(2)]
        rows_t = p_sb[:, :, :, :].rearrange("p a h f -> p (a h f)")[:, 0:2 * H2 * C]\
            .rearrange("p (a f) -> p a f", a=2)
        silu_sb = pt_sb[0:C, :, 0:M]
        act_sb = sb("act_sb", [C, 2, M])
        act_tt = sb("act_tt", [MH, 2, 2 * C])
        outs = x_all[0:C, 0:OUTS, :]
        acc1 = w_ring[:, 0:N * L].rearrange("p (n f) -> p n f", n=N)
        last_sb = w_ring[0:E, N * L:(N + 1) * L]

        bank = [stack.enter_context(nc.psum_tensor(f"bank{i}", [P, 512], F32)) for i in range(8)]

        s = {name: sem(name) for name in """
            x_in0 x_in1 x_in2 x_in3 first_in shared_in ctx_in0 ctx_in1 fills_in
            ident_ready consts_ready zeros_ready fill_step vb_ready fill_ready tanh_ready setup_step norm1_ready
            x1n_ready x_plus qk_done v_done qk_out v_out s_done nmax_ready p_ready p_inv_ready
            pt_done pt_out h_done h_out ht_done x1_ready att_step xn2_ready xn_saved w_row_ready w_saved
            xt_done xt_out lg_done lgmax_ready es_ready route_step sel_ready pos_done wov_ready
            wovt_done wov_out slots_ready meta_in0 meta_in1 gu_done th_ready act_ready down_done y_ready y_saved
            w_in0 w_in1 table_in newest_t newest_ready newest_mm tables_ready table_step
            idx_now rows_in0 rows_in1 rows_in2 rows_in3
            rows_in4 rows_in5 rows_in6 rows_in7 t_done t_out eg_done silu_ready a_ready
            at_done at_out slot_w_ready o_done o_ready acc_in0 acc_in1 lasts_saved0 lasts_saved1 lasts_in
            acc0_back0 acc0_back1 ov_done sum_step sum_ready result_saved waited_dve waited_pe waited_act waited_pool""".split()}

        block = stack.enter_context(nc.Block())

        @block.sync
        def _(sp):
            for i in range(4):
                sp.dma_start(x_all[:, 4 * i:4 * i + 4, :], x[:, 4 * i:4 * i + 4, :]).then_inc(s[f"x_in{i}"], 16)
            sp.wait_ge(s["zeros_ready"], 1)
            zero4 = zeros[:, :].rearrange("p (a f) -> p a f", a=1).to_broadcast([P, 4, 1024])
            sp.dma_start(acc_dram[1][0:T, :].rearrange("(p a) f -> p (a f)", p=P)
                         .rearrange("p (a f) -> p a f", a=4), zero4).then_inc(s["fills_in"], 16)
            for d, words in ((xn_dram, XW), (acc_dram[0], L), (acc_dram[1], L)):
                sp.dma_start(d[T:T + C, :], zeros[0:C, 0:words]).then_inc(s["fills_in"], 16)
            sp.wait_ge(s["fill_ready"], 1)
            sp.dma_start(table_dram.rearrange("(c e) w -> c (e w)", c=C), table_fill[:, :])\
                .then_inc(s["fills_in"], 16)

            def load_weights(g, par):
                fixed = isinstance(g, int)
                at = g % RING if fixed else sp.snap(g % RING)
                at_gu = at * (GE * GU) if fixed else sp.snap(at * (GE * GU))
                at_d = at * (GE * DW) if fixed else sp.snap(at * (GE * DW))
                landed = (g // 2) * 32 if fixed else sp.snap((g // 2) * 32)
                freed = (g - RING + 1) * GE if fixed else sp.snap((g - RING + 1) * GE)
                wait(sp, s[f"w_in{par}"], landed)
                wait(sp, s["o_done"], freed)
                sp.dma_start(w_ring[:, bass.ds(at_gu, GE * GU)], wgu[g]).then_inc(s[f"w_in{par}"], 16)
                sp.dma_start(d_ring[:, bass.ds(at_d, GE * DW)], wd[g]).then_inc(s[f"w_in{par}"], 16)

            def saves(r):
                if 2 <= r:
                    lo = (r - 2) * (2 * P)
                    wait(sp, s["y_ready"], 2 * (r - 1))
                    sp.dma_start(acc_dram[0][bass.ds(lo, 2 * P), :].rearrange("(n p) f -> p n f", p=P),
                                 x_all[:, 2 * r - 4:2 * r - 2, :]).then_inc(s["y_saved"], 16)
                if 1 <= r <= PAIRS:
                    lo = (r - 1) * (2 * P)
                    wait(sp, s["w_row_ready"], r)
                    sp.dma_start(xn_dram[bass.ds(lo, 2 * P), L:XW].rearrange("(n p) f -> p n f", p=P),
                                 w_row[:, :, :]).then_inc(s["w_saved"], 16)
                if r < PAIRS:
                    lo = r * (2 * P)
                    wait(sp, s["xn2_ready"], r + 1)
                    sp.dma_start(xn_dram[bass.ds(lo, 2 * P), 0:L].rearrange("(n p) f -> p n f", p=P),
                                 xn2[:, :, :]).then_inc(s["xn_saved"], 16)

            for r in range(PAIRS + 2):
                for g in range(2 * r, min(2 * r + 2, RING)):
                    load_weights(g, g % 2)
                saves(r)

            sp.wait_ge(s["meta_in0"], 16 * K * N // 2)
            sp.wait_ge(s["meta_in1"], 16 * K * N // 2)
            sp.dma_start(table[:, :], table_dram.rearrange("(c e) w -> c (e w)", c=C)).then_inc(s["table_in"], 16)

            with sp.Fori(RING // 2, GROUPS // 2) as h:
                for par in range(2):
                    load_weights(2 * h + par, par)

            sp.wait_ge(s["acc_in0"], 16 * E // 2)
            sp.wait_ge(s["acc_in1"], 16 * E // 2)
            for par in range(2):
                sp.wait_ge(s[f"lasts_saved{par}"], 8 * E // SAVED)
            sp.dma_start(last_sb, last_dram).then_inc(s["lasts_in"], 16)

            for h in range(2):
                half = slice(h * T // 2, (h + 1) * T // 2)
                for acc, to in ((acc_dram[0], x_all), (acc_dram[1], acc1)):
                    sp.dma_start(to[:, h * N // 2:(h + 1) * N // 2, :],
                                 acc[half, :].rearrange("(n p) f -> p n f", p=P))\
                        .then_inc(s[f"acc0_back{h}"], 16)
            for r in range(PAIRS):
                sp.wait_ge(s["sum_ready"], r + 1)
                sp.dma_start(out[:, 2 * r:2 * r + 2, :], x_all[:, 2 * r:2 * r + 2, :]).then_inc(s["result_saved"], 16)
            sp.wait_ge(s["result_saved"], 16 * PAIRS)

        qk_ps = bank[0]
        v_ps = bank[1][:, 0:L]
        s_ps = bank[2]
        pt_ps = bank[3]
        down_ps = [bank[3][:, 0:L], bank[3][:, L:2 * L]]
        h_ps = bank[4][:, 0:L]
        ht_ps = bank[4][:, L:2 * L]
        wt_ps = bank[4][0:E, 0:2 * P]
        gu_ps = [bank[6], bank[5], bank[6]]
        xt_ps = bank[5]
        lg_ps = bank[7][:, 0:2 * E]
        pos_ps = bank[7][:, 2 * E:4 * E]
        cnt_ps = bank[7][:, 4 * E:5 * E]

        @block.tensor
        def _(pe):
            def mm(o, lhsT, rhs, start=True, stop=True):
                return pe.matmul(o, lhsT, rhs, start=start, stop=stop, skip_group_check=True)

            def project(r, i):
                t = 2 * r + i
                wait(pe, s["x1n_ready"], t + 1)
                wait(pe, s["qk_out"], t)
                mm(qk_ps[:, 0:L], qkv_sb[:, 0:P], x1n[:, i, :])
                c = ctx_sb[:, ctx_par[0], i, :]
                mm(qk_ps[:, L:2 * L], qkv_sb[:, P:2 * P], c).then_inc(s["qk_done"], 1)
                wait(pe, s["v_out"], t)
                for h in range(2):
                    last = mm(v_ps[:, h * P:(h + 1) * P], c[:, h * P:(h + 1) * P], qkv_sb[:, 2 * P:3 * P])
                last.then_inc(s["v_done"], 1)

            def scores(r, i):
                t = 2 * r + i
                wait(pe, s["qk_out"], t + 1)
                wait(pe, s["p_ready"], t)
                for h in range(2):
                    last = mm(s_ps[:, h * L:(h + 1) * L], qk_sb[:, i, h * P:(h + 1) * P], qk_sb[:, i, L:2 * L])
                last.then_inc(s["s_done"], 1)

            def turn_p(r, i):
                t = 2 * r + i
                wait(pe, s["p_ready"], t + 1)
                wait(pe, s["pt_out"], t)
                if i == 0:
                    wait(pe, s["y_ready"], 2 * (r - 1))
                for h in range(2):
                    for k in range(2):
                        last = pe.transpose(pt_ps[:, k * L + h * P:k * L + (h + 1) * P],
                                            p_sb[:, i, h, k * P:(k + 1) * P], ident[:, :])
                last.then_inc(s["pt_done"], 1)

            def attend(r, i):
                t = 2 * r + i
                wait(pe, s["pt_out"], t + 1)
                wait(pe, s["v_out"], t + 1)
                wait(pe, s["x1_ready"], t)
                if i == 0:
                    wait(pe, s["wov_out"], r - 1)
                for h in range(2):
                    for k in range(2):
                        last = mm(h_ps[:, h * P:(h + 1) * P], pt_sb[:, i, k * L + h * P:k * L + (h + 1) * P],
                                  v_sb[:, i, k * P:(k + 1) * P], start=k == 0, stop=k == 1)
                last.then_inc(s["h_done"], 1)

            def turn_h(r, i):
                t = 2 * r + i
                wait(pe, s["h_out"], t + 1)
                for h in range(2):
                    last = pe.transpose(ht_ps[:, h * P:(h + 1) * P], h_sb[:, i, h, :], ident[:, :])
                last.then_inc(s["ht_done"], 1)

            def turn_x(r):
                wait(pe, s["xn2_ready"], r)
                wait(pe, s["act_ready"], 3 * (r - 1) - 1)
                for i in range(2):
                    for h in range(H2):
                        last = pe.transpose(xt_ps[:, h * L + i * P:h * L + (i + 1) * P],
                                            xn2[:, i, h * P:(h + 1) * P], ident[:, :])
                last.then_inc(s["xt_done"], 1)

            def logits(r):
                wait(pe, s["xt_out"], r)
                wait(pe, s["wov_ready"], r - 1)
                for i in range(2):
                    for h in range(H2):
                        last = mm(lg_ps[:, i * E:(i + 1) * E], xt_sb[:, h, i * P:(i + 1) * P], gate_sb[:, h, :],
                                  start=h == 0, stop=h == H2 - 1)
                last.then_inc(s["lg_done"], 1)

            def shared_up(r, m):
                lo, n = MT[m]
                if m == 0:
                    wait(pe, s["xt_out"], r)
                    wait(pe, s["act_ready"], 3 * (r - 1))
                if m == 2:
                    wait(pe, s["act_ready"], 3 * r - 2)
                for b in range(2):
                    for h in range(H2):
                        last = mm(gu_ps[m][0:n, b * L:(b + 1) * L], sgu_sb[:, h, b * MS + lo:b * MS + lo + n],
                                  xt_sb[:, h, :], start=h == 0, stop=h == H2 - 1)
                last.then_inc(s["gu_done"], 1)

            def places(r):
                wait(pe, s["sel_ready"], r)
                mm(pos_ps[:, 0:E], before[:, :], sel[:, 0, :])
                mm(pos_ps[:, E:2 * E], before[:, :], sel[:, 1, :], stop=False)
                mm(pos_ps[:, E:2 * E], ones_b[:, :], sel[:, 0, :], start=False)
                mm(cnt_ps, ones_b[:, :], sel[:, 0, :], stop=False)
                mm(cnt_ps, ones_b[:, :], sel[:, 1, :], start=False).then_inc(s["pos_done"], 1)

            def shared_down(r, i):
                wait(pe, s["act_ready"], 3 * (r - 1))
                if i == 0:
                    wait(pe, s["pt_out"], 2 * r if not isinstance(r, int) else min(2 * r, N))
                else:
                    wait(pe, s["y_ready"], 2 * (r - 2) + 1)
                for m, (lo, n) in enumerate(MT):
                    last = mm(down_ps[i], act_t[0:n, m, i * P:(i + 1) * P], sd_sb[0:n, m, :],
                              start=m == 0, stop=m == 2)
                last.then_inc(s["down_done"], 1)

            def turn_w(r):
                wait(pe, s["x1_ready"], 2 * r if not isinstance(r, int) else min(2 * r, N))
                wait_apart(pe, s["wov_ready"], r - 1, waited)
                for i in range(2):
                    last = pe.transpose(wt_ps[:, i * P:(i + 1) * P], w_over[:, i, :], ident[:, :])
                last.then_inc(s["wovt_done"], 1)

            ctx_par = [0]
            waited = s["waited_pe"]
            pe.wait_ge(s["ident_ready"], 2)
            pe.wait_ge(s["first_in"], 32)

            def step(r, att, route, finish, par=0):
                ctx_par[0] = par
                if att:
                    wait(pe, s[f"ctx_in{par}"], r * 8 + 16 - 8 * par)
                    project(r, 0)
                if finish:
                    shared_down(r, 0)
                if att:
                    scores(r, 0)
                    project(r, 1)
                if finish:
                    turn_w(r)
                if route:
                    turn_x(r)
                if finish:
                    shared_down(r, 1)
                if att and route:
                    scores(r, 1)
                if route:
                    logits(r)
                if att:
                    turn_p(r, 0)
                    if not route:
                        scores(r, 1)
                if route:
                    shared_up(r, 0)
                if att:
                    attend(r, 0)
                    turn_p(r, 1)
                if route:
                    shared_up(r, 1)
                if att:
                    turn_h(r, 0)
                    attend(r, 1)
                if route:
                    places(r)
                    shared_up(r, 2)
                if att:
                    turn_h(r, 1)

            step(0, True, False, False, 0)
            pe.wait_ge(s["shared_in"], 16 * 4)
            pe.wait_ge(s["consts_ready"], 3)
            step(1, True, True, False, 1)
            with pe.Fori(1, PAIRS // 2) as h:
                step(2 * h, True, True, True, 0)
                step(2 * h + 1, True, True, True, 1)
            step(PAIRS, False, True, True)
            step(PAIRS + 1, False, False, True)

            nt_ps, nr_ps = bank[0][0:E, 0:P], bank[0][0:C, P:P + E]
            pe.wait_ge(s["route_step"], K_ROUTE * PAIRS)
            pe.wait_ge(s["qk_out"], N)
            pe.transpose(nt_ps, newest[:, :], ident[:, :]).then_inc(s["newest_t"], 1)
            pe.wait_ge(s["newest_ready"], 1)
            mm(nr_ps, newest_sel[:, :], ident[0:E, 0:E]).then_inc(s["newest_mm"], 1)

            t_ps = bank[2][:, 0:H2 * C]
            at_ps = bank[3][0:MH, 0:2 * C]
            eg_ps = [bank[4][0:C, 0:2 * M], bank[5][0:C, 0:2 * M]]
            o_ps = [bank[6][0:C, 0:L], bank[7][0:C, 0:L]]

            def turn_rows(e, b):
                wait(pe, s[f"rows_in{b % ROWS}"], (e - b % ROWS) * (16 // ROWS) + 16)
                wait(pe, s["t_out"], e)
                for h in range(H2):
                    last = pe.transpose(t_ps[:, h * C:(h + 1) * C], rows[b % ROWS][:, h * P:(h + 1) * P],
                                        ident[0:C, 0:C])
                last.then_inc(s["t_done"], 1)

            def at_ring(e, words):
                return e % (RING * GE) * words

            def up(e, b):
                if b % GE == 0:
                    wait(pe, s[f"w_in{b // GE % 2}"], e * (16 // GE) + 32 - 16 * (b // GE % 2))
                at = at_ring(e, GU)
                at = at if isinstance(at, int) else pe.snap(at)
                wait(pe, s["t_out"], e + 1)
                wait(pe, s["a_ready"], e - 1)
                for h in range(H2):
                    last = mm(eg_ps[b % 2], rows_t[:, b % 2, h * C:(h + 1) * C],
                              w_ring[:, bass.ds(at + h * 2 * M, 2 * M)], start=h == 0, stop=h == H2 - 1)
                last.then_inc(s["eg_done"], 1)

            def turn_act(e, b):
                wait(pe, s["a_ready"], e + 1)
                wait(pe, s["at_out"], e)
                for m in range(2):
                    last = pe.transpose(at_ps[:, m * C:(m + 1) * C], act_sb[:, b % 2, m * MH:(m + 1) * MH],
                                        ident[0:C, 0:C])
                last.then_inc(s["at_done"], 1)

            def down(e, b):
                at = at_ring(e, DW)
                at = at if isinstance(at, int) else pe.snap(at)
                wait(pe, s["at_out"], e + 1)
                wait(pe, s["o_ready"], e - 1)
                for m in range(2):
                    last = mm(o_ps[b % 2], act_tt[:, b % 2, m * C:(m + 1) * C],
                              d_ring[:, bass.ds(at + m * L, L)], start=m == 0, stop=m == 1)
                last.then_inc(s["o_done"], 1)

            def expert(e, b):
                known = isinstance(e, int)
                if not known or e < E - 1:
                    turn_rows(e + 1, b + 1)
                if not known or e < E:
                    up(e, b)
                if not known or e > 1:
                    down(e - 2, b - 2)
                if not known or 0 < e <= E:
                    turn_act(e - 1, b - 1)

            pe.wait_ge(s["p_ready"], N)
            pe.wait_ge(s["y_ready"], N)
            pe.wait_ge(s["wov_out"], PAIRS)
            pe.wait_ge(s["act_ready"], 3 * PAIRS)
            pe.wait_ge(s["wov_ready"], PAIRS)
            turn_rows(0, 0)
            for e in range(10):
                expert(e, e)
            with pe.Fori(1, E // 8 - 1) as q:
                for b in range(2, 10):
                    expert(8 * q + b, b)
            for e in range(E - 6, E + 2):
                expert(e, e)

            pe.wait_ge(s["lasts_in"], 16)
            for t in range(N):
                r, i = t // 2, t % 2
                wait(pe, s["sum_ready"], r - 3)
                mm(bank[r % 4][:, i * L:(i + 1) * L], w_over_t[:, t * P:(t + 1) * P], last_sb)\
                    .then_inc(s["ov_done"], 1)

        @block.scalar
        def _(act):
            act.dma_start(cols_sb[:, :], cols).then_inc(s["first_in"], 16)
            act.dma_start(qkv_sb[:, :], qkv).then_inc(s["first_in"], 16)
            act.dma_start(ctx_sb[:, 0, :, :], ctx[:, 0:2, :]).then_inc(s["ctx_in0"], 16)
            act.dma_start(ctx_sb[:, 1, :, :], ctx[:, 2:4, :]).then_inc(s["ctx_in1"], 16)
            act.dma_start(gate_sb[:, :, :], gate).then_inc(s["shared_in"], 16)
            act.dma_start(sgu_sb[:, :, :], sgu).then_inc(s["shared_in"], 16)
            act.dma_start(sd_sb[:, 0:2, :], sd).then_inc(s["shared_in"], 16)
            act.dma_start(sd_sb[0:MT[2][1], 2, :], sd2).then_inc(s["shared_in"], 16)
            act.wait_ge(s["first_in"], 32)
            act.activation(tanh_g[:, :], cols_sb[:, 3:5], ACT.Tanh).then_inc(s["tanh_ready"], 1)

            def norm1(r, i):
                t = 2 * r + i
                wait(act, s["norm1_ready"], 1 if isinstance(r, int) and r < 2 else 2)
                wait(act, s["qk_done"], t - 1)
                at = t if isinstance(t, int) else act.snap(t)
                act.activation(x1n[:, i, :], x_all[:, bass.ds(at, 1), :].rearrange("p a f -> p (a f)"),
                               ACT.Identity, scale=rstd1[:, bass.ds(at, 1)], bias=shift1[:, bass.ds(at, 1)])\
                    .then_inc(s["x1n_ready"], 1)

            def add_bias(r, i):
                t = 2 * r + i
                wait_apart(act, s["x1n_ready"], t + 1, s["waited_act"])
                at = t if isinstance(t, int) else act.snap(t)
                tile = x_all[:, bass.ds(at, 1), :].rearrange("p a f -> p (a f)")
                act.activation(tile, tile, ACT.Identity, bias=vb_g[:, :]).then_inc(s["x_plus"], 1)

            def take_qkv(r, i):
                t = 2 * r + i
                wait(act, s["qk_done"], t + 1)
                wait(act, s["s_done"], t - 1)
                act.activation(qk_sb[:, i, 0:L], qk_ps[:, 0:L], ACT.Identity, bias=cols_sb[:, 0:1])
                act.activation(qk_sb[:, i, L:2 * L], qk_ps[:, L:2 * L], ACT.Identity, bias=cols_sb[:, 1:2])\
                    .then_inc(s["qk_out"], 1)
                wait(act, s["v_done"], t + 1)
                wait(act, s["h_done"], t - 1)
                act.activation(v_sb[:, i, :], v_ps, ACT.Copy).then_inc(s["v_out"], 1)

            def exps(r, i):
                t = 2 * r + i
                wait(act, s["nmax_ready"], t + 1)
                wait(act, s["pt_done"], t - 1)
                wait(act, s["p_inv_ready"], t - 1)
                for h in range(2):
                    last = act.activation(p_sb[:, i, h, :], s_ps[:, h * L:(h + 1) * L], ACT.Exp,
                                          bias=neg_max[:, i, h:h + 1], accum_out=p_sum[:, i, h:h + 1])
                last.then_inc(s["p_ready"], 1)

            def take_pt(r, i):
                t = 2 * r + i
                wait(act, s["pt_done"], t + 1)
                wait(act, s["h_done"], t - 1)
                act.activation(pt_sb[:, i, :], pt_ps[:, :], ACT.Copy).then_inc(s["pt_out"], 1)

            def take_h(r, i):
                t = 2 * r + i
                wait(act, s["h_done"], t + 1)
                wait(act, s["p_inv_ready"], t + 1)
                wait(act, s["ht_done"], t - 1)
                for h in range(2):
                    last = act.activation(h_sb[:, i, h, :], h_ps[:, h * P:(h + 1) * P], ACT.Copy,
                                          scale=p_inv[:, i, h:h + 1])
                last.then_inc(s["h_out"], 1)

            def take_xt(r):
                wait(act, s["xt_done"], r)
                wait(act, s["gu_done"], 3 * (r - 1))
                act.activation(xt_sb[:, :, :].rearrange("p h t -> p (h t)"), xt_ps[:, :], ACT.Copy)\
                    .then_inc(s["xt_out"], 1)

            def exp_logits(r):
                wait(act, s["lgmax_ready"], r)
                for i in range(2):
                    last = act.activation(es[:, i, :], lg_ps[:, i * E:(i + 1) * E], ACT.Exp,
                                          bias=lg_max[:, i:i + 1], accum_out=es_sum[:, i:i + 1])
                last.then_inc(s["es_ready"], 1)

            def tanh_part(r, m):
                lo, n = MT[m]
                wait(act, s["gu_done"], 3 * (r - 1) + m + 1)
                b = m % 2
                wait(act, s["act_ready"], 3 * (r - 1) + m - 1 - (m == 0))
                act.activation(tanh_sb[0:n, b, :], gu_ps[m][0:n, 0:L], ACT.Tanh, scale=0.5)\
                    .then_inc(s["th_ready"], 1)

            def take_wov(r):
                wait(act, s["wovt_done"], r - 1)
                at = (r - 2) * (2 * P)
                at = at if isinstance(at, int) else act.snap(at)
                act.activation(w_over_t[:, bass.ds(at, 2 * P)], wt_ps, ACT.Copy).then_inc(s["wov_out"], 1)

            def step(r, att, route, finish, par=0, load=True):
                if att:
                    take_qkv(r, 0)
                    exps(r, 0)
                    take_qkv(r, 1)
                if finish:
                    take_wov(r)
                if route:
                    take_xt(r)
                if att and load:
                    at = 2 * r + 4
                    at = at if isinstance(at, int) else act.snap(at)
                    act.dma_start(ctx_sb[:, par, :, :], ctx[:, bass.ds(at, 2), :]).then_inc(s[f"ctx_in{par}"], 16)
                if route:
                    exp_logits(r)
                if att:
                    take_pt(r, 0)
                    exps(r, 1)
                if route:
                    tanh_part(r, 0)
                if att:
                    take_h(r, 0)
                    take_pt(r, 1)
                if route:
                    tanh_part(r, 1)
                if att:
                    take_h(r, 1)
                    if not isinstance(r, int) or r < PAIRS - 1:
                        norm1(r + 1, 0)
                        norm1(r + 1, 1)
                if route:
                    tanh_part(r, 2)
                if att and (not isinstance(r, int) or r < PAIRS - 1):
                    add_bias(r + 1, 0)
                    add_bias(r + 1, 1)

            norm1(0, 0)
            norm1(0, 1)
            act.wait_ge(s["vb_ready"], 1)
            add_bias(0, 0)
            add_bias(0, 1)
            step(0, True, False, False, 0)
            step(1, True, True, False, 1)
            with act.Fori(1, PAIRS // 2 - 1) as h:
                step(2 * h, True, True, True, 0)
                step(2 * h + 1, True, True, True, 1)
            step(PAIRS - 2, True, True, True, 0, load=False)
            step(PAIRS - 1, True, True, True, 1, load=False)
            step(PAIRS, False, True, True)
            step(PAIRS + 1, False, False, True)

            t_ps = bank[2][:, 0:H2 * C]
            eg_ps = [bank[4][0:C, 0:2 * M], bank[5][0:C, 0:2 * M]]
            o_ps = [bank[6][0:C, 0:L], bank[7][0:C, 0:L]]

            def take_rows(e, b):
                wait(act, s["t_done"], e + 1)
                wait(act, s["eg_done"], e - 1)
                act.activation(rows_t[:, b % 2, :], t_ps, ACT.Copy).then_inc(s["t_out"], 1)

            def silu(e, b):
                wait(act, s["eg_done"], e + 1)
                wait(act, s["a_ready"], e - 1)
                act.activation(silu_sb[:, b % 2, :], eg_ps[b % 2][:, 0:M], ACT.Silu).then_inc(s["silu_ready"], 1)

            def take_out(e, b):
                wait(act, s["o_done"], e + 1)
                wait(act, s["slot_w_ready"], e + 1)
                wait(act, s[f"acc_in{b % 2}"], 8 * (e - OUTS) + 16 - 8 * (b % 2))
                wait(act, s[f"lasts_saved{b // SAVED % 2}"], 2 * (e - b % SAVED) - 8 * (b // SAVED % 2))
                act.activation(outs[:, b % OUTS, :], o_ps[b % 2], ACT.Copy, scale=slot_w[:, b % 4:b % 4 + 1])\
                    .then_inc(s["o_ready"], 1)

            def save_lasts(e, b):
                at = e - (SAVED - 1)
                at = at if isinstance(at, int) else act.snap(at)
                wait(act, s["o_ready"], e + 1)
                lo = (b - (SAVED - 1)) % OUTS
                act.dma_start(last_dram[bass.ds(at, SAVED), :].rearrange("(a e) f -> a e f", a=1),
                              outs[LAST:C, lo:lo + SAVED, :]).then_inc(s[f"lasts_saved{b // SAVED % 2}"], 16)

            def expert(e, b):
                known = isinstance(e, int)
                if not known or e < E - 1:
                    take_rows(e + 1, b + 1)
                if not known or e < E:
                    silu(e, b)
                if not known or e > 1:
                    take_out(e - 2, b - 2)
                    if b % SAVED == 1:
                        save_lasts(e - 2, b - 2)

            act.wait_ge(s["y_saved"], 16 * PAIRS)
            take_rows(0, 0)
            for e in range(11):
                expert(e, e)
            with act.Fori(0, (E - 16) // 8) as q:
                for b in range(11, 19):
                    expert(8 * q + b, b)
            for e in range(E - 5, E + 2):
                expert(e, e)

        @block.vector
        def _(dve):
            setup = Steps(dve, s["setup_step"], 0)
            waited = s["waited_dve"]
            dve.memset(zeros[:, :], 0.0).then_inc(s["zeros_ready"], 1)

            def newton_start(go, var, guess, nhalf):
                go.did(dve.tensor_scalar(guess.bitcast(I32), var.bitcast(I32), 1, None, ALU.logical_shift_right))
                go.did(dve.tensor_scalar(nhalf, var, -0.5, None, ALU.mult))

            def newton_guess(go, guess):
                go.settled()
                go.did(dve.tensor_scalar(guess.bitcast(I32), guess.bitcast(I32), -1.0, MAGIC, ALU.mult, ALU.add))

            def newton_square(go, guess, newt):
                go.settled()
                go.did(dve.tensor_tensor(newt, guess, guess, ALU.mult))

            def newton_scale(go, newt, nhalf):
                go.settled()
                go.did(dve.tensor_tensor(newt, newt, nhalf, ALU.mult))

            def newton_update(go, guess, newt):
                go.settled()
                go.did(dve.scalar_tensor_tensor(guess, newt, 1.5, guess, ALU.add, ALU.mult))

            def stats1(c):
                dve.wait_ge(s[f"x_in{c}"], 16)
                for t in range(4 * c, 4 * c + 4):
                    setup.did(dve.bn_stats(stats[:, t, :], x_all[:, t, :]))

            def scales1(lo, hi):
                setup.settled()
                for t in range(lo, hi):
                    setup.did(dve.bn_aggr(mv[:, t, :], stats[:, t, :]))
                setup.settled()
                var, guess, nhalf, newt = (a[:, lo:hi] for a in (var1, rstd1, nhalf1, newt1))
                setup.did(dve.tensor_scalar(var, mv[:, lo:hi, 1], EPS, None, ALU.add))
                setup.settled()
                newton_start(setup, var, guess, nhalf)
                newton_guess(setup, guess)
                for _ in range(3):
                    newton_square(setup, guess, newt)
                    newton_scale(setup, newt, nhalf)
                    newton_update(setup, guess, newt)
                setup.settled()
                dve.scalar_tensor_tensor(shift1[:, lo:hi], mv[:, lo:hi, 0], -1.0, guess, ALU.mult, ALU.mult)\
                    .then_inc(s["norm1_ready"], 1)

            stats1(0)
            scales1(0, 4)
            dve.wait_ge(s["tanh_ready"], 1)
            dve.tensor_tensor(vb_g[:, :], cols_sb[:, 2:3], tanh_g[:, 0:1], ALU.mult).then_inc(s["vb_ready"], 1)

            def smax(r, i):
                t = 2 * r + i
                wait(dve, s["s_done"], t + 1)
                wait(dve, s["p_ready"], t - 1)
                dve.tensor_reduce(neg_max[:, i, :], s_ps[:, :].rearrange("p (h k) -> p h k", h=2), AX, ALU.max,
                                  negate=True).then_inc(s["nmax_ready"], 1)

            def inverse_sum(r, i):
                t = 2 * r + i
                wait(dve, s["p_ready"], t + 1)
                wait(dve, s["h_out"], t - 1)
                dve.reciprocal(p_inv[:, i, :], p_sum[:, i, :]).then_inc(s["p_inv_ready"], 1)

            def residual(r, i, at, go):
                t = 2 * r + i
                wait(dve, s["ht_done"], t + 1)
                wait(dve, s["x_plus"], t + 1)
                tile = x_all[:, at + i, :] if isinstance(at, int) else \
                    x_all[:, bass.ds(at + i, 1), :].rearrange("p a f -> p (a f)")
                dve.scalar_tensor_tensor(tile, ht_ps, tanh_g[:, 0:1], tile, ALU.mult, ALU.add)\
                    .then_inc(s["x1_ready"], 1)
                wait_apart(dve, s["x1_ready"], t + 1, waited)
                go.did(dve.bn_stats(stats2[:, i, :], tile))
                go.settled(waited)
                go.did(dve.bn_aggr(mv2[:, i, :], stats2[:, i, :]))

            def norm2(r, at, go):
                go.settled()
                wait(dve, s["xt_done"], r)
                wait(dve, s["xn_saved"], 16 * r)
                for i in range(2):
                    tile = x_all[:, at + i, :] if isinstance(at, int) else \
                        x_all[:, bass.ds(at + i, 1), :].rearrange("p a f -> p (a f)")
                    ins = dve.tensor_scalar(xn2[:, i, :], tile, mv2[:, i, 0:1], guess[:, i:i + 1],
                                            ALU.subtract, ALU.mult)
                    if i == 0:
                        go.did(ins)
                    else:
                        ins.then_inc(s["xn2_ready"], 1)

            def shared_act(r, m, go, half):
                lo, n = MT[m]
                g, u = gu_ps[m][0:n, 0:L], gu_ps[m][0:n, L:2 * L]
                if half == 0:
                    wait(dve, s["th_ready"], 3 * (r - 1) + m + 1)
                    go.did(dve.scalar_tensor_tensor(half_sb[0:n, m % 2, :], tanh_sb[0:n, m % 2, :], 1.0, g,
                                                    ALU.add, ALU.mult))
                else:
                    go.settled()
                    if m == 0:
                        wait(dve, s["down_done"], 2 * (r - 1))
                    dve.scalar_tensor_tensor(act_t[0:n, m, :], half_sb[0:n, m % 2, :], 0.5, u, ALU.mult, ALU.mult)\
                        .then_inc(s["act_ready"], 1)

            def max_logit(r):
                wait(dve, s["lg_done"], r)
                wait(dve, s["es_ready"], r - 1)
                dve.tensor_reduce(lg_max[:, :], lg_ps.rearrange("p (i e) -> p i e", i=2), AX, ALU.max, negate=True)\
                    .then_inc(s["lgmax_ready"], 1)

            def choose_groups(r, go):
                wait(dve, s["es_ready"], r)
                go.did(dve.tensor_reduce(g_max[:, :, 0:NG], es[:, :, :].rearrange("p i (g e) -> p i g e", g=NG),
                                         AX, ALU.max))
                go.did(dve.reciprocal(es_inv[:, :], es_sum[:, :]))
                go.settled(waited)
                for i in range(2):
                    go.did(dve.max(g_top[:, i, :], g_max[:, i, 0:NG]))
                go.settled()
                go.did(dve.memset(g_top[:, :, TG:8], GONE))
                go.did(dve.tensor_tensor(es_w[:, :], es_inv[:, :], tanh_g[:, 1:2].to_broadcast([P, 2]), ALU.mult))
                go.settled(waited)
                for i in range(2):
                    go.did(dve.match_replace(g_rep[:, i, :], g_top[:, i, :], g_max[:, i, :], TAKEN))
                go.settled()
                for i in range(2):
                    go.did(dve.scalar_tensor_tensor(
                        kept[:, i, 0:E].rearrange("p (g e) -> p g e", g=NG),
                        g_rep[:, i, 0:NG].rearrange("p (g a) -> p g a", a=1).to_broadcast([P, NG, E // NG]), 0.0,
                        es[:, i, :].rearrange("p (g e) -> p g e", g=NG), ALU.is_lt, ALU.mult))

            def choose_experts(r, go):
                go.settled(waited)
                for i in range(2):
                    go.did(dve.max(e_top[:, i, :], kept[:, i, 0:E]))
                go.settled()
                go.did(dve.memset(e_top[:, :, K:8], GONE))
                go.settled(waited)
                for i in range(2):
                    go.did(dve.match_replace(e_rep[:, i, :], e_top[:, i, :], kept[:, i, :], TAKEN))
                go.settled()
                wait(dve, s["pos_done"], r - 1)
                dve.tensor_scalar(sel[:, :, :], e_rep[:, :, 0:E], 0.0, None, ALU.is_lt).then_inc(s["sel_ready"], 1)
                wait(dve, s["sel_ready"], r)
                wait(dve, s["w_saved"], 16 * (r - 1))
                for i in range(2):
                    ins = dve.scalar_tensor_tensor(w_row[:, i, :], kept[:, i, 0:E], es_w[:, i:i + 1], sel[:, i, :],
                                                   ALU.mult, ALU.mult)
                    if i == 0:
                        go.did(ins)
                    else:
                        ins.then_inc(s["w_row_ready"], 1)

            def place(r, at, go):
                wait(dve, s["pos_done"], r)
                wait(dve, s["wovt_done"], r - 1)
                go.did(dve.tensor_tensor(
                    pos[:, :, :], pos_ps.rearrange("p (i e) -> p i e", i=2),
                    counts[:, :].rearrange("p (a e) -> p a e", a=1).to_broadcast([P, 2, E]), ALU.add))
                for i in range(2):
                    tok = token[:, at + i:at + i + 1] if isinstance(at, int) else token[:, bass.ds(at + i, 1)]
                    go.did(dve.scalar_tensor_tensor(newest[:, :], sel[:, i, :], tok, newest[:, :],
                                                    ALU.mult, ALU.max))
                    go.settled()
                go.did(dve.tensor_tensor(counts[:, :], counts[:, :], cnt_ps, ALU.add))
                wait(dve, s["w_row_ready"], r)
                dve.scalar_tensor_tensor(w_over[:, :, :], pos[:, :, :], float(LAST), w_row[:, :, :],
                                         ALU.is_ge, ALU.mult).then_inc(s["wov_ready"], 1)

            def row_codes(go, part):
                if part == 0:
                    go.did(dve.scalar_tensor_tensor(
                        code[:, :, :], pos[:, :, :], -float(E),
                        row_base[:, :].rearrange("p (a e) -> p a e", a=1).to_broadcast([P, 2, E]),
                        ALU.mult, ALU.add))
                elif part == 1:
                    go.settled()
                    go.did(dve.tensor_tensor(row_code[:, :, :], code[:, :, :], sel[:, :, :], ALU.mult))
                else:
                    go.settled(waited)
                    for i in range(2):
                        go.did(dve.max(row_top[:, i, :], row_code[:, i, :]))

            def slots(r, at, buf, go):
                wait_apart(dve, s[f"meta_in{buf}"], 16 * K * (r - 1 - buf), waited)
                toks = token[:, at:at + 2] if isinstance(at, int) else token[:, bass.ds(at, 2)]
                go.did(dve.tensor_copy(meta[:, buf, :, 0].bitcast(I32), toks))
                go.settled()
                dve.tensor_scalar(slot_idx[:, buf, :].rearrange("p (i k) -> p i k", i=2), row_top[:, :, 0:K],
                                  -1.0, float(FAR), ALU.mult, ALU.add).then_inc(s["slots_ready"], 1)

            def shared_out(r, i, at):
                wait(dve, s["down_done"], 2 * (r - 2) + i + 1)
                tile = x_all[:, at + i, :] if isinstance(at, int) else \
                    x_all[:, bass.ds(at + i, 1), :].rearrange("p a f -> p (a f)")
                dve.scalar_tensor_tensor(tile, down_ps[i], tanh_g[:, 1:2], tile, ALU.mult, ALU.add)\
                    .then_inc(s["y_ready"], 1)

            def step(r, att, route, finish, par=0):
                fixed = isinstance(r, int)
                go_a = Steps(dve, s["att_step"], r * K_ATT)
                go_r = Steps(dve, s["route_step"], (r - 1) * K_ROUTE)
                at = 2 * r if fixed else dve.snap(2 * r)
                at_r = 2 * r - 2 if fixed else dve.snap(2 * r - 2)
                at_f = 2 * r - 4 if fixed else dve.snap(2 * r - 4)
                first = fixed and r == 0
                if finish:
                    shared_out(r, 0, at_f)
                if att:
                    smax(r, 0)
                    inverse_sum(r, 0)
                if first:
                    stats1(1)
                if finish:
                    shared_out(r, 1, at_f)
                if att:
                    smax(r, 1)
                if first:
                    stats1(2)
                if route:
                    max_logit(r)
                    choose_groups(r, go_r)
                    choose_experts(r, go_r)
                if att:
                    inverse_sum(r, 1)
                if route:
                    shared_act(r, 0, go_r, 0)
                    shared_act(r, 0, go_r, 1)
                if att:
                    residual(r, 0, at, go_a)
                if first:
                    stats1(3)
                if route:
                    shared_act(r, 1, go_r, 0)
                    shared_act(r, 1, go_r, 1)
                    place(r, at_r, go_r)
                if att:
                    residual(r, 1, at, go_a)
                if route:
                    shared_act(r, 2, go_r, 0)
                if att:
                    go_a.settled()
                    go_a.did(dve.tensor_scalar(var2[:, :], mv2[:, :, 1], EPS, None, ALU.add))
                if route:
                    shared_act(r, 2, go_r, 1)
                if att:
                    go_a.settled()
                    newton_start(go_a, var2[:, :], guess[:, :], nhalf[:, :])
                for n in range(3):
                    if route:
                        row_codes(go_r, n)
                    if att:
                        if n == 0:
                            newton_guess(go_a, guess[:, :])
                        newton_square(go_a, guess[:, :], newt[:, :])
                        newton_scale(go_a, newt[:, :], nhalf[:, :])
                        newton_update(go_a, guess[:, :], newt[:, :])
                if route:
                    slots(r, at_r, (par + 1) % 2, go_r)
                if att:
                    norm2(r, at, go_a)
                if first:
                    scales1(4, N)
                assert not att or go_a.n == K_ATT, go_a.n
                assert not route or go_r.n == K_ROUTE, go_r.n

            step(0, True, False, False, 0)
            dve.wait_ge(s["consts_ready"], 9)
            step(1, True, True, False, 1)
            with dve.Fori(1, PAIRS // 2) as h:
                step(2 * h, True, True, True, 0)
                step(2 * h + 1, True, True, True, 1)
            step(PAIRS, False, True, True, 0)
            step(PAIRS + 1, False, False, True)

            go = Steps(dve, s["table_step"], 0)
            nt_ps, nr_ps = bank[0][0:E, 0:P], bank[0][0:C, P:P + E]
            dve.wait_ge(s["newest_t"], 1)
            go.did(dve.tensor_reduce(newest_col[:, :], nt_ps, AX, ALU.max))
            go.did(dve.memset(newest_sel[:, :], 0.0))
            go.settled()
            dve.tensor_copy(newest_sel[:, LAST:C], newest_col[:, :]).then_inc(s["newest_ready"], 1)
            dve.wait_ge(s["newest_mm"], 1)
            dve.wait_ge(s["table_in"], 16)
            names = table[:, :].bitcast(I32).rearrange("c (e w) -> c e w", w=W)[:, :, 0]
            dve.tensor_tensor(gidx[:, :], names, nr_ps, ALU.add).then_inc(s["tables_ready"], 1)
            dve.tensor_scalar(sidx[:, :], names, last_dump[0:C, :], None, ALU.add).then_inc(s["tables_ready"], 1)
            at_ps = bank[3][0:MH, 0:2 * C]
            eg_ps = [bank[4][0:C, 0:2 * M], bank[5][0:C, 0:2 * M]]

            def take_act(e, b):
                wait(dve, s["at_done"], e + 1)
                wait(dve, s["o_done"], e - 1)
                dve.tensor_copy(act_tt[:, b % 2, :], at_ps).then_inc(s["at_out"], 1)

            def multiply(e, b):
                wait(dve, s["silu_ready"], e + 1)
                wait(dve, s["at_done"], e - 1)
                dve.tensor_tensor(act_sb[:, b % 2, :], silu_sb[:, b % 2, :], eg_ps[b % 2][:, M:2 * M], ALU.mult)\
                    .then_inc(s["a_ready"], 1)

            def slot_weight(e, b):
                at = L + e if isinstance(e, int) else dve.snap(L + e)
                wait(dve, s[f"rows_in{b % ROWS}"], (e - b % ROWS) * (16 // ROWS) + 16)
                wait(dve, s["o_ready"], e - 3)
                dve.tensor_scalar(slot_w[:, b % 4:b % 4 + 1], rows[b % ROWS][:, bass.ds(at, 1)],
                                  not_last[0:C, :], is_last[0:C, :], ALU.mult, ALU.add)\
                    .then_inc(s["slot_w_ready"], 1)

            slot_weight(0, 0)
            multiply(0, 0)
            for e in range(1, 9):
                slot_weight(e, e)
                multiply(e, e)
                take_act(e - 1, e - 1)
            with dve.Fori(1, E // 8 - 1) as q:
                for b in range(1, 9):
                    slot_weight(8 * q + b, b)
                    multiply(8 * q + b, b)
                    take_act(8 * q + b - 1, b - 1)
            for e in range(E - 7, E):
                slot_weight(e, e)
                multiply(e, e)
                take_act(e - 1, e - 1)
            take_act(E - 1, E - 1)

            for r in range(PAIRS):
                dve.wait_ge(s[f"acc0_back{r // (PAIRS // 2)}"], 32)
                a = x_all[:, 2 * r:2 * r + 2, :].rearrange("p n f -> p (n f)")
                dve.tensor_tensor(a, a, acc1[:, 2 * r:2 * r + 2, :].rearrange("p n f -> p (n f)"), ALU.add)\
                    .then_inc(s["sum_step"], 1)
                dve.wait_ge(s["sum_step"], r + 1)
                dve.wait_ge(s["ov_done"], 2 * r + 2)
                dve.tensor_tensor(a, a, bank[r % 4][:, :], ALU.add).then_inc(s["sum_ready"], 1)

        @block.gpsimd
        def _(pool):
            pool.memset(ident[:, :], 0.0).then_inc(s["ident_ready"], 1)
            pool.wait_ge(s["ident_ready"], 1)
            pool.affine_select(out=ident[:, :], in_=ident[:, :], compare_op=ALU.not_equal, fill=1.0, base=0,
                               pattern=[[-1, P]], channel_multiplier=1).then_inc(s["ident_ready"], 1)
            pool.memset(ones_b[:, :], 1.0).then_inc(s["consts_ready"], 1)
            pool.wait_ge(s["consts_ready"], 1)
            pool.wait_ge(s["ident_ready"], 2)
            pool.tensor_copy(ident_b[:, :], ident[:, :]).then_inc(s["consts_ready"], 1)
            pool.affine_select(out=before[:, :], in_=ones_b[:, :], compare_op=ALU.is_ge, fill=0.0, base=-1,
                               pattern=[[1, P]], channel_multiplier=-1).then_inc(s["consts_ready"], 1)
            pool.iota(row_id[:, :], pattern=[[0, 1]], base=0, channel_multiplier=1,
                      allow_small_or_imprecise_dtypes=True)
            pool.iota(row_base[:, :], pattern=[[-1, E]], base=FAR, channel_multiplier=0,
                      allow_small_or_imprecise_dtypes=True)
            pool.iota(token[:, :], pattern=[[P, N]], base=0, channel_multiplier=1,
                      allow_small_or_imprecise_dtypes=True).then_inc(s["consts_ready"], 1)
            for a, value in ((counts, 0.0), (newest, 0.0), (g_max, GONE), (kept, GONE), (meta, 0.0)):
                pool.memset(a[:], value).then_inc(s["consts_ready"], 1)
            pool.memset(table_fill[:, :], 0.0).then_inc(s["fill_step"], 1)
            pool.wait_ge(s["consts_ready"], 4)
            pool.tensor_scalar(is_last[:, :], row_id[:, :], float(LAST), None, ALU.is_equal).then_inc(s["fill_step"], 1)
            pool.wait_ge(s["fill_step"], 2)
            pool.tensor_scalar(not_last[:, :], is_last[:, :], -1.0, 1.0, ALU.mult, ALU.add)
            pool.tensor_scalar(last_dump[:, :], is_last[:, :], float(T + LAST), None, ALU.mult)
            pool.tensor_scalar(fill0[:, :], row_id[:, :], float(T), None, ALU.add).then_inc(s["fill_step"], 1)
            pool.wait_ge(s["fill_step"], 3)
            pool.tensor_tensor(fill0[:, :], fill0[:, :], last_dump[:, :], ALU.subtract).then_inc(s["fill_step"], 1)
            pool.wait_ge(s["fill_step"], 4)
            pool.tensor_copy(table_fill[:, :].bitcast(I32).rearrange("c (e w) -> c e w", w=W)[:, :, 0:1],
                             fill0[0:C, :].rearrange("c (a b) -> c a b", a=1).to_broadcast([C, E, 1]))\
                .then_inc(s["fill_ready"], 1)

            last_row = pool.to_reg(LAST * E - 1)
            waited = s["waited_pool"]

            def scatter(r, buf):
                wait_apart(pool, s["slots_ready"], r, waited)
                for k in range(2 * K):
                    pool.indirect_dma_start(
                        table_dram, bass.IndirectOffsetOnAxis(ap=slot_idx[:, buf, k:k + 1], axis=0),
                        meta[:, buf, k // K, :], None, bounds_check=last_row, oob_is_err=False)\
                        .then_inc(s[f"meta_in{buf}"], 16)

            pool.wait_ge(s["fills_in"], 80)
            scatter(1, 0)
            with pool.Fori(1, PAIRS // 2) as h:
                for par in range(2):
                    scatter(2 * h + par, (par + 1) % 2)
            scatter(PAIRS, 1)

            def gather(e, b, col):
                pool.indirect_dma_start(rows[b % ROWS], None, xn_dram,
                                        bass.IndirectOffsetOnAxis(ap=gidx_now[:, col:col + 1], axis=0))\
                    .then_inc(s[f"rows_in{b % ROWS}"], 16)

            def add_up(e, b):
                wait(pool, s["o_ready"], e + 1)
                wait_apart(pool, s[f"acc_in{b % 2}"], 8 * e - 8 * (b % 2), waited)
                pool.indirect_dma_start(acc_dram[b % 2],
                                        bass.IndirectOffsetOnAxis(ap=sidx_now[:, b:b + 1], axis=0),
                                        outs[:, b % OUTS, :], None, compute_op=ALU.add)\
                    .then_inc(s[f"acc_in{b % 2}"], 16)

            pool.wait_ge(s["tables_ready"], 2)
            pool.wait_ge(s["xn_saved"], 16 * PAIRS)
            pool.wait_ge(s["w_saved"], 16 * PAIRS)
            pool.wait_ge(s["y_saved"], 16 * PAIRS)
            pool.tensor_copy(gidx_now[:, 8:8 + AHEAD], gidx[:, 0:AHEAD]).then_inc(s["idx_now"], 1)
            pool.wait_ge(s["idx_now"], 1)
            for e in range(AHEAD):
                gather(e, e, 8 + e)

            def eight(q, n):
                for half in range(2):
                    at = 8 * q + 4 * half
                    at_g = at + AHEAD
                    m = max(min(n - 4 * half, 4), 0)
                    if not isinstance(q, int):
                        at, at_g = pool.snap(at), pool.snap(at_g)
                    wait(pool, s["t_done"], 8 * q + AHEAD - 4 + 4 * half)
                    if m > 0:
                        pool.tensor_copy(gidx_now[:, 4 * half:4 * half + m], gidx[:, bass.ds(at_g, m)])\
                            .then_inc(s["idx_now"], 1)
                    pool.tensor_copy(sidx_now[:, 4 * half:4 * half + 4], sidx[:, bass.ds(at, 4)])\
                        .then_inc(s["idx_now"], 1)
                    wait_apart(pool, s["idx_now"], 4 * q + 2 * half + 2 + (m > 0), waited)
                    for b in range(4 * half, 4 * half + 4):
                        if b < n:
                            gather(8 * q + AHEAD + b, b + AHEAD, b)
                        add_up(8 * q + b, b)

            eight(0, 8)
            with pool.Fori(1, E // 8 - 1) as q:
                eight(q, 8)
            eight(E // 8 - 1, 8 - AHEAD)


def kernel(**inputs):
    import numpy as np
    import concourse.bacc as bacc
    from concourse.bass_utils import run_bass_kernel_spmd

    a = {k: np.asarray(v) for k, v in inputs.items()}

    qkv = np.concatenate([a[f"L0_xattn_{n}W"].T for n in "QKV"], axis=1)
    cols = np.stack([a["L0_xattn_Qb"], a["L0_xattn_Kb"], a["L0_xattn_Vb"],
                     np.repeat(a["g_xattn"], P), np.repeat(a["g_ffn"], P)], axis=1)
    gu = np.concatenate([a["L0_ffn_Wg"], a["L0_ffn_Wu"]], axis=1)
    gu = gu.reshape(GROUPS, GE, 2 * M, H2, P).transpose(0, 4, 1, 3, 2).reshape(GROUPS, P, GE * GU)
    wd = a["L0_ffn_Wd"].reshape(GROUPS, GE, L, 2, MH).transpose(0, 4, 1, 3, 2).reshape(GROUPS, MH, GE * DW)
    sgu = np.concatenate([a["L0_ffn_Sg"], a["L0_ffn_Su"]], axis=0).reshape(2 * MS, H2, P).transpose(2, 1, 0)
    sd = a["L0_ffn_Sd"].T
    arrays = {
        "x_in": a["x"].transpose(1, 0, 2),
        "ctx_in": a["ctx_2048"].transpose(1, 0, 2),
        "cols_in": cols,
        "qkv_in": qkv,
        "gate_in": a["L0_ffn_gate_weight"].reshape(E, H2, P).transpose(2, 1, 0),
        "sgu_in": sgu,
        "sd_in": sd[0:2 * P].reshape(2, P, L).transpose(1, 0, 2),
        "sd2_in": sd[2 * P:],
        "wgu_in": gu,
        "wd_in": wd,
    }
    arrays = {k: np.ascontiguousarray(v) for k, v in arrays.items()}
    nc = bacc.Bacc("TRN2", target_bir_lowering=False, num_devices=1)
    args = [nc.dram_tensor(k, v.shape, mybir.dt.from_np(v.dtype), kind="ExternalInput").ap()
            for k, v in arrays.items()]
    args.append(nc.dram_tensor("result", (P, N, L), F32, kind="ExternalOutput").ap())
    build(nc, *args)
    r = run_bass_kernel_spmd(nc, [arrays], core_ids=[0])
    return r.results[0]["result"].transpose(1, 0, 2)
```

```python
from contextlib import ExitStack

import concourse.bass as bass
from concourse import mybir

F32 = mybir.dt.float32
BF16 = mybir.dt.bfloat16
I32 = mybir.dt.int32
U32 = mybir.dt.uint32
ACT = mybir.ActivationFunctionType
ALU = mybir.AluOpType
AX = mybir.AxisListType.X

P = 128
N = 16
PAIRS = N // 2
L = 256
H2 = L // P
T = N * P
E = 64
K = 6
NG = 8
TG = 3
C = 96
LAST = C - 1
M = 176
MH = M // 2
MS = 352
MT = [(0, 128), (128, 128), (256, 96)]
EPS = 1e-5
W = 16
GONE = -2.0
TAKEN = -1.0
FAR = 262144
XW = L + E
GE = 2
GROUPS = E // GE
RING = 12
SAVED = 4
GU = H2 * 2 * M
DW = 2 * L
AHEAD = 6
ROWS = 8
OUTS = 8
MAGIC = 1597463007.0
K_ATT = 18
K_ROUTE = 25
K_CHOOSE = 16
QUARTERS = 4
X_LOADS = ((0, 2), (2, 4), (4, 10), (10, 16))
NQ = PAIRS // 2

def wait(eng, sem, value):
    if not isinstance(value, int) or value > 0:
        eng.wait_ge(sem, value)


def wait_apart(eng, sem, value, waited):
    wait(eng, sem, value)
    if not isinstance(value, int):
        eng.sem_inc(waited, 1)


class Steps:

    def __init__(self, eng, sem, base):
        self.eng, self.sem, self.base, self.n = eng, sem, base, 0

    def did(self, instruction):
        instruction.then_inc(self.sem, 1)
        self.n += 1

    def settled(self, waited=None):
        if waited is None:
            wait(self.eng, self.sem, self.base + self.n)
        else:
            wait_apart(self.eng, self.sem, self.base + self.n, waited)


def build(nc, x, ctx, cols, qkv, gate, sgu, sd, sd2, wgu, wd, out):
    xn_dram = nc.dram_tensor("xn_rows", (T + C, XW), F32).ap()
    even_dram = nc.dram_tensor("even_rows", (T + C, L), F32).ap()
    table_dram = nc.dram_tensor("slot_table", (C * E, W), F32).ap()
    last_dram = nc.dram_tensor("last_rows", (E, L), F32).ap()

    with ExitStack() as stack:
        def sb(name, shape, dt=F32):
            return stack.enter_context(nc.sbuf_tensor(name, shape, dt))

        def sem(name):
            return stack.enter_context(nc.semaphore(name))

        ident = sb("ident", [P, P])
        ident_b = sb("ident_b", [P, P], BF16)
        before = sb("before", [P, P], BF16)
        ones_b = sb("ones_b", [P, P], BF16)
        row_base = sb("row_base", [P, E])
        row_id = sb("row_id", [P, 1])
        is_last = sb("is_last", [P, 1])
        not_last = sb("not_last", [P, 1])
        last_dump = sb("last_dump", [P, 1])
        token = sb("token", [P, N])
        fill0 = sb("fill0", [P, 1])
        zeros = sb("zeros", [P, 512])
        cols_sb = sb("cols_sb", [P, 5])
        tanh_g = sb("tanh_g", [P, 2])
        vb_g = sb("vb_g", [P, 1])
        qkv_sb = sb("qkv_sb", [P, 3 * P])
        gate_sb = sb("gate_sb", [P, H2, E])
        sgu_sb = sb("sgu_sb", [P, H2, 2 * MS])
        sd_sb = sb("sd_sb", [P, 3, L])
        x_all = sb("x_all", [P, N, L])
        ctx_sb = sb("ctx_sb", [P, 2, 2, L])
        stats = sb("stats", [P, N, 6])
        mv = sb("mv", [P, N, 2])
        var = sb("var", [P, N + 2])
        nhalf = sb("nhalf", [P, N + 2])
        guess = sb("guess", [P, N + 2])
        newt = sb("newt", [P, N + 2])
        shift1 = sb("shift1", [P, N])
        x1n = sb("x1n", [P, 2, L])
        qk_sb = sb("qk_sb", [P, 2, 2 * L])
        v_sb = sb("v_sb", [P, 2, 2 * P])
        neg_max = sb("neg_max", [P, 2, 2])
        p_sb = sb("p_sb", [P, 2, 2, L])
        p_sum = sb("p_sum", [P, 2, 2])
        p_inv = sb("p_inv", [P, 2, 2])
        pt_sb = sb("pt_sb", [P, 2, 2 * L])
        h_sb = sb("h_sb", [P, 2, 2, P])
        stats2 = sb("stats2", [P, 2, 6])
        mv2 = sb("mv2", [P, 2, 2])
        xn2 = sb("xn2", [P, 2, L])
        xt_sb = sb("xt_sb", [P, H2, 2 * P])
        lg_max = sb("lg_max", [P, 2])
        es = sb("es", [P, 2, E])
        es_sum = sb("es_sum", [P, 2])
        es_inv = sb("es_inv", [P, 2])
        es_w = sb("es_w", [P, 2])
        g_max = sb("g_max", [P, 2, NG + 8 - TG])
        g_top = sb("g_top", [P, 2, 8])
        g_rep = sb("g_rep", [P, 2, NG + 8 - TG])
        kept = sb("kept", [P, 2, E + 8 - K])
        e_top = sb("e_top", [P, 2, 8])
        e_rep = sb("e_rep", [P, 2, E + 8 - K])
        sel = sb("sel", [P, 2, E], BF16)
        w_row = sb("w_row", [P, 2, E])
        counts = sb("counts", [P, E])
        pos = sb("pos", [P, 2, E])
        newest = sb("newest", [P, E])
        w_over = sb("w_over", [P, 2, E])
        code = sb("code", [P, 2, E])
        row_code = sb("row_code", [P, 2, E])
        row_top = sb("row_top", [P, 2, 8])
        slot_idx = sb("slot_idx", [P, 2, 2 * K], I32)
        meta = sb("meta", [P, 2, 2, W])
        xt_late = sb("xt_late", [P, NQ, H2 * 2 * P])
        w_over_t = sb("w_over_t", [P, T])
        tanh_sb = sb("tanh_sb", [P, 2, 2 * P])
        half_sb = sb("half_sb", [P, 2, 2 * P])
        act_t = sb("act_t", [P, 3, 2 * P])
        w_ring = sb("w_ring", [P, RING * GE * GU])
        d_ring = sb("d_ring", [MH, RING * GE * DW])
        table = sb("table", [C, E * W])
        table_fill = table
        gidx = sb("gidx", [C, E], I32)
        sidx = sb("sidx", [C, E], I32)
        slot_w = sb("slot_w", [C, 4])
        newest_col = sb("newest_col", [E, 1])
        newest_sel = sb("newest_sel", [E, C])
        gidx_now = sb("gidx_now", [C, 8 + AHEAD], I32)
        sidx_now = sb("sidx_now", [C, 8], I32)
        rows = [a[0:C].rearrange("p a f -> p (a f)") if len(a.shape) == 3 else
                a[0:C].rearrange("p a b f -> p (a b f)") for a in (qk_sb[:], ctx_sb[:], x1n[:], v_sb[:])]
        rows = [rows[k][:, i * XW:(i + 1) * XW] for k, n in ((0, 3), (1, 3), (2, 1), (3, 1)) for i in range(n)]
        rows_t = p_sb[:, :, :, :].rearrange("p a h f -> p (a h f)")[:, 0:2 * H2 * C]\
            .rearrange("p (a f) -> p a f", a=2)
        silu_sb = pt_sb[0:C, :, 0:M]
        act_sb = h_sb[0:C, :, :, :].rearrange("p a h f -> p a (h f)")[:, :, 0:M]
        act_tt = pt_sb[0:MH, :, 2 * P:2 * P + 2 * C]
        outs = [x_all[0:C, 4 * (b // 2) + b % 2, :] for b in range(OUTS)]
        even_sb = w_ring[:, 0:N * L].rearrange("p (n f) -> p n f", n=N)
        last_sb = sb("last_sb", [P, L])
        last_parts = sb("last_parts", [P, 3, L], BF16)
        high_mid, high_low = [xt_late[:, NQ // 2 * k:NQ // 2 * (k + 1), :].rearrange("p q f -> p (q f)")
                              .bitcast(BF16) for k in range(2)]

        bank = [stack.enter_context(nc.psum_tensor(f"bank{i}", [P, 512], F32)) for i in range(8)]

        s = {name: sem(name) for name in """
            x_in0 x_in1 x_in2 x_in3 first_in shared_in ctx_in0 ctx_in1 fills_in
            ident_ready consts_ready zeros_ready fill_step vb_ready fill_ready tanh_ready setup_step norm1_ready
            x1n_ready x_plus qk_done v_done qk_out v_out s_done nmax_ready p_ready p_inv_ready
            pt_done pt_out h_done h_out ht_done x1_ready att_step xn2_ready xn_saved w_row_ready w_saved
            xt_done xt_out xt_kept up_step lg_done lgmax_ready es_ready route_step sel_ready pos_done wov_ready
            wovt_done wov_out slots_ready meta_in0 meta_in1 gu_done th_ready act_ready down_done y_ready y_saved
            w_in0 w_in1 table_in newest_t newest_ready newest_mm tables_ready table_step
            idx_now rows_in0 rows_in1 rows_in2 rows_in3
            rows_in4 rows_in5 rows_in6 rows_in7 t_done t_out eg_done silu_ready a_ready
            at_done at_out slot_w_ready o_done o_ready acc_in0 acc_in1 lasts_saved0 lasts_saved1 lasts_in
            even_back0 even_back1 even_back2 even_back3 w_parts_ready w_part_step last_parts_ready last_part_step ov_done sum_ready result_added waited_dve waited_pe waited_act waited_pool""".split()}

        block = stack.enter_context(nc.Block())

        @block.sync
        def _(sp):
            for i, (lo, hi) in enumerate(X_LOADS):
                sp.dma_start(x_all[:, lo:hi, :], x[:, lo:hi, :]).then_inc(s[f"x_in{i}"], 16)
                if i == 0:
                    sp.dma_start(ctx_sb[:, 0, :, :], ctx[:, 0:2, :]).then_inc(s["ctx_in0"], 16)
            sp.wait_ge(s["zeros_ready"], 1)
            sp.wait_ge(s["shared_in"], 16 * 4)
            zero8 = zeros[:, :].rearrange("p (a f) -> p a f", a=1).to_broadcast([P, 8, 512])
            sp.dma_start(even_dram[0:T, :].rearrange("(p a) f -> p (a f)", p=P)
                         .rearrange("p (a f) -> p a f", a=8), zero8).then_inc(s["fills_in"], 16)
            for d, words in ((xn_dram, XW), (even_dram, L), (out, L)):
                sp.dma_start(d[T:T + C, :], zeros[0:C, 0:words]).then_inc(s["fills_in"], 16)
            sp.wait_ge(s["fill_ready"], 1)
            sp.dma_start(table_dram.rearrange("(c e) w -> c (e w)", c=C), table_fill[:, :])\
                .then_inc(s["fills_in"], 16)

            def load_weights(g, par):
                fixed = isinstance(g, int)
                at = g % RING if fixed else sp.snap(g % RING)
                at_gu = at * (GE * GU) if fixed else sp.snap(at * (GE * GU))
                at_d = at * (GE * DW) if fixed else sp.snap(at * (GE * DW))
                landed = (g // 2) * 32 if fixed else sp.snap((g // 2) * 32)
                freed = (g - RING + 1) * GE if fixed else sp.snap((g - RING + 1) * GE)
                wait(sp, s[f"w_in{par}"], landed)
                wait(sp, s["o_done"], freed)
                sp.dma_start(w_ring[:, bass.ds(at_gu, GE * GU)], wgu[g]).then_inc(s[f"w_in{par}"], 16)
                sp.dma_start(d_ring[:, bass.ds(at_d, GE * DW)], wd[g]).then_inc(s[f"w_in{par}"], 16)

            def save_y(q, pair):
                sp.wait_ge(s["y_ready"], 2 * q + 2)
                sp.dma_start(out[pair * 2 * P:(pair + 1) * 2 * P, :].rearrange("(n p) f -> p n f", p=P),
                             x_all[:, 2 * pair:2 * pair + 2, :]).then_inc(s["y_saved"], 16)

            def saves(r):
                if 1 <= r <= PAIRS:
                    lo = (r - 1) * (2 * P)
                    sp.wait_ge(s["xn2_ready"], r)
                    sp.dma_start(xn_dram[lo:lo + 2 * P, 0:L].rearrange("(n p) f -> p n f", p=P),
                                 xn2[:, :, :]).then_inc(s["xn_saved"], 16)
                if 3 <= r <= PAIRS + 1 and r % 2 == 1:
                    save_y((r - 3) // 2, r - 3)
                if 1 <= r <= PAIRS:
                    sp.wait_ge(s["w_row_ready"], r)
                    sp.dma_start(xn_dram[lo:lo + 2 * P, L:XW].rearrange("(n p) f -> p n f", p=P),
                                 w_row[:, :, :]).then_inc(s["w_saved"], 16)

            for r in range(PAIRS + 2):
                for g in range(2 * r, min(2 * r + 2, RING)):
                    load_weights(g, g % 2)
                saves(r)
            for j in range(NQ):
                save_y(NQ + j, 2 * j + 1)
                if j == 0:
                    sp.wait_ge(s["meta_in0"], 16 * K * N // 2)
                    sp.wait_ge(s["meta_in1"], 16 * K * N // 2)
                    sp.dma_start(table[:, :], table_dram.rearrange("(c e) w -> c (e w)", c=C))\
                        .then_inc(s["table_in"], 16)

            with sp.Fori(RING // 2, GROUPS // 2) as h:
                for par in range(2):
                    load_weights(2 * h + par, par)

            sp.wait_ge(s["lasts_saved0"], 8 * E // SAVED)
            sp.wait_ge(s["lasts_saved1"], 8 * E // SAVED - 16)
            sp.dma_start(last_sb[0:E - SAVED, :], last_dram[0:E - SAVED, :]).then_inc(s["lasts_in"], 16)
            sp.wait_ge(s["acc_in0"], 16 * E // 2)
            n = N // QUARTERS
            for q in range(QUARTERS):
                sp.dma_start(even_sb[:, n * q:n * (q + 1), :],
                             even_dram[P * n * q:P * n * (q + 1), :].rearrange("(n p) f -> p n f", p=P))\
                    .then_inc(s[f"even_back{q}"], 16)

        qk_ps = bank[0]
        v_ps = bank[1][:, 0:L]
        s_ps = bank[2]
        pt_ps = bank[3]
        down_ps = [bank[6][:, 0:L], bank[6][:, L:2 * L]]
        late_ps = [bank[3][:, 0:L], bank[6][:, 0:L]]
        late_gu_ps = [bank[2], bank[0], bank[5]]
        h_ps = bank[4][:, 0:L]
        ht_ps = bank[1][:, L:2 * L]
        wt_ps = bank[7][0:E, 2 * P:4 * P]
        gu_ps = [bank[6], bank[5], bank[6]]
        xt_ps = bank[5]
        lg_ps = bank[7][:, 0:2 * E]
        pos_ps = bank[7][:, 2 * E:4 * E]
        cnt_ps = bank[7][:, 0:E]

        @block.tensor
        def _(pe):
            def mm(o, lhsT, rhs, start=True, stop=True):
                return pe.matmul(o, lhsT, rhs, start=start, stop=stop, skip_group_check=True)

            def queries_keys(r, i, par):
                t = 2 * r + i
                if i == 0:
                    wait(pe, s[f"ctx_in{par}"], r * 8 + 16 - 8 * par)
                wait(pe, s["x1n_ready"], t + 1)
                wait(pe, s["qk_out"], t)
                mm(qk_ps[:, 0:L], qkv_sb[:, 0:P], x1n[:, i, :])
                mm(qk_ps[:, L:2 * L], qkv_sb[:, P:2 * P], ctx_sb[:, par, i, :]).then_inc(s["qk_done"], 1)

            def values(r, i, par):
                t = 2 * r + i
                wait(pe, s["v_out"], t)
                wait(pe, s["x1_ready"], 2 * r)
                for h in range(2):
                    last = mm(v_ps[:, h * P:(h + 1) * P], ctx_sb[:, par, i, h * P:(h + 1) * P], qkv_sb[:, 2 * P:3 * P])
                last.then_inc(s["v_done"], 1)

            def scores(r, i):
                t = 2 * r + i
                wait(pe, s["qk_out"], t + 1)
                wait(pe, s["p_ready"], t)
                for h in range(2):
                    last = mm(s_ps[:, h * L:(h + 1) * L], qk_sb[:, i, h * P:(h + 1) * P], qk_sb[:, i, L:2 * L])
                last.then_inc(s["s_done"], 1)

            def turn_p(r, i):
                t = 2 * r + i
                wait(pe, s["p_ready"], t + 1)
                wait(pe, s["pt_out"], t)
                for h in range(2):
                    for k in range(2):
                        last = pe.transpose(pt_ps[:, k * L + h * P:k * L + (h + 1) * P],
                                            p_sb[:, i, h, k * P:(k + 1) * P], ident[:, :])
                last.then_inc(s["pt_done"], 1)

            def attend(r, i):
                t = 2 * r + i
                wait(pe, s["pt_out"], t + 1)
                wait(pe, s["v_out"], t + 1)
                wait(pe, s["h_out"], t)
                for h in range(2):
                    for k in range(2):
                        last = mm(h_ps[:, h * P:(h + 1) * P], pt_sb[:, i, k * L + h * P:k * L + (h + 1) * P],
                                  v_sb[:, i, k * P:(k + 1) * P], start=k == 0, stop=k == 1)
                last.then_inc(s["h_done"], 1)

            def turn_h(r, i):
                t = 2 * r + i
                wait(pe, s["h_out"], t + 1)
                wait(pe, s["v_out"], 2 * r + 2)
                wait(pe, s["x1_ready"], t)
                for h in range(2):
                    last = pe.transpose(ht_ps[:, h * P:(h + 1) * P], h_sb[:, i, h, :], ident[:, :])
                last.then_inc(s["ht_done"], 1)

            def turn_x(r, h, par):
                wait(pe, s["xn2_ready"], r)
                wait(pe, s["xt_out"], r - 1)
                wait(pe, s["xt_kept"], h - 1 + par)
                wait(pe, s["act_ready"], 3 * h - 1)
                for i in range(2):
                    for k in range(H2):
                        last = pe.transpose(xt_ps[:, k * L + i * P:k * L + (i + 1) * P],
                                            xn2[:, i, k * P:(k + 1) * P], ident[:, :])
                last.then_inc(s["xt_done"], 1)

            def logits(r):
                wait(pe, s["xt_out"], r)
                wait(pe, s["wov_ready"], r - 1)
                for i in range(2):
                    for h in range(H2):
                        last = mm(lg_ps[:, i * E:(i + 1) * E], xt_sb[:, h, i * P:(i + 1) * P], gate_sb[:, h, :],
                                  start=h == 0, stop=h == H2 - 1)
                last.then_inc(s["lg_done"], 1)

            def shared_up(q, m, xt, ps):
                lo, n = MT[m]
                if m == 0:
                    wait(pe, s["act_ready"], 3 * q)
                    wait(pe, s["y_ready"], 2 * q)
                if m == 2:
                    wait(pe, s["act_ready"], 3 * q + 1)
                for b in range(2):
                    for h in range(H2):
                        last = mm(ps[m][0:n, b * L:(b + 1) * L], sgu_sb[:, h, b * MS + lo:b * MS + lo + n],
                                  xt[:, h * L:(h + 1) * L], start=h == 0, stop=h == H2 - 1)
                last.then_inc(s["gu_done"], 1)

            def places(r):
                wait(pe, s["sel_ready"], r - 1)
                wait(pe, s["wov_out"], r - 2)
                mm(pos_ps[:, 0:E], before[:, :], sel[:, 0, :])
                mm(pos_ps[:, E:2 * E], before[:, :], sel[:, 1, :], stop=False)
                mm(pos_ps[:, E:2 * E], ones_b[:, :], sel[:, 0, :], start=False)
                mm(cnt_ps, ones_b[:, :], sel[:, 0, :], stop=False)
                mm(cnt_ps, ones_b[:, :], sel[:, 1, :], start=False).then_inc(s["pos_done"], 1)

            def shared_down(q, i, to):
                wait(pe, s["act_ready"], 3 * q + 3)
                wait(pe, s["y_ready"], 2 * q + i if to is down_ps else 2 * q - 1 + i)
                for m, (lo, n) in enumerate(MT):
                    last = mm(to[i], act_t[0:n, m, i * P:(i + 1) * P], sd_sb[0:n, m, :],
                              start=m == 0, stop=m == 2)
                last.then_inc(s["down_done"], 1)

            def turn_w(r):
                wait(pe, s["es_ready"], r if not isinstance(r, int) else min(r, PAIRS))
                wait_apart(pe, s["wov_ready"], r - 1, waited)
                for i in range(2):
                    last = pe.transpose(wt_ps[:, i * P:(i + 1) * P], w_over[:, i, :], ident[:, :])
                last.then_inc(s["wovt_done"], 1)

            waited = s["waited_pe"]
            pe.wait_ge(s["ident_ready"], 2)
            pe.wait_ge(s["first_in"], 32)
            xt = xt_sb[:, :, :].rearrange("p h t -> p (h t)")

            def step(r, h, par, att=True, turn=True, place=True):
                if att:
                    scores(r, 0)
                    queries_keys(r, 1, par)
                    values(r, 0, par)
                if place:
                    places(r)
                    if par == 0:
                        shared_up(h - 1, 2, xt, gu_ps)
                    else:
                        shared_down(h - 1, 1, down_ps)
                if att:
                    scores(r, 1)
                    turn_p(r, 0)
                    values(r, 1, par)
                    attend(r, 0)
                if turn:
                    turn_x(r, h, par)
                if att:
                    turn_p(r, 1)
                if turn:
                    logits(r)
                    if par == 1:
                        shared_up(h, 0, xt, gu_ps)
                        shared_up(h, 1, xt, gu_ps)
                if place and par == 0:
                    shared_down(h - 1, 0, down_ps)
                if att:
                    turn_h(r, 0)
                    attend(r, 1)
                    if not isinstance(r, int) or r < PAIRS - 1:
                        queries_keys(r + 1, 0, 1 - par)
                    turn_h(r, 1)
                if place:
                    turn_w(r)

            queries_keys(0, 0, 0)
            step(0, 0, 0, turn=False, place=False)
            pe.wait_ge(s["shared_in"], 16 * 4)
            pe.wait_ge(s["consts_ready"], 3)
            step(1, 0, 1, place=False)
            with pe.Fori(1, PAIRS // 2 - 1) as h:
                step(2 * h, h, 0)
                step(2 * h + 1, h, 1)
            step(PAIRS - 2, NQ - 1, 0)
            step(PAIRS - 1, NQ - 1, 1)
            def late_up(q, m):
                lo, n = MT[m]
                if q == NQ:
                    pe.wait_ge(*((s["p_ready"], N), (s["qk_out"], N), (s["xt_kept"], NQ))[m])
                else:
                    pe.wait_ge(s["act_ready"], 3 * (q - 1) + m + 1)
                xt_q = xt_late[:, q - NQ, :]
                for b in range(2):
                    for h in range(H2):
                        last = mm(late_gu_ps[m][0:n, b * L:(b + 1) * L],
                                  sgu_sb[:, h, b * MS + lo:b * MS + lo + n],
                                  xt_q[:, h * L:(h + 1) * L], start=h == 0, stop=h == H2 - 1)
                last.then_inc(s["gu_done"], 1)

            t_ps = bank[2][:, 0:H2 * C]
            at_ps = bank[3][0:MH, 0:2 * C]
            eg_ps = [bank[4][0:C, 0:2 * M], bank[5][0:C, 0:2 * M]]
            o_ps = [bank[6][0:C, 0:L], bank[7][0:C, 0:L]]

            def turn_rows(e, b):
                wait(pe, s[f"rows_in{b % ROWS}"], (e - b % ROWS) * (16 // ROWS) + 16)
                wait(pe, s["t_out"], e)
                for h in range(H2):
                    last = pe.transpose(t_ps[:, h * C:(h + 1) * C], rows[b % ROWS][:, h * P:(h + 1) * P],
                                        ident[0:C, 0:C])
                last.then_inc(s["t_done"], 1)

            def at_ring(e, words):
                return e % (RING * GE) * words

            def up(e, b):
                if b % GE == 0:
                    wait(pe, s[f"w_in{b // GE % 2}"], e * (16 // GE) + 32 - 16 * (b // GE % 2))
                at = at_ring(e, GU)
                at = at if isinstance(at, int) else pe.snap(at)
                wait(pe, s["t_out"], e + 1)
                wait(pe, s["a_ready"], e - 1)
                for h in range(H2):
                    last = mm(eg_ps[b % 2], rows_t[:, b % 2, h * C:(h + 1) * C],
                              w_ring[:, bass.ds(at + h * 2 * M, 2 * M)], start=h == 0, stop=h == H2 - 1)
                last.then_inc(s["eg_done"], 1)

            shared_up(NQ - 1, 2, xt, gu_ps)
            places(PAIRS)
            pe.wait_ge(s["xt_kept"], 1)
            late_up(NQ, 0)
            late_up(NQ, 1)
            turn_x(PAIRS, NQ, 0)
            shared_down(NQ - 1, 0, down_ps)
            logits(PAIRS)
            shared_down(NQ - 1, 1, down_ps)
            late_up(NQ, 2)
            turn_w(PAIRS)
            places(PAIRS + 1)
            late_up(NQ + 1, 0)
            pe.wait_ge(s["pt_out"], N)
            pe.wait_ge(s["h_out"], N)
            for q in range(NQ + 1, 2 * NQ):
                if q > NQ + 1:
                    late_up(q, 0)
                late_up(q, 1)
                shared_down(q - 1, 0, late_ps)
                shared_down(q - 1, 1, late_ps)
                if q == NQ + 1:
                    turn_w(PAIRS + 1)
                    nt_ps, nr_ps = bank[1][0:E, 0:P], bank[1][0:C, P:P + E]
                    pe.wait_ge(s["route_step"], K_ROUTE * PAIRS)
                    pe.wait_ge(s["v_out"], N)
                    pe.wait_ge(s["x1_ready"], N)
                    pe.transpose(nt_ps, newest[:, :], ident[:, :]).then_inc(s["newest_t"], 1)
                elif q == NQ + 2:
                    pe.wait_ge(s["newest_ready"], 1)
                    mm(nr_ps, newest_sel[:, :], ident[0:E, 0:E]).then_inc(s["newest_mm"], 1)
                late_up(q, 2)
            pe.wait_ge(s["act_ready"], 3 * (2 * NQ - 1) + 1)
            turn_rows(0, 0)
            up(0, 0)
            shared_down(2 * NQ - 1, 0, late_ps)
            shared_down(2 * NQ - 1, 1, late_ps)

            def turn_act(e, b):
                wait(pe, s["a_ready"], e + 1)
                wait(pe, s["at_out"], e)
                for m in range(2):
                    last = pe.transpose(at_ps[:, m * C:(m + 1) * C], act_sb[:, b % 2, m * MH:(m + 1) * MH],
                                        ident[0:C, 0:C])
                last.then_inc(s["at_done"], 1)

            def down(e, b):
                at = at_ring(e, DW)
                at = at if isinstance(at, int) else pe.snap(at)
                wait(pe, s["at_out"], e + 1)
                wait(pe, s["o_ready"], e - 1)
                for m in range(2):
                    last = mm(o_ps[b % 2], act_tt[:, b % 2, m * C:(m + 1) * C],
                              d_ring[:, bass.ds(at + m * L, L)], start=m == 0, stop=m == 1)
                last.then_inc(s["o_done"], 1)

            def expert(e, b):
                known = isinstance(e, int)
                if not known or e < E - 1:
                    turn_rows(e + 1, b + 1)
                if not known or e < E:
                    up(e, b)
                if not known or e > 1:
                    down(e - 2, b - 2)
                if not known or 0 < e <= E:
                    turn_act(e - 1, b - 1)

            pe.wait_ge(s["p_ready"], N)
            pe.wait_ge(s["y_ready"], N)
            pe.wait_ge(s["wov_out"], PAIRS)
            pe.wait_ge(s["act_ready"], 3 * PAIRS)
            pe.wait_ge(s["wov_ready"], PAIRS)
            turn_rows(1, 1)
            for e in range(1, 10):
                expert(e, e)
            with pe.Fori(1, E // 8 - 1) as q:
                for b in range(2, 10):
                    expert(8 * q + b, b)
            for e in range(E - 6, E + 2):
                expert(e, e)

            pe.wait_ge(s["t_out"], E)
            pe.wait_ge(s["at_out"], E)
            early = (0, 2, 4, 6)
            pe.wait_ge(s["last_parts_ready"], 1)
            for t in early:
                pe.wait_ge(s["w_parts_ready"], t + 1)
                mm(bank[t // 2][:, 0:L], high_mid[:, t * P:(t + 1) * P], last_parts[:, 0, :], stop=False)
            pe.wait_ge(s["last_parts_ready"], 2)
            for t in range(N):
                pe.wait_ge(s["w_parts_ready"], t + 1)
                if t // 2 == 6:
                    pe.wait_ge(s["o_ready"], E)
                for k, part in enumerate((high_mid, high_mid, high_low)):
                    if k == 0 and t in early:
                        continue
                    last = mm(bank[t // 2][:, t % 2 * L:(t % 2 + 1) * L], part[:, t * P:(t + 1) * P],
                              last_parts[:, k, :], start=k == 0, stop=k == 2)
                last.then_inc(s["ov_done"], 1)

        @block.scalar
        def _(act):
            act.dma_start(cols_sb[:, :], cols).then_inc(s["first_in"], 16)
            act.dma_start(qkv_sb[:, :], qkv).then_inc(s["first_in"], 16)
            act.dma_start(ctx_sb[:, 1, :, :], ctx[:, 2:4, :]).then_inc(s["ctx_in1"], 16)
            act.dma_start(gate_sb[:, :, :], gate).then_inc(s["shared_in"], 16)
            act.dma_start(sgu_sb[:, :, :], sgu).then_inc(s["shared_in"], 16)
            act.dma_start(sd_sb[:, 0:2, :], sd).then_inc(s["shared_in"], 16)
            act.dma_start(sd_sb[0:MT[2][1], 2, :], sd2).then_inc(s["shared_in"], 16)
            act.wait_ge(s["zeros_ready"], 1)
            act.activation(tanh_sb[:, 0, 0:2], zeros[:, 0:2], ACT.Tanh)
            act.wait_ge(s["first_in"], 32)
            act.activation(tanh_g[:, :], cols_sb[:, 3:5], ACT.Tanh).then_inc(s["tanh_ready"], 1)

            def norm1(r, i):
                t = 2 * r + i
                wait(act, s["norm1_ready"], min(r, 2) + 1 if isinstance(r, int) else 3)
                wait(act, s["qk_done"], t - 1)
                at = t if isinstance(t, int) else act.snap(t)
                at_s = at if isinstance(t, int) and t < 4 else at + 2 if isinstance(t, int) else act.snap(t + 2)
                act.activation(x1n[:, i, :], x_all[:, bass.ds(at, 1), :].rearrange("p a f -> p (a f)"),
                               ACT.Identity, scale=guess[:, bass.ds(at_s, 1)], bias=shift1[:, bass.ds(at, 1)])\
                    .then_inc(s["x1n_ready"], 1)

            def add_bias(r, i):
                t = 2 * r + i
                wait_apart(act, s["x1n_ready"], t + 1, s["waited_act"])
                at = t if isinstance(t, int) else act.snap(t)
                tile = x_all[:, bass.ds(at, 1), :].rearrange("p a f -> p (a f)")
                act.activation(tile, tile, ACT.Identity, bias=vb_g[:, :]).then_inc(s["x_plus"], 1)

            def take_qk(r, i):
                t = 2 * r + i
                wait(act, s["qk_done"], t + 1)
                wait(act, s["s_done"], t - 1)
                act.activation(qk_sb[:, i, 0:L], qk_ps[:, 0:L], ACT.Identity, bias=cols_sb[:, 0:1])
                act.activation(qk_sb[:, i, L:2 * L], qk_ps[:, L:2 * L], ACT.Identity, bias=cols_sb[:, 1:2])\
                    .then_inc(s["qk_out"], 1)

            def take_v(r, i):
                t = 2 * r + i
                wait(act, s["v_done"], t + 1)
                wait(act, s["h_done"], t - 1)
                act.activation(v_sb[:, i, :], v_ps, ACT.Copy).then_inc(s["v_out"], 1)

            def exps(r, i):
                t = 2 * r + i
                wait(act, s["nmax_ready"], t + 1)
                wait(act, s["pt_done"], t - 1)
                wait(act, s["p_inv_ready"], t - 1)
                for h in range(2):
                    last = act.activation(p_sb[:, i, h, :], s_ps[:, h * L:(h + 1) * L], ACT.Exp,
                                          bias=neg_max[:, i, h:h + 1], accum_out=p_sum[:, i, h:h + 1])
                last.then_inc(s["p_ready"], 1)

            def take_pt(r, i):
                t = 2 * r + i
                wait(act, s["pt_done"], t + 1)
                wait(act, s["h_done"], t - 1)
                act.activation(pt_sb[:, i, :], pt_ps[:, :], ACT.Copy).then_inc(s["pt_out"], 1)

            def take_h(r, i):
                t = 2 * r + i
                wait(act, s["h_done"], t + 1)
                wait(act, s["p_inv_ready"], t + 1)
                wait(act, s["ht_done"], t - 1)
                for h in range(2):
                    last = act.activation(h_sb[:, i, h, :], h_ps[:, h * P:(h + 1) * P], ACT.Copy,
                                          scale=p_inv[:, i, h:h + 1])
                last.then_inc(s["h_out"], 1)

            def take_xt(r, h):
                wait(act, s["xt_done"], r)
                wait(act, s["lg_done"], r - 1)
                wait(act, s["gu_done"], 3 * h)
                act.activation(xt_sb[:, :, :].rearrange("p h t -> p (h t)"), xt_ps[:, :], ACT.Copy)\
                    .then_inc(s["xt_out"], 1)

            def keep_xt(h):
                at = h - 1 if isinstance(h, int) else act.snap(h - 1)
                act.activation(xt_late[:, bass.ds(at, 1), :].rearrange("p a f -> p (a f)"), xt_ps[:, :], ACT.Copy)\
                    .then_inc(s["xt_kept"], 1)

            def exp_logits(r):
                wait(act, s["lgmax_ready"], r)
                for i in range(2):
                    last = act.activation(es[:, i, :], lg_ps[:, i * E:(i + 1) * E], ACT.Exp,
                                          bias=lg_max[:, i:i + 1], accum_out=es_sum[:, i:i + 1])
                last.then_inc(s["es_ready"], 1)

            def tanh_part(q, m, ps):
                lo, n = MT[m]
                wait(act, s["gu_done"], 3 * q + m + 1)
                b = m % 2
                wait(act, s["act_ready"], 3 * q + (0 if m == 0 else m - 1))
                act.activation(tanh_sb[0:n, b, :], ps[m][0:n, 0:L], ACT.Tanh, scale=0.5)\
                    .then_inc(s["th_ready"], 1)

            def take_wov(r):
                wait(act, s["wovt_done"], r - 1)
                at = (r - 2) * (2 * P)
                at = at if isinstance(at, int) else act.snap(at)
                act.activation(w_over_t[0:E, bass.ds(at, 2 * P)], wt_ps, ACT.Copy).then_inc(s["wov_out"], 1)

            def step(r, h, par, att=True, turn=True, place=True):
                ahead = att and (not isinstance(r, int) or r < PAIRS - 1)
                if att:
                    take_qk(r, 1)
                    exps(r, 0)
                    take_v(r, 0)
                if place and par == 0:
                    tanh_part(h - 1, 2, gu_ps)
                if att:
                    take_pt(r, 0)
                    take_v(r, 1)
                    if not isinstance(r, int) or r < PAIRS - 2:
                        at = 2 * r + 4
                        at = at if isinstance(at, int) else act.snap(at)
                        act.dma_start(ctx_sb[:, par, :, :], ctx[:, bass.ds(at, 2), :]).then_inc(s[f"ctx_in{par}"], 16)
                if att:
                    exps(r, 1)
                if turn:
                    take_xt(r, h)
                if att:
                    take_h(r, 0)
                    take_pt(r, 1)
                if turn:
                    exp_logits(r)
                    if par == 1:
                        tanh_part(h, 0, gu_ps)
                if ahead:
                    norm1(r + 1, 0)
                if turn and par == 1:
                    tanh_part(h, 1, gu_ps)
                if turn and par == 0:
                    keep_xt(h)
                if att:
                    take_h(r, 1)
                if ahead:
                    take_qk(r + 1, 0)
                if place:
                    take_wov(r)
                if ahead:
                    norm1(r + 1, 1)
                    add_bias(r + 1, 0)
                    add_bias(r + 1, 1)

            norm1(0, 0)
            norm1(0, 1)
            take_qk(0, 0)
            act.wait_ge(s["vb_ready"], 1)
            add_bias(0, 0)
            add_bias(0, 1)
            step(0, 0, 0, turn=False, place=False)
            step(1, 0, 1, place=False)
            with act.Fori(1, PAIRS // 2 - 1) as h:
                step(2 * h, h, 0)
                step(2 * h + 1, h, 1)
            step(PAIRS - 2, NQ - 1, 0)
            step(PAIRS - 1, NQ - 1, 1)
            tanh_part(NQ - 1, 2, gu_ps)
            take_xt(PAIRS, NQ)
            exp_logits(PAIRS)
            keep_xt(NQ)
            for q in range(NQ, 2 * NQ):
                tanh_part(q, 0, late_gu_ps)
                tanh_part(q, 1, late_gu_ps)
                if q < NQ + 2:
                    take_wov(PAIRS + q - NQ)
                tanh_part(q, 2, late_gu_ps)

            t_ps = bank[2][:, 0:H2 * C]
            eg_ps = [bank[4][0:C, 0:2 * M], bank[5][0:C, 0:2 * M]]
            o_ps = [bank[6][0:C, 0:L], bank[7][0:C, 0:L]]

            def take_rows(e, b):
                wait(act, s["t_done"], e + 1)
                wait(act, s["eg_done"], e - 1)
                act.activation(rows_t[:, b % 2, :], t_ps, ACT.Copy).then_inc(s["t_out"], 1)

            def silu(e, b):
                wait(act, s["eg_done"], e + 1)
                wait(act, s["a_ready"], e - 1)
                act.activation(silu_sb[:, b % 2, :], eg_ps[b % 2][:, 0:M], ACT.Silu).then_inc(s["silu_ready"], 1)

            def take_out(e, b):
                wait(act, s["o_done"], e + 1)
                wait(act, s["slot_w_ready"], e + 1)
                wait(act, s[f"acc_in{b % 2}"], 8 * (e - OUTS) + 16 - 8 * (b % 2))
                wait(act, s[f"lasts_saved{b // SAVED % 2}"], 2 * (e - b % SAVED) - 8 * (b // SAVED % 2))
                act.activation(outs[b % OUTS], o_ps[b % 2], ACT.Copy, scale=slot_w[:, b % 4:b % 4 + 1])\
                    .then_inc(s["o_ready"], 1)

            def save_lasts(e, b):
                at = e - (SAVED - 1)
                at = at if isinstance(at, int) else act.snap(at)
                wait(act, s["o_ready"], e + 1)
                lo = (b - (SAVED - 1)) % OUTS
                lasts = x_all[LAST:C, :, :].rearrange("p (a b c) f -> p a b (c f)", b=2, c=2)\
                    [:, lo // 2:lo // 2 + SAVED // 2, 0, :]
                act.dma_start(last_dram[bass.ds(at, SAVED), :].rearrange("(o a c) f -> o a (c f)", o=1, c=2),
                              lasts).then_inc(s[f"lasts_saved{b // SAVED % 2}"], 16)

            def expert(e, b):
                known = isinstance(e, int)
                if not known or e < E - 1:
                    take_rows(e + 1, b + 1)
                if not known or e < E:
                    silu(e, b)
                if not known or e > 1:
                    take_out(e - 2, b - 2)
                    if known and e - 2 >= E - SAVED:
                        act.wait_ge(s["o_ready"], e - 1)
                        act.dma_start(last_sb[e - 2:e - 1, :], outs[(b - 2) % OUTS][LAST:C])\
                            .then_inc(s["lasts_in"], 16)
                    elif b % SAVED == 1:
                        save_lasts(e - 2, b - 2)

            take_rows(0, 0)
            for e in range(2):
                expert(e, e)
            act.wait_ge(s["y_saved"], 16 * PAIRS)
            for e in range(2, 11):
                expert(e, e)
            with act.Fori(0, (E - 16) // 8) as q:
                for b in range(11, 19):
                    expert(8 * q + b, b)
            for e in range(E - 5, E + 2):
                expert(e, e)

        @block.vector
        def _(dve):
            setup = Steps(dve, s["setup_step"], 0)
            waited = s["waited_dve"]
            dve.memset(zeros[:, :], 0.0).then_inc(s["zeros_ready"], 1)

            def newton_start(go, c):
                go.did(dve.tensor_scalar(guess[:, c].bitcast(I32), var[:, c].bitcast(I32), 1, None,
                                         ALU.logical_shift_right))
                go.did(dve.tensor_scalar(nhalf[:, c], var[:, c], -0.5, None, ALU.mult))

            def newton_guess(go, c):
                go.settled()
                go.did(dve.tensor_scalar(guess[:, c].bitcast(I32), guess[:, c].bitcast(I32), -1.0, MAGIC,
                                         ALU.mult, ALU.add))

            def newton_square(go, c):
                go.settled()
                go.did(dve.tensor_tensor(newt[:, c], guess[:, c], guess[:, c], ALU.mult))

            def newton_scale(go, c):
                go.settled()
                go.did(dve.tensor_tensor(newt[:, c], newt[:, c], nhalf[:, c], ALU.mult))

            def newton_update(go, c):
                go.settled()
                go.did(dve.scalar_tensor_tensor(guess[:, c], newt[:, c], 1.5, guess[:, c], ALU.add, ALU.mult))

            def stats1(c):
                dve.wait_ge(s[f"x_in{c}"], 16)
                for t in range(*X_LOADS[c]):
                    setup.did(dve.bn_stats(stats[:, t, :], x_all[:, t, :]))

            def variances1(lo, hi, c):
                setup.settled()
                for t in range(lo, hi):
                    setup.did(dve.bn_aggr(mv[:, t, :], stats[:, t, :]))
                setup.settled()
                setup.did(dve.tensor_scalar(var[:, c], mv[:, lo:hi, 1], EPS, None, ALU.add))
                setup.settled()

            def shifts1(lo, hi, c):
                dve.scalar_tensor_tensor(shift1[:, lo:hi], mv[:, lo:hi, 0], -1.0, guess[:, c], ALU.mult, ALU.mult)\
                    .then_inc(s["norm1_ready"], 1)

            def scales1(lo, hi):
                c = slice(lo, hi)
                variances1(lo, hi, c)
                newton_start(setup, c)
                newton_guess(setup, c)
                for _ in range(3):
                    newton_square(setup, c)
                    newton_scale(setup, c)
                    newton_update(setup, c)
                setup.settled()
                shifts1(lo, hi, c)

            for c in range(2):
                stats1(c)
                scales1(*X_LOADS[c])
            dve.wait_ge(s["tanh_ready"], 1)
            dve.tensor_tensor(vb_g[:, :], cols_sb[:, 2:3], tanh_g[:, 0:1], ALU.mult).then_inc(s["vb_ready"], 1)

            def smax(r, i):
                t = 2 * r + i
                wait(dve, s["s_done"], t + 1)
                wait(dve, s["p_ready"], t - 1)
                dve.tensor_reduce(neg_max[:, i, :], s_ps[:, :].rearrange("p (h k) -> p h k", h=2), AX, ALU.max,
                                  negate=True).then_inc(s["nmax_ready"], 1)

            def inverse_sum(r, i):
                t = 2 * r + i
                wait(dve, s["p_ready"], t + 1)
                wait(dve, s["h_out"], t - 1)
                dve.reciprocal(p_inv[:, i, :], p_sum[:, i, :]).then_inc(s["p_inv_ready"], 1)

            def residual(r, i, at, go):
                t = 2 * r + i
                wait(dve, s["ht_done"], t + 1)
                wait(dve, s["x_plus"], t + 1)
                tile = x_all[:, at + i, :] if isinstance(at, int) else \
                    x_all[:, bass.ds(at + i, 1), :].rearrange("p a f -> p (a f)")
                dve.scalar_tensor_tensor(tile, ht_ps, tanh_g[:, 0:1], tile, ALU.mult, ALU.add)\
                    .then_inc(s["x1_ready"], 1)

            def statistics(r, i, at, go, part):
                if part == 1:
                    go.settled(waited)
                    go.did(dve.bn_aggr(mv2[:, i, :], stats2[:, i, :]))
                    return
                t = 2 * r + i
                tile = x_all[:, at + i, :] if isinstance(at, int) else \
                    x_all[:, bass.ds(at + i, 1), :].rearrange("p a f -> p (a f)")
                wait_apart(dve, s["x1_ready"], t + 1, waited)
                go.did(dve.bn_stats(stats2[:, i, :], tile))

            def norm2(r, at, go):
                go.settled()
                wait(dve, s["xt_done"], r)
                wait(dve, s["xn_saved"], 16 * r)
                for i in range(2):
                    tile = x_all[:, at + i, :] if isinstance(at, int) else \
                        x_all[:, bass.ds(at + i, 1), :].rearrange("p a f -> p (a f)")
                    ins = dve.tensor_scalar(xn2[:, i, :], tile, mv2[:, i, 0:1], guess[:, 4 + i:5 + i],
                                            ALU.subtract, ALU.mult)
                    if i == 0:
                        go.did(ins)
                    else:
                        ins.then_inc(s["xn2_ready"], 1)

            def shared_act(q, m, half, ps):
                lo, n = MT[m]
                g, u = ps[m][0:n, 0:L], ps[m][0:n, L:2 * L]
                if half == 0:
                    wait(dve, s["th_ready"], 3 * q + m + 1)
                    dve.scalar_tensor_tensor(half_sb[0:n, m % 2, :], tanh_sb[0:n, m % 2, :], 1.0, g,
                                             ALU.add, ALU.mult).then_inc(s["up_step"], 1)
                else:
                    wait(dve, s["up_step"], 3 * q + m + 1)
                    if m == 0:
                        wait(dve, s["down_done"], 2 * q)
                    dve.scalar_tensor_tensor(act_t[0:n, m, :], half_sb[0:n, m % 2, :], 0.5, u, ALU.mult, ALU.mult)\
                        .then_inc(s["act_ready"], 1)

            def max_logit(r):
                wait(dve, s["lg_done"], r)
                wait(dve, s["es_ready"], r - 1)
                dve.tensor_reduce(lg_max[:, :], lg_ps.rearrange("p (i e) -> p i e", i=2), AX, ALU.max, negate=True)\
                    .then_inc(s["lgmax_ready"], 1)

            def choose(r, go, part):
                if part == 0:
                    wait(dve, s["es_ready"], r)
                    go.did(dve.tensor_reduce(g_max[:, :, 0:NG], es[:, :, :].rearrange("p i (g e) -> p i g e", g=NG),
                                             AX, ALU.max))
                    go.did(dve.reciprocal(es_inv[:, :], es_sum[:, :]))
                elif part == 1:
                    go.settled(waited)
                    for i in range(2):
                        go.did(dve.max(g_top[:, i, :], g_max[:, i, 0:NG]))
                elif part == 2:
                    go.settled()
                    go.did(dve.memset(g_top[:, :, TG:8], GONE))
                    go.did(dve.tensor_tensor(es_w[:, :], es_inv[:, :], tanh_g[:, 1:2].to_broadcast([P, 2]), ALU.mult))
                elif part == 3:
                    go.settled(waited)
                    for i in range(2):
                        go.did(dve.match_replace(g_rep[:, i, :], g_top[:, i, :], g_max[:, i, :], TAKEN))
                elif part == 4:
                    go.settled()
                    for i in range(2):
                        go.did(dve.scalar_tensor_tensor(
                            kept[:, i, 0:E].rearrange("p (g e) -> p g e", g=NG),
                            g_rep[:, i, 0:NG].rearrange("p (g a) -> p g a", a=1).to_broadcast([P, NG, E // NG]), 0.0,
                            es[:, i, :].rearrange("p (g e) -> p g e", g=NG), ALU.is_lt, ALU.mult))
                elif part == 5:
                    go.settled(waited)
                    for i in range(2):
                        go.did(dve.max(e_top[:, i, :], kept[:, i, 0:E]))
                elif part == 6:
                    go.settled()
                    go.did(dve.memset(e_top[:, :, K:8], GONE))
                elif part == 7:
                    go.settled(waited)
                    for i in range(2):
                        go.did(dve.match_replace(e_rep[:, i, :], e_top[:, i, :], kept[:, i, :], TAKEN))
                elif part == 8:
                    go.settled()
                    wait(dve, s["pos_done"], r - 1)
                    dve.tensor_scalar(sel[:, :, :], e_rep[:, :, 0:E], 0.0, None, ALU.is_lt).then_inc(s["sel_ready"], 1)
                else:
                    wait(dve, s["sel_ready"], r)
                    wait(dve, s["w_saved"], 16 * (r - 1))
                    for i in range(2):
                        ins = dve.scalar_tensor_tensor(w_row[:, i, :], kept[:, i, 0:E], es_w[:, i:i + 1],
                                                       sel[:, i, :], ALU.mult, ALU.mult)
                        if i == 0:
                            go.did(ins)
                        else:
                            ins.then_inc(s["w_row_ready"], 1)

            def place(r, at, go, part):
                if part == 0:
                    wait(dve, s["pos_done"], r - 1)
                    go.did(dve.tensor_tensor(
                        pos[:, :, :], pos_ps.rearrange("p (i e) -> p i e", i=2),
                        counts[:, :].rearrange("p (a e) -> p a e", a=1).to_broadcast([P, 2, E]), ALU.add))
                elif part in (1, 2):
                    i = part - 1
                    tok = token[:, at + i:at + i + 1] if isinstance(at, int) else token[:, bass.ds(at + i, 1)]
                    go.settled()
                    go.did(dve.scalar_tensor_tensor(newest[:, :], sel[:, i, :], tok, newest[:, :],
                                                    ALU.mult, ALU.max))
                elif part == 3:
                    go.did(dve.tensor_tensor(counts[:, :], counts[:, :], cnt_ps, ALU.add))
                elif part == 4:
                    wait(dve, s["w_row_ready"], r - 1)
                    wait(dve, s["wovt_done"], r - 2)
                    dve.scalar_tensor_tensor(w_over[:, :, :], pos[:, :, :], float(LAST), w_row[:, :, :],
                                             ALU.is_ge, ALU.mult).then_inc(s["wov_ready"], 1)
                elif part == 5:
                    go.did(dve.scalar_tensor_tensor(
                        code[:, :, :], pos[:, :, :], -float(E),
                        row_base[:, :].rearrange("p (a e) -> p a e", a=1).to_broadcast([P, 2, E]),
                        ALU.mult, ALU.add))
                elif part == 6:
                    go.settled()
                    go.did(dve.tensor_tensor(row_code[:, :, :], code[:, :, :], sel[:, :, :], ALU.mult))
                else:
                    go.settled(waited)
                    for i in range(2):
                        go.did(dve.max(row_top[:, i, :], row_code[:, i, :]))

            def slots(r, at, buf, go):
                wait_apart(dve, s[f"meta_in{buf}"], 16 * K * (r - 2 - buf), waited)
                toks = token[:, at:at + 2] if isinstance(at, int) else token[:, bass.ds(at, 2)]
                go.did(dve.tensor_copy(meta[:, buf, :, 0].bitcast(I32), toks))
                go.settled()
                dve.tensor_scalar(slot_idx[:, buf, :].rearrange("p (i k) -> p i k", i=2), row_top[:, :, 0:K],
                                  -1.0, float(FAR), ALU.mult, ALU.add).then_inc(s["slots_ready"], 1)

            def shared_out(q, i, at, ps):
                wait(dve, s["down_done"], 2 * q + i + 1)
                tile = x_all[:, at, :] if isinstance(at, int) else \
                    x_all[:, bass.ds(at, 1), :].rearrange("p a f -> p (a f)")
                dve.scalar_tensor_tensor(tile, ps[i], tanh_g[:, 1:2], tile, ALU.mult, ALU.add)\
                    .then_inc(s["y_ready"], 1)

            def tile_at(n):
                return n if isinstance(n, int) else dve.snap(n)

            def step(r, h, par, att=True, turn=True, place_=True):
                first = isinstance(r, int) and r == 0
                last = isinstance(r, int) and r == PAIRS
                go_b = Steps(dve, s["att_step"], (r - 1) * K_ATT + 2)
                go_a = Steps(dve, s["att_step"], r * K_ATT)
                go_p = Steps(dve, s["route_step"], (r - 2) * K_ROUTE + K_CHOOSE)
                go_c = Steps(dve, s["route_step"], (r - 1) * K_ROUTE)
                at_b = tile_at(2 * r - 2)
                at_c = tile_at(2 * r - 4) if place_ else None
                if turn:
                    residual(r - 1, 1, at_b, go_b)
                if att:
                    smax(r, 0)
                if first:
                    stats1(3)
                    variances1(4, N, slice(6, N + 2))
                if turn:
                    statistics(r - 1, 1, at_b, go_b, 0)
                    statistics(r - 1, 1, at_b, go_b, 1)
                    go_b.settled()
                    go_b.did(dve.tensor_scalar(var[:, 4:6], mv2[:, :, 1], EPS, None, ALU.add))
                    go_b.settled()
                    c = slice(4, N + 2) if isinstance(r, int) and r == 1 else slice(4, 6)
                    newton_start(go_b, c)
                    newton_guess(go_b, c)
                for n in range(9):
                    if place_ and n < 5:
                        place(r, at_c, go_p, n)
                    if att and n == 7:
                        smax(r, 1)
                    if turn and n % 3 == 0:
                        newton_square(go_b, c)
                    elif turn and n % 3 == 1:
                        newton_scale(go_b, c)
                    elif turn:
                        newton_update(go_b, c)
                if turn:
                    norm2(r - 1, at_b, go_b)
                    if isinstance(r, int) and r == 1:
                        shifts1(4, N, slice(6, N + 2))
                if place_:
                    place(r, at_c, go_p, 5)
                if att:
                    inverse_sum(r, 0)
                if place_:
                    place(r, at_c, go_p, 6)
                    if par == 0:
                        shared_act(h - 1, 2, 0, gu_ps)
                    place(r, at_c, go_p, 7)
                    if par == 0:
                        shared_act(h - 1, 2, 1, gu_ps)
                    slots(r, at_c, par, go_p)
                    assert go_p.n == K_ROUTE - K_CHOOSE, go_p.n
                if place_ and par == 1 and att:
                    shared_out(h - 1, 1, tile_at(2 * r - 5), down_ps)
                up = turn and att and par == 1
                if last:
                    shared_out(NQ - 1, 0, at_c, down_ps)
                if turn:
                    max_logit(r)
                if last:
                    shared_out(NQ - 1, 1, N - 3, down_ps)
                if turn:
                    choose(r, go_c, 0)
                    choose(r, go_c, 1)
                if att:
                    inverse_sum(r, 1)
                if turn:
                    choose(r, go_c, 2)
                early = att and par == 0
                if early:
                    residual(r, 0, tile_at(2 * r), go_a)
                if turn:
                    choose(r, go_c, 3)
                if early:
                    statistics(r, 0, tile_at(2 * r), go_a, 0)
                if turn:
                    choose(r, go_c, 4)
                if early:
                    statistics(r, 0, tile_at(2 * r), go_a, 1)
                if place_ and par == 0 and not last:
                    shared_out(h - 1, 0, at_c, down_ps)
                if up:
                    shared_act(h, 0, 0, gu_ps)
                if turn:
                    choose(r, go_c, 5)
                if up:
                    shared_act(h, 0, 1, gu_ps)
                late = att and par == 1
                if late:
                    residual(r, 0, tile_at(2 * r), go_a)
                if turn:
                    choose(r, go_c, 6)
                if late:
                    statistics(r, 0, tile_at(2 * r), go_a, 0)
                if turn:
                    choose(r, go_c, 7)
                if late:
                    statistics(r, 0, tile_at(2 * r), go_a, 1)
                if turn:
                    choose(r, go_c, 8)
                if last:
                    shared_act(NQ, 0, 0, late_gu_ps)
                if up:
                    shared_act(h, 1, 0, gu_ps)
                if turn:
                    choose(r, go_c, 9)
                if last:
                    shared_act(NQ, 0, 1, late_gu_ps)
                if up:
                    shared_act(h, 1, 1, gu_ps)
                if turn:
                    assert go_c.n == K_CHOOSE, go_c.n
                    assert go_b.n == K_ATT - 2, go_b.n

            def slot_tables():
                dve.wait_ge(s["newest_mm"], 1)
                dve.wait_ge(s["table_in"], 16)
                names = table[:, :].bitcast(I32).rearrange("c (e w) -> c e w", w=W)[:, :, 0]
                dve.tensor_tensor(gidx[:, :], names, nr_ps, ALU.add).then_inc(s["tables_ready"], 1)
                dve.tensor_scalar(sidx[:, :], names, last_dump[0:C, :], None, ALU.add).then_inc(s["tables_ready"], 1)

            stats1(2)
            step(0, 0, 0, turn=False, place_=False)
            dve.wait_ge(s["consts_ready"], 9)
            step(1, 0, 1, place_=False)
            with dve.Fori(1, PAIRS // 2) as h:
                step(2 * h, h, 0)
                step(2 * h + 1, h, 1)
            step(PAIRS, NQ, 0, att=False)
            step(PAIRS + 1, NQ, 1, att=False, turn=False)
            for m in range(1, 3):
                shared_act(NQ, m, 0, late_gu_ps)
                shared_act(NQ, m, 1, late_gu_ps)
            for q in range(NQ + 1, 2 * NQ + 1):
                if q == 2 * NQ - 1:
                    slot_tables()
                if q < 2 * NQ:
                    shared_act(q, 0, 0, late_gu_ps)
                for i in range(2):
                    shared_out(q - 1, i, 4 * (q - 1 - NQ) + 2 + i, late_ps)
                if q < 2 * NQ:
                    shared_act(q, 0, 1, late_gu_ps)
                    for m in range(1, 3):
                        shared_act(q, m, 0, late_gu_ps)
                        shared_act(q, m, 1, late_gu_ps)
                if q == NQ + 1:
                    go = Steps(dve, s["table_step"], 0)
                    nt_ps, nr_ps = bank[1][0:E, 0:P], bank[1][0:C, P:P + E]
                    dve.wait_ge(s["newest_t"], 1)
                    go.did(dve.tensor_reduce(newest_col[:, :], nt_ps, AX, ALU.max))
                    go.did(dve.memset(newest_sel[:, :], 0.0))
                    go.settled()
                    dve.tensor_copy(newest_sel[:, LAST:C], newest_col[:, :]).then_inc(s["newest_ready"], 1)

            at_ps = bank[3][0:MH, 0:2 * C]
            eg_ps = [bank[4][0:C, 0:2 * M], bank[5][0:C, 0:2 * M]]

            def take_act(e, b):
                wait(dve, s["at_done"], e + 1)
                wait(dve, s["o_done"], e - 1)
                dve.tensor_copy(act_tt[:, b % 2, :], at_ps).then_inc(s["at_out"], 1)

            def multiply(e, b):
                wait(dve, s["silu_ready"], e + 1)
                wait(dve, s["at_done"], e - 1)
                dve.tensor_tensor(act_sb[:, b % 2, :], silu_sb[:, b % 2, :], eg_ps[b % 2][:, M:2 * M], ALU.mult)\
                    .then_inc(s["a_ready"], 1)

            def slot_weight(e, b):
                at = L + e if isinstance(e, int) else dve.snap(L + e)
                wait(dve, s[f"rows_in{b % ROWS}"], (e - b % ROWS) * (16 // ROWS) + 16)
                wait(dve, s["o_ready"], e - 3)
                dve.tensor_scalar(slot_w[:, b % 4:b % 4 + 1], rows[b % ROWS][:, bass.ds(at, 1)],
                                  not_last[0:C, :], is_last[0:C, :], ALU.mult, ALU.add)\
                    .then_inc(s["slot_w_ready"], 1)

            def weight_parts(t):
                at = slice(t * P, (t + 1) * P)
                w = w_over_t[:, at]
                go.did(dve.tensor_copy(w_over_t[E:P, at], w_over_t[0:E, at]))
                go.settled()
                go.did(dve.tensor_copy(high_low[:, at], w))
                go.settled()
                go.did(dve.tensor_tensor(w, w, high_low[:, at], ALU.subtract))
                go.settled()
                go.did(dve.tensor_copy(high_mid[:, at], w))
                go.settled()
                go.did(dve.tensor_tensor(high_low[E:P, at], w_over_t[E:P, at], high_mid[E:P, at], ALU.subtract))
                dve.tensor_copy(high_mid[0:E, at], high_low[0:E, at]).then_inc(s["w_parts_ready"], 1)

            go = Steps(dve, s["w_part_step"], 0)
            dve.wait_ge(s["wov_out"], PAIRS)
            weight_parts(0)
            slot_weight(0, 0)
            multiply(0, 0)
            for e in range(1, 9):
                slot_weight(e, e)
                multiply(e, e)
                take_act(e - 1, e - 1)
                weight_parts(e)
            with dve.Fori(1, E // 8 - 1) as q:
                for b in range(1, 9):
                    slot_weight(8 * q + b, b)
                    multiply(8 * q + b, b)
                    take_act(8 * q + b - 1, b - 1)
            for e in range(E - 7, E):
                slot_weight(e, e)
                multiply(e, e)
                take_act(e - 1, e - 1)
                if e < E - 2:
                    weight_parts(N // 2 + 1 + e - (E - 7))
            take_act(E - 1, E - 1)
            weight_parts(N - 2)
            weight_parts(N - 1)

            high, middle, low_high = [last_parts[:, k, :] for k in range(3)]
            go = Steps(dve, s["last_part_step"], 0)
            dve.wait_ge(s["lasts_in"], 16 * (1 + SAVED))
            go.did(dve.tensor_copy(last_sb[E:P, :], last_sb[0:E, :]))
            go.settled()
            go.did(dve.tensor_copy(high, last_sb[:, :]))
            go.settled()
            dve.tensor_copy(low_high[E:P], high[E:P]).then_inc(s["last_parts_ready"], 1)
            go.did(dve.tensor_tensor(last_sb[:, :], last_sb[:, :], high, ALU.subtract))
            go.settled()
            go.did(dve.tensor_copy(middle, last_sb[:, :]))
            go.settled()
            dve.tensor_tensor(low_high[0:E], last_sb[0:E, :], middle[0:E], ALU.subtract)\
                .then_inc(s["last_parts_ready"], 1)

            for r in range(PAIRS):
                dve.wait_ge(s[f"even_back{r * QUARTERS // PAIRS}"], 16)
                dve.wait_ge(s["ov_done"], 2 * r + 2)
                a = even_sb[:, 2 * r:2 * r + 2, :].rearrange("p n f -> p (n f)")
                dve.tensor_tensor(a, a, bank[r][:, :], ALU.add).then_inc(s["sum_ready"], 1)

        @block.gpsimd
        def _(pool):
            pool.memset(ident[:, :], 0.0).then_inc(s["ident_ready"], 1)
            pool.wait_ge(s["ident_ready"], 1)
            pool.affine_select(out=ident[:, :], in_=ident[:, :], compare_op=ALU.not_equal, fill=1.0, base=0,
                               pattern=[[-1, P]], channel_multiplier=1).then_inc(s["ident_ready"], 1)
            pool.memset(ones_b[:, :], 1.0).then_inc(s["consts_ready"], 1)
            pool.wait_ge(s["consts_ready"], 1)
            pool.wait_ge(s["ident_ready"], 2)
            pool.tensor_copy(ident_b[:, :], ident[:, :]).then_inc(s["consts_ready"], 1)
            pool.affine_select(out=before[:, :], in_=ones_b[:, :], compare_op=ALU.is_ge, fill=0.0, base=-1,
                               pattern=[[1, P]], channel_multiplier=-1).then_inc(s["consts_ready"], 1)
            pool.iota(row_id[:, :], pattern=[[0, 1]], base=0, channel_multiplier=1,
                      allow_small_or_imprecise_dtypes=True)
            pool.iota(row_base[:, :], pattern=[[-1, E]], base=FAR, channel_multiplier=0,
                      allow_small_or_imprecise_dtypes=True)
            pool.iota(token[:, :], pattern=[[P, N]], base=0, channel_multiplier=1,
                      allow_small_or_imprecise_dtypes=True).then_inc(s["consts_ready"], 1)
            for a, value in ((counts, 0.0), (newest, 0.0), (g_max, GONE), (kept, GONE), (meta, 0.0)):
                pool.memset(a[:], value).then_inc(s["consts_ready"], 1)
            pool.memset(table_fill[:, :], 0.0).then_inc(s["fill_step"], 1)
            pool.wait_ge(s["consts_ready"], 4)
            pool.tensor_scalar(is_last[:, :], row_id[:, :], float(LAST), None, ALU.is_equal).then_inc(s["fill_step"], 1)
            pool.wait_ge(s["fill_step"], 2)
            pool.tensor_scalar(not_last[:, :], is_last[:, :], -1.0, 1.0, ALU.mult, ALU.add)
            pool.tensor_scalar(last_dump[:, :], is_last[:, :], float(T + LAST), None, ALU.mult)
            pool.tensor_scalar(fill0[:, :], row_id[:, :], float(T), None, ALU.add).then_inc(s["fill_step"], 1)
            pool.wait_ge(s["fill_step"], 3)
            pool.tensor_tensor(fill0[:, :], fill0[:, :], last_dump[:, :], ALU.subtract).then_inc(s["fill_step"], 1)
            pool.wait_ge(s["fill_step"], 4)
            pool.tensor_copy(table_fill[:, :].bitcast(I32).rearrange("c (e w) -> c e w", w=W)[:, :, 0:1],
                             fill0[0:C, :].rearrange("c (a b) -> c a b", a=1).to_broadcast([C, E, 1]))\
                .then_inc(s["fill_ready"], 1)

            last_row = pool.to_reg(LAST * E - 1)
            waited = s["waited_pool"]

            def scatter(r, buf):
                wait_apart(pool, s["slots_ready"], r, waited)
                for k in range(2 * K):
                    pool.indirect_dma_start(
                        table_dram, bass.IndirectOffsetOnAxis(ap=slot_idx[:, buf, k:k + 1], axis=0),
                        meta[:, buf, k // K, :], None, bounds_check=last_row, oob_is_err=False)\
                        .then_inc(s[f"meta_in{buf}"], 16)

            pool.wait_ge(s["fills_in"], 80)
            with pool.Fori(0, PAIRS // 2) as h:
                for par in range(2):
                    scatter(2 * h + (par + 1), par)

            def gather(e, b, col):
                pool.indirect_dma_start(rows[b % ROWS], None, xn_dram,
                                        bass.IndirectOffsetOnAxis(ap=gidx_now[:, col:col + 1], axis=0))\
                    .then_inc(s[f"rows_in{b % ROWS}"], 16)

            def add_up(e, b):
                wait(pool, s["o_ready"], e + 1)
                wait_apart(pool, s[f"acc_in{b % 2}"], 8 * e - 8 * (b % 2), waited)
                pool.indirect_dma_start(out if b % 2 else even_dram,
                                        bass.IndirectOffsetOnAxis(ap=sidx_now[:, b:b + 1], axis=0),
                                        outs[b % OUTS], None, compute_op=ALU.add)\
                    .then_inc(s[f"acc_in{b % 2}"], 16)

            pool.wait_ge(s["tables_ready"], 2)
            pool.wait_ge(s["xn_saved"], 16 * PAIRS)
            pool.wait_ge(s["w_saved"], 16 * PAIRS)
            pool.wait_ge(s["s_done"], N)
            pool.wait_ge(s["h_done"], N)
            pool.wait_ge(s["v_done"], N)
            pool.tensor_copy(gidx_now[:, 8:8 + AHEAD], gidx[:, 0:AHEAD]).then_inc(s["idx_now"], 1)
            pool.wait_ge(s["idx_now"], 1)
            for e in range(AHEAD):
                gather(e, e, 8 + e)

            def eight(q, n):
                for half in range(2):
                    at = 8 * q + 4 * half
                    at_g = at + AHEAD
                    m = max(min(n - 4 * half, 4), 0)
                    if not isinstance(q, int):
                        at, at_g = pool.snap(at), pool.snap(at_g)
                    wait(pool, s["t_done"], 8 * q + AHEAD - 4 + 4 * half)
                    if m > 0:
                        pool.tensor_copy(gidx_now[:, 4 * half:4 * half + m], gidx[:, bass.ds(at_g, m)])\
                            .then_inc(s["idx_now"], 1)
                    pool.tensor_copy(sidx_now[:, 4 * half:4 * half + 4], sidx[:, bass.ds(at, 4)])\
                        .then_inc(s["idx_now"], 1)
                    wait_apart(pool, s["idx_now"], 4 * q + 2 * half + 2 + (m > 0), waited)
                    for b in range(4 * half, 4 * half + 4):
                        if b < n:
                            gather(8 * q + AHEAD + b, b + AHEAD, b)
                        add_up(8 * q + b, b)

            pool.wait_ge(s["y_saved"], 16 * PAIRS)
            eight(0, 8)
            with pool.Fori(1, E // 8 - 1) as q:
                eight(q, 8)
            eight(E // 8 - 1, 8 - AHEAD)

            pool.wait_ge(s["acc_in1"], 16 * E // 2)
            n = N // QUARTERS
            for q in range(QUARTERS):
                pool.wait_ge(s["sum_ready"], PAIRS // QUARTERS * (q + 1))
                pool.dma_start(out[P * n * q:P * n * (q + 1), :].rearrange("(n p) f -> p n f", p=P),
                               even_sb[:, n * q:n * (q + 1), :], accum_op=ALU.add).then_inc(s["result_added"], 16)
            pool.wait_ge(s["result_added"], 16 * QUARTERS)


def kernel(**inputs):
    import numpy as np
    import concourse.bacc as bacc
    from concourse.bass_utils import run_bass_kernel_spmd

    a = {k: np.asarray(v) for k, v in inputs.items()}

    qkv = np.concatenate([a[f"L0_xattn_{n}W"].T for n in "QKV"], axis=1)
    cols = np.stack([a["L0_xattn_Qb"], a["L0_xattn_Kb"], a["L0_xattn_Vb"],
                     np.repeat(a["g_xattn"], P), np.repeat(a["g_ffn"], P)], axis=1)
    gu = np.concatenate([a["L0_ffn_Wg"], a["L0_ffn_Wu"]], axis=1)
    gu = gu.reshape(GROUPS, GE, 2 * M, H2, P).transpose(0, 4, 1, 3, 2).reshape(GROUPS, P, GE * GU)
    wd = a["L0_ffn_Wd"].reshape(GROUPS, GE, L, 2, MH).transpose(0, 4, 1, 3, 2).reshape(GROUPS, MH, GE * DW)
    sgu = np.concatenate([a["L0_ffn_Sg"], a["L0_ffn_Su"]], axis=0).reshape(2 * MS, H2, P).transpose(2, 1, 0)
    sd = a["L0_ffn_Sd"].T
    arrays = {
        "x_in": a["x"].transpose(1, 0, 2),
        "ctx_in": a["ctx_2048"].transpose(1, 0, 2),
        "cols_in": cols,
        "qkv_in": qkv,
        "gate_in": a["L0_ffn_gate_weight"].reshape(E, H2, P).transpose(2, 1, 0),
        "sgu_in": sgu,
        "sd_in": sd[0:2 * P].reshape(2, P, L).transpose(1, 0, 2),
        "sd2_in": sd[2 * P:],
        "wgu_in": gu,
        "wd_in": wd,
    }
    arrays = {k: np.ascontiguousarray(v) for k, v in arrays.items()}
    nc = bacc.Bacc("TRN2", target_bir_lowering=False, num_devices=1)
    args = [nc.dram_tensor(k, v.shape, mybir.dt.from_np(v.dtype), kind="ExternalInput").ap()
            for k, v in arrays.items()]
    args.append(nc.dram_tensor("result", (T + C, L), F32, kind="ExternalOutput").ap())
    build(nc, *args)
    r = run_bass_kernel_spmd(nc, [arrays], core_ids=[0])
    return r.results[0]["result"][0:T].reshape(N, P, L)
```
